# Optimizing a Trainium2 kernel written in Bass

```python
import numpy as np
import jax
import jax.numpy as jnp

def _softmax(x, axis=-1):
    return jax.nn.softmax(x, axis=axis)

def _gelu(x):
    return jax.nn.gelu(x, approximate=True)

def _silu(x):
    return jax.nn.silu(x)

def _sigmoid(x):
    return jax.nn.sigmoid(x)

def _layernorm(x, axis=-1, eps=1e-05):
    m = jnp.mean(x, axis=axis, keepdims=True)
    v = jnp.var(x, axis=axis, keepdims=True)
    return (x - m) / jnp.sqrt(v + eps)

def _scatter_add(tgt, idx, src, axis=0):
    return tgt.at[idx].add(src)

def _segment_sum(src, seg, n):
    return jax.ops.segment_sum(src, seg, n)
kernel_name = 'mk_gnn_preln_d4_gnn_r32_3d7805'

def setup_inputs(seed: int=0):
    np.random.seed(seed)
    _w = jnp.asarray

    def _rec_inputs():
        import jax
        import jax.numpy as jnp
        _gk = jax.random.key(seed)
        x = -0.0003713 + 1 * jax.random.normal(jax.random.fold_in(_gk, 1), (3125, 256), jnp.float32)
        _s = jax.random.randint(jax.random.fold_in(_gk, 2), (25000,), 0, 3125, jnp.int32)
        _d = jax.random.randint(jax.random.fold_in(_gk, 3), (25000,), 0, 3125, jnp.int32)
        _loop = jnp.arange(3125, dtype=jnp.int32)
        src = jnp.concatenate([_s, _d, _loop])
        dst = jnp.concatenate([_d, _s, _loop])
        _o = jnp.argsort(dst, stable=True)
        src = src[_o]
        dst = dst[_o]
        edge_type_8 = jax.random.randint(jax.random.fold_in(_gk, 12), (53125,), 0, 8, jnp.int32)
        edge_weight = jax.random.uniform(jax.random.fold_in(_gk, 13), (53125,), jnp.float32, 0.0, 0.999999)
        edge_weight1 = jax.random.uniform(jax.random.fold_in(_gk, 14), (53125, 1), jnp.float32, 0.0, 0.999999)
        return (x, src, dst, edge_type_8, edge_weight, edge_weight1)
    x, src, dst, edge_type_8, edge_weight, edge_weight1 = _rec_inputs()

    def _L0_gnn_setup():
        import jax, jax.numpy as jnp
        import numpy as np
        N_NODES, N_EDGES, D_IN, D_HID, N_LAYERS = (50000, 25000, 256, 256, 3)
        key = jax.random.key(seed)
        k_x, k_e, k_w = jax.random.split(key, 3)
        x = jax.random.normal(k_x, (N_NODES, D_IN), dtype=jnp.float32)
        edge_index = jax.random.randint(k_e, (2, N_EDGES), 0, N_NODES, dtype=jnp.int32)
        W = jax.random.normal(k_w, (N_LAYERS, D_IN, D_HID), dtype=jnp.float32) * (1.0 / np.sqrt(D_IN))
        b = jnp.zeros((N_LAYERS, D_HID), dtype=jnp.float32)
        return {'x': x, 'edge_index': edge_index, 'W': W, 'b': b}
    _L0_gnn_all = _L0_gnn_setup()
    _L0_gnn_in = {k: v for k, v in _L0_gnn_all.items() if k in ('W', 'b')}
    del _L0_gnn_all

    def _L1_gnn_setup():
        import jax, jax.numpy as jnp
        import numpy as np
        N_NODES = 50000
        N_EDGES = 18750
        C_IN = 256
        C_OUT = 256
        N_REL = 8
        key = jax.random.key(seed)
        ks = jax.random.split(key, 7)
        x = jax.random.normal(ks[0], (N_NODES, C_IN), dtype=jnp.float32)
        edge_index = jax.random.randint(ks[1], (2, N_EDGES), 0, N_NODES, dtype=jnp.int64)
        edge_type = jax.random.randint(ks[2], (N_EDGES,), 0, N_REL, dtype=jnp.int64)
        edge_weight = jax.random.uniform(ks[3], (N_EDGES,), dtype=jnp.float32)
        weight = jax.random.normal(ks[4], (N_REL, C_IN, C_OUT), dtype=jnp.float32) * (1.0 / np.sqrt(C_IN))
        root = jax.random.normal(ks[5], (C_IN, C_OUT), dtype=jnp.float32) * (1.0 / np.sqrt(C_IN))
        bias = jnp.zeros((C_OUT,), dtype=jnp.float32)
        return {'x': x, 'edge_index': edge_index, 'edge_type': edge_type, 'edge_weight': edge_weight, 'weight': weight, 'root': root, 'bias': bias}
    _L1_gnn_all = _L1_gnn_setup()
    _L1_gnn_in = {k: v for k, v in _L1_gnn_all.items() if k in ('weight', 'root', 'bias')}
    del _L1_gnn_all

    def _L2_gnn_setup():
        import jax, jax.numpy as jnp
        import numpy as np
        N = 50000
        E = 25000
        HEADS = 4
        C = 64
        IN = 256
        NEG_SLOPE = 0.2

        def _gat_forward(x, edge_index, W, att_src, att_dst, bias):
            n = x.shape[0]
            h = (x @ W).reshape(n, HEADS, C)
            loop = jnp.arange(n, dtype=edge_index.dtype)
            src = jnp.concatenate([edge_index[0], loop])
            dst = jnp.concatenate([edge_index[1], loop])
            a_src = jnp.einsum('nhc,hc->nh', h, att_src)
            a_dst = jnp.einsum('nhc,hc->nh', h, att_dst)
            logits = a_src[src] + a_dst[dst]
            logits = jnp.where(logits >= 0, logits, NEG_SLOPE * logits)
            seg_max = jax.ops.segment_max(logits, dst, num_segments=n)
            seg_max = jnp.where(jnp.isfinite(seg_max), seg_max, 0.0)
            ex = jnp.exp(logits - seg_max[dst])
            denom = jax.ops.segment_sum(ex, dst, num_segments=n)
            alpha = ex / (denom[dst] + 1e-16)
            msgs = alpha[:, :, None] * h[src]
            out = jax.ops.segment_sum(msgs, dst, num_segments=n)
            out = out.reshape(n, HEADS * C) + bias
            return jax.nn.relu(out)
        key = jax.random.key(seed)
        k = jax.random.split(key, 6)
        x = jax.random.normal(k[0], (N, IN), dtype=jnp.float32)
        edge_index = jax.random.randint(k[1], (2, E), 0, N, dtype=jnp.int64)
        W = jax.random.normal(k[2], (IN, HEADS * C), dtype=jnp.float32) * (1.0 / np.sqrt(IN))
        att_src = jax.random.normal(k[3], (HEADS, C), dtype=jnp.float32) * (1.0 / np.sqrt(C))
        att_dst = jax.random.normal(k[4], (HEADS, C), dtype=jnp.float32) * (1.0 / np.sqrt(C))
        bias = jax.random.normal(k[5], (HEADS * C,), dtype=jnp.float32) * 0.02
        return {'x': x, 'edge_index': edge_index, 'W': W, 'att_src': att_src, 'att_dst': att_dst, 'bias': bias}
    _L2_gnn_all = _L2_gnn_setup()
    _L2_gnn_in = {k: v for k, v in _L2_gnn_all.items() if k in ('W', 'att_src', 'att_dst', 'bias')}
    del _L2_gnn_all

    def _L3_gnn_setup():
        import jax, jax.numpy as jnp
        import numpy as np
        N_NODES = 50000
        N_EDGES = 25000
        DIM = 256
        key = jax.random.key(seed)
        ks = jax.random.split(key, 8)
        x = jax.random.normal(ks[0], (N_NODES, DIM), dtype=jnp.float32)
        row = jax.random.randint(ks[1], (N_EDGES,), 0, N_NODES)
        col = jax.random.randint(ks[2], (N_EDGES,), 0, N_NODES)
        col = jnp.where(col == row, (col + 1) % N_NODES, col)
        edge_index = jnp.stack([row, col]).astype(jnp.int64)
        edge_weight = jax.random.uniform(ks[3], (N_EDGES, 1), dtype=jnp.float32)
        bound = 1.0 / np.sqrt(DIM)
        W1 = jax.random.uniform(ks[4], (DIM, DIM), minval=-bound, maxval=bound, dtype=jnp.float32)
        b1 = jax.random.uniform(ks[5], (DIM,), minval=-bound, maxval=bound, dtype=jnp.float32)
        W2 = jax.random.uniform(ks[6], (DIM, DIM), minval=-bound, maxval=bound, dtype=jnp.float32)
        b2 = jax.random.uniform(ks[7], (DIM,), minval=-bound, maxval=bound, dtype=jnp.float32)
        return {'x': x, 'edge_index': edge_index, 'edge_weight': edge_weight, 'W1': W1, 'b1': b1, 'W2': W2, 'b2': b2}
    _L3_gnn_all = _L3_gnn_setup()
    _L3_gnn_in = {k: v for k, v in _L3_gnn_all.items() if k in ('W1', 'b1', 'W2', 'b2')}
    del _L3_gnn_all
    return {'x': x, 'src': src, 'dst': dst, 'edge_type_8': edge_type_8, 'edge_weight': edge_weight, 'edge_weight1': edge_weight1, 'L0_gnn_W': _L0_gnn_in['W'], 'L0_gnn_b': _L0_gnn_in['b'], 'L1_gnn_weight': _L1_gnn_in['weight'], 'L1_gnn_root': _L1_gnn_in['root'], 'L1_gnn_bias': _L1_gnn_in['bias'], 'L2_gnn_W': _L2_gnn_in['W'], 'L2_gnn_att_src': _L2_gnn_in['att_src'], 'L2_gnn_att_dst': _L2_gnn_in['att_dst'], 'L2_gnn_bias': _L2_gnn_in['bias'], 'L3_gnn_W1': _L3_gnn_in['W1'], 'L3_gnn_b1': _L3_gnn_in['b1'], 'L3_gnn_W2': _L3_gnn_in['W2'], 'L3_gnn_b2': _L3_gnn_in['b2']}

def reference(x, src, dst, edge_type_8, edge_weight, edge_weight1, L0_gnn_W, L0_gnn_b, L1_gnn_weight, L1_gnn_root, L1_gnn_bias, L2_gnn_W, L2_gnn_att_src, L2_gnn_att_dst, L2_gnn_bias, L3_gnn_W1, L3_gnn_b1, L3_gnn_W2, L3_gnn_b2):
    import jax
    import jax.numpy as jnp

    def _L0_gnn_ref(x, edge_index, W, b):
        import jax, jax.numpy as jnp
        import numpy as np
        N_NODES, N_EDGES, D_IN, D_HID, N_LAYERS = (50000, 25000, 256, 256, 3)
        'Stacked GCNConv (PyG semantics: self-loops + symmetric norm) with ReLU.\n            Dropout is identity (eval mode) for a deterministic baseline.'
        N = x.shape[0]
        loops = jnp.arange(N, dtype=edge_index.dtype)
        src = jnp.concatenate([edge_index[0], loops])
        dst = jnp.concatenate([edge_index[1], loops])
        deg = jax.ops.segment_sum(jnp.ones(dst.shape, jnp.float32), dst, num_segments=N)
        dinv = jnp.where(deg > 0, jax.lax.rsqrt(deg), 0.0)
        norm = (dinv[src] * dinv[dst])[:, None]
        h = x
        for l in range(W.shape[0]):
            t = h @ W[l]
            msg = t[src] * norm
            agg = jax.ops.segment_sum(msg, dst, num_segments=N)
            h = jax.nn.relu(agg + b[l])
        return h

    def _L1_gnn_ref(x, edge_index, edge_type, edge_weight, weight, root, bias):
        import jax, jax.numpy as jnp
        import numpy as np
        N_NODES = 50000
        N_EDGES = 18750
        C_IN = 256
        C_OUT = 256
        N_REL = 8
        "RGCNConv (no bases/blocks), aggr='mean', root_weight=True, bias=True.\n\n            Equivalent to the PyG per-relation loop:\n                for r: out += scatter_mean(x[src_r] * w_r, dst_r) @ weight[r]\n                out += x @ root + bias\n            but fused: one segmented mean over (relation, dst) pairs followed by a\n            grouped GEMM over relations.\n            "
        N, C = x.shape
        R = weight.shape[0]
        src, dst = (edge_index[0], edge_index[1])
        msg = x[src] * edge_weight[:, None]
        seg = edge_type * N + dst
        sums = jax.ops.segment_sum(msg, seg, num_segments=R * N)
        cnt = jax.ops.segment_sum(jnp.ones_like(edge_weight), seg, num_segments=R * N)
        h = sums / jnp.maximum(cnt, 1.0)[:, None]
        h = h.reshape(R, N, C)
        out = jnp.einsum('rnc,rco->no', h, weight)
        out = out + x @ root + bias
        return out

    def _L2_gnn_ref(x, edge_index, W, att_src, att_dst, bias):
        import jax, jax.numpy as jnp
        import numpy as np
        N = 50000
        E = 25000
        HEADS = 4
        C = 64
        IN = 256
        NEG_SLOPE = 0.2

        def _gat_forward(x, edge_index, W, att_src, att_dst, bias):
            n = x.shape[0]
            h = (x @ W).reshape(n, HEADS, C)
            loop = jnp.arange(n, dtype=edge_index.dtype)
            src = jnp.concatenate([edge_index[0], loop])
            dst = jnp.concatenate([edge_index[1], loop])
            a_src = jnp.einsum('nhc,hc->nh', h, att_src)
            a_dst = jnp.einsum('nhc,hc->nh', h, att_dst)
            logits = a_src[src] + a_dst[dst]
            logits = jnp.where(logits >= 0, logits, NEG_SLOPE * logits)
            seg_max = jax.ops.segment_max(logits, dst, num_segments=n)
            seg_max = jnp.where(jnp.isfinite(seg_max), seg_max, 0.0)
            ex = jnp.exp(logits - seg_max[dst])
            denom = jax.ops.segment_sum(ex, dst, num_segments=n)
            alpha = ex / (denom[dst] + 1e-16)
            msgs = alpha[:, :, None] * h[src]
            out = jax.ops.segment_sum(msgs, dst, num_segments=n)
            out = out.reshape(n, HEADS * C) + bias
            return jax.nn.relu(out)
        return _gat_forward(x, edge_index, W, att_src, att_dst, bias)

    def _L3_gnn_ref(x, edge_index, edge_weight, W1, b1, W2, b2):
        import jax, jax.numpy as jnp
        import numpy as np
        N_NODES = 50000
        N_EDGES = 25000
        DIM = 256
        n = x.shape[0]
        loops = jnp.arange(n)
        row = jnp.concatenate([edge_index[0], loops])
        col = jnp.concatenate([edge_index[1], loops])
        ew = jnp.concatenate([edge_weight, jnp.ones((n, 1), x.dtype)], axis=0)
        deg = jnp.zeros((n,), x.dtype).at[col].add(1.0)
        dinv = jnp.where(deg > 0, deg ** (-0.5), 0.0)[:, None]
        norm = dinv[row] * ew * dinv[col]

        def gcn_layer(h, W, b):
            h = h @ W.T + b
            msg = norm * h[row]
            out = jax.ops.segment_sum(msg, col, num_segments=n)
            return jax.nn.relu(out)
        h = gcn_layer(x, W1, b1)
        h = gcn_layer(h, W2, b2)
        return h
    edge_index = jnp.stack([src, dst])
    h = jnp.maximum(_layernorm(x, axis=-1), 0.0)
    x = x + _L0_gnn_ref(h, edge_index, L0_gnn_W, L0_gnn_b)
    h = jnp.maximum(_layernorm(x, axis=-1), 0.0)
    x = x + _L1_gnn_ref(h, edge_index, edge_type_8, edge_weight, L1_gnn_weight, L1_gnn_root, L1_gnn_bias)
    h = jnp.maximum(_layernorm(x, axis=-1), 0.0)
    x = x + _L2_gnn_ref(h, edge_index, L2_gnn_W, L2_gnn_att_src, L2_gnn_att_dst, L2_gnn_bias)
    h = jnp.maximum(_layernorm(x, axis=-1), 0.0)
    x = x + _L3_gnn_ref(h, edge_index, edge_weight1, L3_gnn_W1, L3_gnn_b1, L3_gnn_W2, L3_gnn_b2)
    return x

_drawn_inputs = setup_inputs


def setup_inputs(seed=0):
    import zlib

    import numpy as np

    out = dict(_drawn_inputs(seed))
    spreads = {'L0_gnn_b': (0.0, 0.1), 'L1_gnn_bias': (0.0, 0.1)}
    factors = {'edge_weight1': 8.0,
     'L2_gnn_att_dst': 56.904,
     'L2_gnn_bias': 5.976,
     'L3_gnn_W1': 4.442,
     'L3_gnn_b1': 8.0,
     'L3_gnn_W2': 3.699,
     'L3_gnn_b2': 7.312,
     'L2_gnn_att_src': 6.264}
    for name, (base, spread) in spreads.items():
        noise = np.random.default_rng([zlib.crc32(name.encode()), seed]).standard_normal(out[name].shape)
        drawn = base * np.exp(spread * noise) if base else spread * noise
        out[name] = jnp.asarray(drawn.astype(out[name].dtype))
    for name, factor in factors.items():
        out[name] = (out[name] * factor).astype(out[name].dtype)
    return out
```

```python
from contextlib import ExitStack

import concourse.bass as bass
from concourse import mybir
from concourse.bass import IndirectOffsetOnAxis

F32 = mybir.dt.float32
BF16 = mybir.dt.bfloat16
I32 = mybir.dt.int32
ALU = mybir.AluOpType
ACT = mybir.ActivationFunctionType
AX = mybir.AxisListType

P = 128
TRIO = 3
TRIOS = 6
SLOTS = TRIO * TRIOS
WORDS = 6
SRC, SRC_TYPE, DST, TYPE, WEIGHT, WEIGHT1 = range(WORDS)
HEADS = 4
SLOPE = 0.2
EPS = 1e-5
FAR = 1.0e30
PARTS = 3 * HEADS
PART_WORDS = PARTS // 2
KC = 2


class Shapes:

    def __init__(self, nodes, edges, width, relations):
        self.nodes, self.edges, self.width, self.relations = nodes, edges, width, relations
        self.tiles = -(-nodes // P)
        self.last = nodes - (self.tiles - 1) * P
        self.rows = max(r for r in range(1, P + 1) if edges % r == 0)
        self.cols = edges // self.rows
        self.group = SLOTS * P
        self.max_groups = self.tiles + edges // self.group
        self.more = self.max_groups - self.tiles






class Core:

    def __init__(self, nc, ctx, s):
        def sb(name, shape, dtype=F32):
            return ctx.enter_context(nc.sbuf_tensor(name, shape, dtype))

        self.sem = lambda name: ctx.enter_context(nc.semaphore(name))
        self.semaphores = lambda name, n: [self.sem(f"{name}{i}") for i in range(n)]
        self.landed = self.semaphores("landed", SLOTS)
        self.passes, self.further = 0, 0
        C, R = s.width, s.relations
        self.identity = sb("identity", [P, P])
        self.lane = sb("lane", [P, P])
        self.relation = sb("relation", [P, TRIO, R])
        self.tile_base = sb("tile_base", [P, s.tiles])
        self.zeros = sb("zeros", [P, 512], BF16)
        self.ones_row = sb("ones_row", [1, P])
        self.plan = sb("plan", [1, s.tiles * 4], I32)
        self.unsorted = sb("unsorted", [1, 1], I32)
        self.x = sb("x_resident", [P, s.tiles * C])
        self.own = sb("own", [P, s.tiles * C])
        self.records = sb("records", [P, (s.max_groups + 1) * SLOTS, WORDS])
        self.dst_in_tile = sb("dst_in_tile", [P, (s.max_groups + 1) * SLOTS])
        self.dst_bf16 = sb("dst_bf16", [P, (s.max_groups + 1) * SLOTS], BF16)
        self.minus_node = sb("minus_node", [P, 1])
        self.count_parts = sb("count_parts", [P, s.tiles, 3, R], BF16)
        self.mean_weight = sb("mean_weight", [P, (s.max_groups + 1) * SLOTS])
        self.counts = sb("counts", [P, s.tiles * R])
        self.one_over_count = sb("one_over_count", [P, s.tiles * R])
        self.dinv = sb("dinv", [P, s.tiles])
        self.attention = sb("attention", [P, s.tiles, 2 * HEADS])
        self.parts = sb("parts", [P, s.tiles * PART_WORDS])
        self.identity_b = sb("identity_b", [P, P], BF16)
        self.pick = sb("pick", [PARTS, HEADS, P], BF16)
        self.w_gcn = sb("w_gcn", [P, 3 * KC, C])
        self.w_relation = sb("w_relation", [P, R * KC, C])
        self.w_root = sb("w_root", [P, KC, C])
        self.w_gat = sb("w_gat", [P, KC, C])
        self.w_out = sb("w_out", [P, 2 * KC, C])
        self.bias_gcn = sb("bias_gcn", [P, 3, C])
        self.bias_gat = sb("bias_gat", [P, C])
        self.att = sb("att", [P, 2, C])
        self.bias_root = sb("bias_root", [1, C])
        self.bias_out = sb("bias_out", [1, 2, C])
        dram = nc.dram_tensor
        self.edge_records = dram("edge_records", (s.edges + s.group, WORDS), F32).ap()
        n = s.tiles * P
        self.table = [dram(f"table_{i}", (n, C), F32).ap() for i in range(2)]
        self.relation_table = dram("relation_table", (n * R, C), F32).ap()
        self.gat_table = dram("gat_table", (n, C + HEADS + PART_WORDS), F32).ap()


def edges_unsorted(engine, k, s):
    return engine.value_load(k.unsorted[0:1, 0:1], min_val=0, max_val=s.rows)


def prepare(nc, k, s, a):
    C, T, R = s.width, s.tiles, s.relations
    with ExitStack() as ctx:
        def sb(name, shape, dtype=F32):
            return ctx.enter_context(nc.sbuf_tensor(name, shape, dtype))

        def psum(name, shape, dtype=F32):
            return ctx.enter_context(nc.psum_tensor(name, shape, dtype))

        rows, cols = s.rows, s.cols
        wide = T * cols
        pieces = [(i, min(512, wide - i)) for i in range(0, wide, 512)]
        ring = 5
        turns = cols // ring
        assert turns * ring == cols
        src = sb("p_src", [rows, cols], I32)
        dst = sb("p_dst", [rows, cols], I32)
        kind = sb("p_kind", [rows, cols], I32)
        weight = sb("p_weight", [rows, cols])
        weight1 = sb("p_weight1", [rows, cols])
        made = sb("p_made", [rows, cols * WORDS])
        tile_f = sb("p_tile_f", [rows, cols])
        place = sb("p_place", [P, wide + 1])
        before = sb("p_before", [rows, rows], BF16)
        ones = sb("p_ones", [rows, P], BF16)
        position = sb("p_position", [rows, cols], I32)
        next_dst = sb("p_next_dst", [rows, cols], I32)
        next_tile = sb("p_next_tile", [rows, cols])
        breaks = sb("p_breaks", [rows, 1], BF16)
        first = sb("p_first", [P, T + 1])
        number = sb("p_number", [P, T])
        multiples = sb("p_multiples", [P, s.more])
        beyond = sb("p_beyond", [P, T, s.more])
        groups = sb("p_groups", [P, T])
        group_end = sb("p_group_end", [P, T])
        part_of = sb("p_part_of", [PARTS, HEADS])
        pad = sb("p_pad", [P, SLOTS, WORDS])
        ring_at = sb("p_ring_at", [rows, ring], I32)
        ring_record = sb("p_ring_record", [rows, ring * WORDS])
        counted = psum("p_counted", [P, 2, 512])
        all_breaks = psum("p_all_breaks", [P, 1])
        turned = psum("p_turned", [P, 2, 512])
        fields = made[:].rearrange("p (c w) -> p c w", w=WORDS)
        int_fields = fields.bitcast(I32)
        w_raw = k.own[:, 0:2 * KC * C].rearrange("p (k c) -> p k c", c=C)
        in_tile = k.own[0:rows, 2 * KC * C:].bitcast(BF16)[:, 0:wide]

        edges_in = k.sem("edges_in")
        x_in = k.sem("x_in")
        weights_in = k.sem("weights_in")
        x_cleared = k.sem("x_cleared")
        constants = k.sem("p_constants")
        drafts = k.sem("p_drafts")
        pad_ready = k.sem("p_pad_ready")
        pad_out = k.sem("p_pad_out")
        tiles_known = k.sem("p_tiles_known")
        counted_ready = k.sem("p_counted_ready")
        counted_taken = k.sem("p_counted_taken")
        columns_counted = k.sem("p_columns_counted")
        before_ready = k.sem("p_before_ready")
        before_taken = k.sem("p_before_taken")
        turned_ready = k.sem("p_turned_ready")
        positions_ready = k.sem("p_positions_ready")
        slot_ready = k.sem("p_slot_ready")
        scattered = k.semaphores("p_scattered", ring)
        records_made = k.sem("p_records_made")
        in_place = k.sem("p_in_place")
        breaks_ready = k.sem("p_breaks_ready")
        breaks_counted = k.sem("p_breaks_counted")
        order_known = k.sem("p_order_known")
        dve_done = k.sem("p_dve_done")
        act_done = k.sem("p_act_done")
        weight_loads = 2 * 3 + R + 2 + 2 + 1 + 1 + 2 + 2
        n_constants = 14
        block = ctx.enter_context(nc.Block())

        @block.sync
        def _(sp):
            for buffer, name in ((dst, "dst"), (src, "src"), (kind, "edge_type_8"), (weight, "edge_weight")):
                sp.dma_start(buffer[:], a[name].rearrange("(p c) -> p c", c=cols)).then_inc(edges_in, 16)
            sp.dma_start(weight1[:], a["edge_weight1"].rearrange("(p c) o -> p (c o)", c=cols)).then_inc(edges_in, 16)
            last_row = (rows - 1) * cols
            sp.dma_start(next_dst[0:rows - 1, :], a["dst"][1:last_row + 1].rearrange("(p c) -> p c", c=cols)
                         ).then_inc(edges_in, 16)
            sp.dma_start(next_dst[rows - 1:rows, 0:cols - 1], a["dst"][last_row + 1:s.edges].unsqueeze(0)
                         ).then_inc(edges_in, 16)
            sp.dma_start(next_dst[rows - 1:rows, cols - 1:cols], a["dst"][s.edges - 1:s.edges].unsqueeze(0)
                         ).then_inc(edges_in, 16)
            sp.dma_start(k.x[:, 0:(T - 1) * C].rearrange("p (t c) -> p t c", c=C),
                         a["x"][0:(T - 1) * P, :].rearrange("(t p) c -> p t c", p=P)).then_inc(x_in, 16)
            sp.wait_ge(x_cleared, 1)
            sp.dma_start(k.x[0:s.last, (T - 1) * C:T * C], a["x"][(T - 1) * P:s.nodes, :]).then_inc(x_in, 16)
            for l in range(3):
                sp.dma_start(k.w_gcn[:, l * KC:(l + 1) * KC, :],
                             a["L0_gnn_W"][l].rearrange("(k p) c -> p k c", p=P)).then_inc(weights_in, 16)
                sp.dma_start(k.bias_gcn[:, l, :], a["L0_gnn_b"][l].partition_broadcast(P)).then_inc(weights_in, 16)
            for r in range(R):
                sp.dma_start(k.w_relation[:, r * KC:(r + 1) * KC, :],
                             a["L1_gnn_weight"][r].rearrange("(k p) c -> p k c", p=P)).then_inc(weights_in, 16)
            for buffer, name in ((k.w_root, "L1_gnn_root"), (k.w_gat, "L2_gnn_W")):
                sp.dma_start(buffer[:], a[name].rearrange("(k p) c -> p k c", p=P)).then_inc(weights_in, 16)
            for i, name in enumerate(("L3_gnn_W1", "L3_gnn_W2")):
                sp.dma_start(w_raw[:, i * KC:(i + 1) * KC, :],
                             a[name].rearrange("(k p) c -> p k c", p=P)).then_inc(weights_in, 16)
            sp.dma_start(k.bias_gat[:], a["L2_gnn_bias"].partition_broadcast(P)).then_inc(weights_in, 16)
            sp.dma_start(k.bias_root[:], a["L1_gnn_bias"].unsqueeze(0)).then_inc(weights_in, 16)
            for i, name in enumerate(("L3_gnn_b1", "L3_gnn_b2")):
                sp.dma_start(k.bias_out[:, i, :], a[name].unsqueeze(0)).then_inc(weights_in, 16)
            for i, name in enumerate(("L2_gnn_att_src", "L2_gnn_att_dst")):
                sp.dma_start(k.att[:, i, :],
                             a[name].rearrange("h c -> (h c)").partition_broadcast(P)).then_inc(weights_in, 16)
            sp.wait_ge(pad_ready, 1)
            sp.dma_start(k.edge_records[s.edges:s.edges + s.group, :].rearrange("(p c) w -> p c w", p=P),
                         pad[:]).then_inc(pad_out, 16)
            sp.wait_ge(records_made, 1)
            sp.dma_start(k.edge_records[0:s.edges, :].rearrange("(p c) w -> p (c w)", c=cols), made[:]).then_inc(in_place, 16)
            sp.wait_ge(in_place, 16)
            sp.wait_ge(pad_out, 16)
            sp.wait_ge(x_in, 32)
            sp.wait_ge(weights_in, 16 * weight_loads)

        @block.gpsimd
        def _(pool):
            pool.iota(k.lane[:], [[1, P]], base=0, channel_multiplier=0,
                      allow_small_or_imprecise_dtypes=True).then_inc(constants, 1)
            pool.iota(k.relation[:], [[0, TRIO], [1, R]], base=0, channel_multiplier=0,
                      allow_small_or_imprecise_dtypes=True).then_inc(constants, 1)
            pool.iota(k.tile_base[:], [[P, T]], base=0, channel_multiplier=0,
                      allow_small_or_imprecise_dtypes=True).then_inc(constants, 1)
            pool.iota(multiples[:], [[s.group, s.more]], base=s.group, channel_multiplier=0,
                      allow_small_or_imprecise_dtypes=True).then_inc(constants, 1)
            pool.iota(k.minus_node[:], [[0, 1]], base=0, channel_multiplier=-1,
                      allow_small_or_imprecise_dtypes=True).then_inc(constants, 1)
            pool.memset(k.dst_bf16[:], 0.0).then_inc(constants, 1)
            pool.memset(ones[:], 1.0).then_inc(constants, 1)
            pool.memset(k.zeros[:], 0.0).then_inc(constants, 1)
            pool.memset(k.ones_row[:], 1.0).then_inc(constants, 1)
            pool.memset(k.records[:], 0.0).then_inc(constants, 1)
            pool.memset(k.mean_weight[:], 0.0).then_inc(constants, 1)
            pool.memset(k.dst_in_tile[:], 0.0).then_inc(constants, 1)
            pool.memset(k.identity[:], 0.0).then_inc(drafts, 1)
            pool.memset(before[:], 1.0).then_inc(drafts, 1)
            pool.memset(pad[:], 0.0).then_inc(drafts, 1)
            pool.wait_ge(drafts, 3)
            pool.memset(pad[:, :, DST:DST + 1], float(2 * P * T)).then_inc(pad_ready, 1)
            pool.affine_select(out=k.identity[:], in_=k.identity[:], compare_op=ALU.not_equal, fill=1.0,
                               base=0, pattern=[[-1, P]], channel_multiplier=1).then_inc(constants, 1)
            pool.affine_select(out=before[:], in_=before[:], compare_op=ALU.is_gt, fill=0.0,
                               base=0, pattern=[[1, rows]], channel_multiplier=-1).then_inc(constants, 1)
            pool.wait_ge(order_known, 1)
            with pool.If(edges_unsorted(pool, k, s) > 0):
                pool.wait_ge(in_place, 16)
                with pool.Fori(0, turns):
                    for i in range(ring):
                        pool.wait_ge(slot_ready, 1)
                        pool.sem_inc(slot_ready, -1)
                        pool.indirect_dma_start(k.edge_records[0:s.edges, :],
                                                IndirectOffsetOnAxis(ap=ring_at[:, i:i + 1], axis=0),
                                                ring_record[:, i * WORDS:(i + 1) * WORDS], None
                                                ).then_inc(scattered[i], 16)

        @block.scalar
        def _(act):
            for i, (at, n) in enumerate(pieces):
                act.wait_ge(counted_ready, 1)
                act.sem_inc(counted_ready, -1)
                act.copy(place[:, 1 + at:1 + at + n], counted[:, i % 2, 0:n]).then_inc(act_done, 1)
                act.wait_ge(act_done, 1)
                act.sem_inc(act_done, -1)
                act.sem_inc(counted_taken, 1)
            act.sem_inc(columns_counted, 1)
            act.wait_ge(turned_ready, 1)
            act.sem_inc(turned_ready, -1)
            for i in range(2):
                for b in range(KC):
                    act.copy(k.w_out[:, i * KC + b, :], turned[:, i, b * C:(b + 1) * C]).then_inc(act_done, 1)
            act.wait_ge(act_done, 2 * KC)
            act.sem_inc(act_done, -(2 * KC))
            act.wait_ge(order_known, 1)
            with act.If(edges_unsorted(act, k, s) > 0):
                act.wait_ge(positions_ready, 1)
                for i in range(ring):
                    act.copy(ring_at[:, i:i + 1], position[:, i:i + 1]).then_inc(act_done, 1)
                    act.copy(ring_record[:, i * WORDS:(i + 1) * WORDS],
                             made[:, i * WORDS:(i + 1) * WORDS]).then_inc(act_done, 1)
                    act.wait_ge(act_done, 2)
                    act.sem_inc(act_done, -2)
                    act.sem_inc(slot_ready, 1)
                with act.Fori(0, turns - 1) as n:
                    for i in range(ring):
                        act.wait_ge(scattered[i], n * 16 + 16)
                        act.copy(ring_at[:, i:i + 1], position[:, bass.ds(n * ring + (ring + i), 1)]).then_inc(act_done, 1)
                        act.copy(ring_record[:, i * WORDS:(i + 1) * WORDS],
                                 made[:, bass.ds(n * (ring * WORDS) + (ring + i) * WORDS, WORDS)]).then_inc(act_done, 1)
                        act.wait_ge(act_done, 2)
                        act.sem_inc(act_done, -2)
                        act.sem_inc(slot_ready, 1)
                for i in range(ring):
                    act.wait_ge(scattered[i], 16 * turns)

        @block.vector
        def _(dve):
            dve.memset(k.x[:, (T - 1) * C:T * C], 0.0).then_inc(x_cleared, 1)
            dve.memset(first[:, T:T + 1], float(s.edges)).then_inc(dve_done, 1)
            dve.wait_ge(dve_done, 1)
            dve.sem_inc(dve_done, -1)
            dve.memset(place[:, 0:1], 0.0).then_inc(dve_done, 1)
            dve.wait_ge(dve_done, 1)
            dve.sem_inc(dve_done, -1)
            dve.wait_ge(edges_in, 16 * 8)
            dve.tensor_scalar(position[:], dst[:], P.bit_length() - 1, None, ALU.arith_shift_right).then_inc(dve_done, 1)
            dve.wait_ge(dve_done, 1)
            dve.sem_inc(dve_done, -1)
            dve.tensor_copy(tile_f[:], position[:]).then_inc(dve_done, 1)
            dve.wait_ge(dve_done, 1)
            dve.sem_inc(dve_done, -1)
            dve.tensor_scalar(next_dst[:], next_dst[:], P.bit_length() - 1, None, ALU.arith_shift_right).then_inc(dve_done, 1)
            dve.wait_ge(dve_done, 1)
            dve.sem_inc(dve_done, -1)
            dve.tensor_copy(next_tile[:], next_dst[:]).then_inc(dve_done, 1)
            dve.wait_ge(dve_done, 1)
            dve.sem_inc(dve_done, -1)
            dve.tensor_tensor(next_tile[:], next_tile[:], tile_f[:], ALU.is_lt).then_inc(dve_done, 1)
            dve.wait_ge(dve_done, 1)
            dve.sem_inc(dve_done, -1)
            dve.tensor_reduce(breaks[:], next_tile[:], AX.X, ALU.max).then_inc(breaks_ready, 1)
            for t in range(T):
                dve.tensor_scalar(in_tile[:, t * cols:(t + 1) * cols], tile_f[:], float(t), None,
                                  ALU.is_equal).then_inc(tiles_known, 1)
            dve.tensor_copy(int_fields[:, :, SRC], src[:]).then_inc(dve_done, 1)
            dve.scalar_tensor_tensor(out=int_fields[:, :, SRC_TYPE], in0=src[:], scalar=float(R), in1=kind[:],
                                     op0=ALU.mult, op1=ALU.add).then_inc(dve_done, 1)
            for word, array in ((DST, dst), (TYPE, kind), (WEIGHT, weight), (WEIGHT1, weight1)):
                dve.tensor_copy(fields[:, :, word], array[:]).then_inc(dve_done, 1)
            dve.wait_ge(dve_done, WORDS)
            dve.sem_inc(dve_done, -WORDS)
            dve.sem_inc(records_made, 1)
            dve.wait_ge(columns_counted, 1)
            dve.sem_inc(columns_counted, -1)
            dve.tensor_tensor_scan(place[:, 1:wide + 1], place[:, 1:wide + 1], place[:, 1:wide + 1],
                                   0.0, ALU.add, ALU.max).then_inc(dve_done, 1)
            dve.wait_ge(dve_done, 1)
            dve.sem_inc(dve_done, -1)
            dve.tensor_copy(first[:, 0:T], place[:, 0:wide].rearrange("p (t c) -> p t c", c=cols)[:, :, 0]).then_inc(dve_done, 1)
            dve.wait_ge(dve_done, 1)
            dve.sem_inc(dve_done, -1)
            dve.tensor_tensor(number[:], first[:, 1:T + 1], first[:, 0:T], ALU.subtract).then_inc(dve_done, 1)
            dve.wait_ge(dve_done, 1)
            dve.sem_inc(dve_done, -1)
            dve.wait_ge(constants, n_constants)
            dve.tensor_tensor(beyond[:], number[:].unsqueeze(2).broadcast_to([P, T, s.more]),
                              multiples[:].unsqueeze(1).broadcast_to([P, T, s.more]), ALU.is_gt).then_inc(dve_done, 1)
            dve.wait_ge(dve_done, 1)
            dve.sem_inc(dve_done, -1)
            dve.tensor_reduce(groups[:], beyond[:], AX.X, ALU.add).then_inc(dve_done, 1)
            dve.wait_ge(dve_done, 1)
            dve.sem_inc(dve_done, -1)
            dve.tensor_scalar(groups[:], groups[:], 1.0, None, ALU.add).then_inc(dve_done, 1)
            dve.wait_ge(dve_done, 1)
            dve.sem_inc(dve_done, -1)
            dve.tensor_tensor_scan(group_end[:], groups[:], groups[:], 0.0, ALU.add, ALU.max).then_inc(dve_done, 1)
            dve.wait_ge(dve_done, 1)
            dve.sem_inc(dve_done, -1)
            plan = k.plan[:].rearrange("p (t w) -> p t w", w=4)
            dve.tensor_reduce(part_of[:], k.identity[0:PARTS, 0:PARTS].rearrange("p (a h) -> p h a", h=HEADS),
                              AX.X, ALU.add).then_inc(dve_done, 1)
            dve.wait_ge(dve_done, 1)
            dve.sem_inc(dve_done, -1)
            dve.tensor_copy(k.pick[:], part_of[:].unsqueeze(2).broadcast_to([PARTS, HEADS, P])).then_inc(dve_done, 1)
            dve.wait_ge(dve_done, 1)
            dve.sem_inc(dve_done, -1)
            dve.tensor_copy(k.identity_b[:], k.identity[:]).then_inc(dve_done, 1)
            dve.wait_ge(dve_done, 1)
            dve.sem_inc(dve_done, -1)
            dve.tensor_copy(plan[:, :, 1], group_end[0:1, :]).then_inc(dve_done, 1)
            dve.tensor_copy(plan[:, :, 3], group_end[0:1, :]).then_inc(dve_done, 1)
            dve.tensor_copy(plan[:, :, 2], first[0:1, 0:T]).then_inc(dve_done, 1)
            dve.tensor_tensor(plan[:, :, 0], group_end[0:1, :], groups[0:1, :], ALU.subtract).then_inc(dve_done, 1)
            dve.wait_ge(dve_done, 4)
            dve.sem_inc(dve_done, -4)
            dve.wait_ge(breaks_counted, 1)
            dve.tensor_copy(k.unsorted[:], all_breaks[0:1, :]).then_inc(dve_done, 1)
            dve.wait_ge(dve_done, 1)
            dve.sem_inc(dve_done, -1)
            dve.sem_inc(order_known, 1)
            with dve.If(edges_unsorted(dve, k, s) > 0):
                for i, (at, n) in enumerate(pieces):
                    dve.wait_ge(before_ready, 1)
                    dve.sem_inc(before_ready, -1)
                    dve.tensor_tensor(place[0:rows, at:at + n], counted[0:rows, i % 2, 0:n],
                                      place[0:rows, at:at + n], ALU.add).then_inc(dve_done, 1)
                    dve.wait_ge(dve_done, 1)
                    dve.sem_inc(dve_done, -1)
                    dve.sem_inc(before_taken, 1)
                dve.tensor_tensor(place[0:rows, 0:wide], place[0:rows, 0:wide], in_tile, ALU.mult).then_inc(dve_done, 1)
                dve.wait_ge(dve_done, 1)
                dve.sem_inc(dve_done, -1)
                dve.tensor_reduce(tile_f[:], place[0:rows, 0:wide].rearrange("p (t c) -> p c t", c=cols),
                                  AX.X, ALU.add).then_inc(dve_done, 1)
                dve.wait_ge(dve_done, 1)
                dve.sem_inc(dve_done, -1)
                dve.tensor_copy(position[:], tile_f[:]).then_inc(dve_done, 1)
                dve.wait_ge(dve_done, 1)
                dve.sem_inc(dve_done, -1)
                dve.sem_inc(positions_ready, 1)

        @block.tensor
        def _(pe):
            pe.wait_ge(constants, n_constants)
            pe.wait_ge(breaks_ready, 1)
            pe.matmul(all_breaks[:], ones[:], breaks[:], start=True, stop=True).then_inc(breaks_counted, 1)
            pe.wait_ge(tiles_known, T)
            for i, (at, n) in enumerate(pieces):
                if i >= 2:
                    pe.wait_ge(counted_taken, 1)
                    pe.sem_inc(counted_taken, -1)
                pe.matmul(counted[:, i % 2, 0:n], ones[:], in_tile[:, at:at + n],
                          start=True, stop=True).then_inc(counted_ready, 1)
            pe.wait_ge(weights_in, 16 * weight_loads)
            for i in range(2):
                for b in range(KC):
                    for n in range(KC):
                        mm = pe.transpose(turned[:, i, b * C + n * P:b * C + (n + 1) * P],
                                          w_raw[:, i * KC + n, b * P:(b + 1) * P], k.identity[:])
            mm.then_inc(turned_ready, 1)
            pe.wait_ge(counted_taken, 2)
            pe.sem_inc(counted_taken, -2)
            pe.wait_ge(order_known, 1)
            with pe.If(edges_unsorted(pe, k, s) > 0):
                for i, (at, n) in enumerate(pieces):
                    if i >= 2:
                        pe.wait_ge(before_taken, 1)
                        pe.sem_inc(before_taken, -1)
                    pe.matmul(counted[0:rows, i % 2, 0:n], before[:], in_tile[:, at:at + n],
                              start=True, stop=True).then_inc(before_ready, 1)
                pe.wait_ge(before_taken, 2)
                pe.sem_inc(before_taken, -2)



def tile_groups(engine, k, s, t):
    g0 = engine.value_load(k.plan[0:1, bass.ds(t * 4, 1)], min_val=0, max_val=s.max_groups - 1)
    g1 = engine.value_load(k.plan[0:1, bass.ds(t * 4 + 1, 1)], min_val=1, max_val=s.max_groups)
    return g0, g1


def all_groups(engine, k, s):
    at = 4 * (s.tiles - 1) + 1
    return engine.value_load(k.plan[0:1, at:at + 1], min_val=1, max_val=s.max_groups)


def count(nc, k, s):
    T, R = s.tiles, s.relations
    with ExitStack() as ctx:
        def sb(name, shape, dtype=F32):
            return ctx.enter_context(nc.sbuf_tensor(name, shape, dtype))

        to_node = sb("c_to_node", [P, SLOTS, P], BF16)
        of_type = sb("c_of_type", [P, SLOTS, R], BF16)
        lane = sb("c_lane", [P, P], BF16)
        degree = sb("c_degree", [P, T])
        count_rest = sb("c_count_rest", [P, T, R])
        root = sb("c_root", [P, T])
        counted = ctx.enter_context(nc.psum_tensor("c_counted", [P, R], F32))
        fetched = k.sem("c_fetched")
        records_in = k.sem("c_records_in")
        masks_ready = k.sem("c_masks_ready")
        masks_used = k.sem("c_masks_used")
        tile_counted = k.sem("c_tile_counted")
        tile_taken = k.sem("c_tile_taken")
        degree_ready = k.sem("c_degree_ready")
        root_ready = k.sem("c_root_ready")
        done = k.sem("c_done")
        words = k.records[:].rearrange("p c w -> p (c w)")
        block = ctx.enter_context(nc.Block())

        @block.sync
        def _(sp):
            with sp.Fori(0, T) as t:
                g0, g1 = tile_groups(sp, k, s, t)
                start = sp.value_load(k.plan[0:1, bass.ds(t * 4 + 2, 1)], min_val=0, max_val=s.edges)
                with sp.Fori(0, g1 - g0) as g:
                    group = nc.s_assert_within(g0 + g, 0, s.max_groups - 1, skip_runtime_bounds_check_because=
                                               "the plan ends a tile's groups at max_groups")
                    edge = nc.s_assert_within(start + g * s.group, 0, s.edges, skip_runtime_bounds_check_because=
                                              "a tile has one group, and more only while they begin at its edges")
                    sp.dma_start(words[:, bass.ds(group * (SLOTS * WORDS), SLOTS * WORDS)],
                                 k.edge_records[bass.ds(edge, s.group), :].rearrange(
                                     "(p c) w -> p (c w)", p=P)).then_inc(fetched, 16)
                    sp.wait_ge(fetched, 16)
                    sp.sem_inc(fetched, -16)
                    sp.sem_inc(records_in, 1)

        @block.vector
        def _(dve):
            def trios(g):
                for i in range(TRIOS):
                    at = bass.ds(g * SLOTS + i * TRIO, TRIO)
                    its = slice(i * TRIO, (i + 1) * TRIO)
                    dve.wait_ge(masks_used, 1)
                    dve.sem_inc(masks_used, -1)
                    for j in range(i * TRIO, (i + 1) * TRIO):
                        dve.tensor_scalar(to_node[:, j, :], lane[:], k.dst_in_tile[:, bass.ds(g * SLOTS + j, 1)], None,
                                          ALU.is_equal).then_inc(done, 1)
                    dve.tensor_tensor(of_type[:, its, :], k.relation[:],
                                      k.records[:, at, TYPE:TYPE + 1].broadcast_to([P, TRIO, R]),
                                      ALU.is_equal).then_inc(masks_ready, 1)
                dve.wait_ge(done, SLOTS + 1)
                dve.sem_inc(done, -(SLOTS + 1))

            dve.tensor_copy(lane[:], k.lane[:]).then_inc(done, 1)
            dve.wait_ge(done, 1)
            dve.sem_inc(done, -1)
            with dve.Fori(0, T) as t:
                g0, g1 = tile_groups(dve, k, s, t)
                with dve.Fori(g0, g1) as g:
                    dve.wait_ge(records_in, 1)
                    dve.sem_inc(records_in, -1)
                    dve.tensor_scalar(k.dst_in_tile[:, bass.ds(g * SLOTS, SLOTS)],
                                      k.records[:, bass.ds(g * SLOTS, SLOTS), DST],
                                      k.tile_base[:, bass.ds(t, 1)], None, ALU.subtract).then_inc(done, 1)
                    dve.wait_ge(done, 1)
                    dve.sem_inc(done, -1)
                    dve.tensor_copy(k.dst_bf16[:, bass.ds(g * SLOTS, SLOTS)],
                                    k.dst_in_tile[:, bass.ds(g * SLOTS, SLOTS)]).then_inc(done, 1)
                    trios(g)
                dve.wait_ge(tile_counted, 1)
                dve.sem_inc(tile_counted, -1)
                dve.tensor_copy(k.counts[:, bass.ds(t * R, R)], counted[:]).then_inc(done, 1)
                dve.wait_ge(done, 1)
                dve.sem_inc(done, -1)
                dve.sem_inc(tile_taken, 1)
            dve.tensor_scalar(k.one_over_count[:], k.counts[:], 1.0, None, ALU.max).then_inc(done, 1)
            dve.wait_ge(done, 1)
            dve.sem_inc(done, -1)
            dve.reciprocal(k.one_over_count[:], k.one_over_count[:]).then_inc(done, 1)
            dve.tensor_reduce(degree[:], k.counts[:].rearrange("p (t r) -> p t r", r=R), AX.X, ALU.add).then_inc(done, 1)
            dve.wait_ge(done, 2)
            dve.sem_inc(done, -2)
            value = k.one_over_count[:].rearrange("p (t r) -> p t r", r=R)
            for i in range(3):
                dve.tensor_copy(k.count_parts[:, :, i, :], value).then_inc(done, 1)
                dve.wait_ge(done, 1)
                dve.sem_inc(done, -1)
                if i < 2:
                    dve.tensor_tensor(count_rest[:], value, k.count_parts[:, :, i, :], ALU.subtract).then_inc(done, 1)
                    dve.wait_ge(done, 1)
                    dve.sem_inc(done, -1)
                    value = count_rest[:]
            dve.tensor_scalar(degree[:], degree[:], 1.0, None, ALU.add).then_inc(degree_ready, 1)
            dve.wait_ge(root_ready, 1)
            dve.reciprocal(k.dinv[:], root[:]).then_inc(done, 1)
            dve.wait_ge(done, 1)
            dve.sem_inc(done, -1)

        @block.scalar
        def _(act):
            act.wait_ge(degree_ready, 1)
            act.activation(root[:], degree[:], ACT.Sqrt).then_inc(root_ready, 1)

        @block.tensor
        def _(pe):
            pe.sem_inc(masks_used, TRIOS)
            pe.sem_inc(tile_taken, 1)
            with pe.Fori(0, T) as t:
                g0, g1 = tile_groups(pe, k, s, t)
                pe.wait_ge(tile_taken, 1)
                pe.sem_inc(tile_taken, -1)
                pe.matmul(counted[:], k.zeros[:, 0:P], k.zeros[:, 0:R], start=True, stop=False)
                with pe.Fori(g0, g1):
                    for i in range(TRIOS):
                        pe.wait_ge(masks_ready, 1)
                        pe.sem_inc(masks_ready, -1)
                        for j in range(i * TRIO, (i + 1) * TRIO):
                            mm = pe.matmul(counted[:], to_node[:, j, :], of_type[:, j, :], start=False, stop=False)
                        mm.then_inc(masks_used, 1)
                pe.matmul(counted[:], k.zeros[:, 0:P], k.zeros[:, 0:R], start=False, stop=True).then_inc(tile_counted, 1)


class Dense:

    def __init__(self, nc, ctx, k, s):
        def sb(n, shape, dtype=F32):
            return ctx.enter_context(nc.sbuf_tensor(f"dense_{n}", shape, dtype))

        self.row = sb("row", [P, s.width])
        self.stats = sb("stats", [P, 6])
        self.mean_var = sb("mean_var", [P, 2])
        self.deviation = sb("deviation", [P, 1])
        self.turned = sb("turned", [P, KC, P])
        self.row_ready = k.sem("row_ready")
        self.row_used = k.sem("row_used")
        self.var_ready = k.sem("var_ready")
        self.deviation_ready = k.sem("deviation_ready")
        self.transposed = k.sem("transposed")
        self.turned_ready = k.sem("turned_ready")
        self.product_ready = k.sem("product_ready")
        self.product_taken = k.sem("product_taken")
        self.kept = k.sem("kept")
        self.stored = k.sem("stored")
        self.done = k.sem("done")
        self.act_done = k.sem("act_done")
        self.acc_ready = k.sem("acc_ready")
        self.acc_taken = k.sem("acc_taken")
        self.slot_used = k.sem("slot_used")
        self.mask_ready = k.sem("mask_ready")
        self.index_ready = k.sem("index_ready")
        bank = ctx.enter_context(nc.psum_tensor("dense", [P, 2, s.width], F32))
        self.in_psum, self.product = bank[:, 0, :], bank[:, 1, :]


def normalize_start(dve, k, s, d, t):
    x = k.x[:, bass.ds(t * s.width, s.width)]
    dve.bn_stats(d.stats[:], x).then_inc(d.done, 1)
    dve.wait_ge(d.done, 1)
    dve.sem_inc(d.done, -1)
    dve.bn_aggr(d.mean_var[:], d.stats[:]).then_inc(d.done, 1)
    dve.wait_ge(d.done, 1)
    dve.sem_inc(d.done, -1)
    dve.tensor_scalar(d.deviation[:], d.mean_var[:, 1:2], EPS, None, ALU.add).then_inc(d.done, 1)
    dve.wait_ge(d.done, 1)
    dve.sem_inc(d.done, -1)
    dve.sem_inc(d.var_ready, 1)


def normalize_finish(dve, k, s, d, t):
    x = k.x[:, bass.ds(t * s.width, s.width)]
    dve.wait_ge(d.deviation_ready, 1)
    dve.sem_inc(d.deviation_ready, -1)
    dve.reciprocal(d.deviation[:], d.deviation[:]).then_inc(d.done, 1)
    dve.wait_ge(d.done, 1)
    dve.sem_inc(d.done, -1)
    dve.tensor_scalar(d.row[:], x, d.mean_var[:, 0:1], d.deviation[:], ALU.subtract, ALU.mult).then_inc(d.row_ready, 1)


def normalize(dve, k, s, d, t):
    normalize_start(dve, k, s, d, t)
    normalize_finish(dve, k, s, d, t)


def square_root(act, d):
    act.wait_ge(d.var_ready, 1)
    act.sem_inc(d.var_ready, -1)
    act.activation(d.deviation[:], d.deviation[:], ACT.Sqrt).then_inc(d.deviation_ready, 1)


def transposed_row(pe, k, d):
    pe.wait_ge(d.row_ready, 1)
    pe.sem_inc(d.row_ready, -1)
    pe.wait_ge(d.product_taken, 1)
    pe.sem_inc(d.product_taken, -1)
    for b in range(KC):
        mm = pe.transpose(d.in_psum[:, b * P:(b + 1) * P], d.row[:, b * P:(b + 1) * P], k.identity[:])
    mm.then_inc(d.transposed, 1)


def relu_turned(act, d):
    act.wait_ge(d.transposed, 1)
    act.sem_inc(d.transposed, -1)
    act.activation(d.turned[:].rearrange("p k n -> p (k n)"), d.in_psum, ACT.Relu).then_inc(d.act_done, 1)
    act.wait_ge(d.act_done, 1)
    act.sem_inc(d.act_done, -1)
    act.sem_inc(d.turned_ready, 1)
    act.sem_inc(d.row_used, 1)


def product(pe, k, s, d, weights, bias):
    pe.wait_ge(d.turned_ready, 1)
    pe.sem_inc(d.turned_ready, -1)
    for b in range(KC):
        mm = pe.matmul(d.product, d.turned[:, b, :], weights[:, b, :],
                       start=(b == 0), stop=(b == KC - 1 and bias is None))
    if bias is not None:
        mm = pe.matmul(d.product, k.ones_row[:], bias, start=False, stop=True)
    mm.then_inc(d.product_ready, 1)


class ToTable:

    def __init__(self, k, s, layer, source):
        self.k, self.s, self.layer = k, s, layer
        self.gcn = source == "gcn"
        self.weights = k.w_gcn[:, (layer + 1) * KC:(layer + 2) * KC, :] if self.gcn else k.w_out[:, KC:2 * KC, :]
        self.bias = None if self.gcn else k.bias_out[:, 1, :]
        self.table = k.table[(layer + 1) % 2]
        self.roots = False
        self.late = False
        self.dense = True

    def open(self, nc, ctx, d):
        self.d = d

    def dve(self, dve, t, acc):
        k, s, d = self.k, self.s, self.d
        dve.wait_ge(d.row_used, 1)
        dve.sem_inc(d.row_used, -1)
        layer_sum(dve, k, s, d, t, acc, k.bias_gcn[:, self.layer, :] if self.gcn else None)
        dve.sem_inc(d.row_ready, 1)

    def pe(self, pe):
        transposed_row(pe, self.k, self.d)
        product(pe, self.k, self.s, self.d, self.weights, self.bias)

    def act(self, act, t):
        k, s, d = self.k, self.s, self.d
        act.wait_ge(d.product_ready, 1)
        act.sem_inc(d.product_ready, -1)
        act.activation(k.own[:, bass.ds(t * s.width, s.width)], d.product, ACT.Copy,
                       scale=k.dinv[:, bass.ds(t, 1)]).then_inc(d.act_done, 1)
        act.wait_ge(d.act_done, 1)
        act.sem_inc(d.act_done, -1)
        act.sem_inc(d.product_taken, 1)
        act.sem_inc(d.kept, 1)

    def sp(self, sp, t):
        k, s, d = self.k, self.s, self.d
        sp.wait_ge(d.kept, 1)
        sp.sem_inc(d.kept, -1)
        sp.dma_start(self.table[bass.ds(t * P, P), :], k.own[:, bass.ds(t * s.width, s.width)]).then_inc(d.stored, 16)
        sp.wait_ge(d.stored, 16)
        sp.sem_inc(d.stored, -16)


def layer_sum(dve, k, s, d, t, acc, bias):
    dve.tensor_tensor(d.row[:], acc[:, 0:s.width], k.own[:, bass.ds(t * s.width, s.width)], ALU.add).then_inc(d.done, 1)
    dve.wait_ge(d.done, 1)
    dve.sem_inc(d.done, -1)
    dve.sem_inc(d.acc_taken, 1)
    if bias is None:
        dve.tensor_scalar(d.row[:], d.row[:], k.dinv[:, bass.ds(t, 1)], None, ALU.mult).then_inc(d.done, 1)
        dve.wait_ge(d.done, 1)
        dve.sem_inc(d.done, -1)
    else:
        dve.scalar_tensor_tensor(out=d.row[:], in0=d.row[:], scalar=k.dinv[:, bass.ds(t, 1)], in1=bias,
                                 op0=ALU.mult, op1=ALU.add).then_inc(d.done, 1)
        dve.wait_ge(d.done, 1)
        dve.sem_inc(d.done, -1)


def add_relu_row(dve, k, s, d, t):
    x = k.x[:, bass.ds(t * s.width, s.width)]
    dve.scalar_tensor_tensor(out=x, in0=d.row[:], scalar=0.0, in1=x, op0=ALU.max, op1=ALU.add).then_inc(d.done, 1)
    dve.wait_ge(d.done, 1)
    dve.sem_inc(d.done, -1)


class ToRelations:

    def __init__(self, k, s):
        self.k, self.s = k, s
        self.roots = True
        self.late = False
        self.dense = True

    def open(self, nc, ctx, d):
        self.d = d
        self.staged = ctx.enter_context(nc.sbuf_tensor("relations_staged", [P, self.s.relations * self.s.width], F32))
        self.pair = ctx.enter_context(nc.psum_tensor("relations_pair", [P, 2, 512], F32))
        self.pair_ready = self.k.sem("relations_pair_ready")
        self.pair_taken = self.k.sem("relations_pair_taken")
        self.staged_free = self.k.sem("relations_staged_free")

    def dve(self, dve, t, acc):
        k, s, d = self.k, self.s, self.d
        dve.wait_ge(d.row_used, 1)
        dve.sem_inc(d.row_used, -1)
        layer_sum(dve, k, s, d, t, acc, k.bias_gcn[:, 2, :])
        add_relu_row(dve, k, s, d, t)
        normalize(dve, k, s, d, t)

    def pe(self, pe):
        k, s, d = self.k, self.s, self.d
        transposed_row(pe, k, d)
        product(pe, k, s, d, k.w_root[:], k.bias_root[:])
        by_half = k.w_relation[:].rearrange("p (r k) c -> p k r c", k=KC)
        for i in range(s.relations // 2):
            pe.wait_ge(self.pair_taken, 1)
            pe.sem_inc(self.pair_taken, -1)
            for b in range(KC):
                mm = pe.matmul(self.pair[:, i % 2, :], d.turned[:, b, :], by_half[:, b, 2 * i:2 * i + 2, :],
                               start=(b == 0), stop=(b == KC - 1))
            mm.then_inc(self.pair_ready, 1)

    def act(self, act, t):
        k, s, d = self.k, self.s, self.d
        act.wait_ge(d.product_ready, 1)
        act.sem_inc(d.product_ready, -1)
        act.copy(k.own[:, bass.ds(t * s.width, s.width)], d.product).then_inc(d.act_done, 1)
        act.wait_ge(d.act_done, 1)
        act.sem_inc(d.act_done, -1)
        act.sem_inc(d.product_taken, 1)
        act.wait_ge(self.staged_free, 1)
        act.sem_inc(self.staged_free, -1)
        for i in range(s.relations // 2):
            act.wait_ge(self.pair_ready, 1)
            act.sem_inc(self.pair_ready, -1)
            act.copy(self.staged[:, i * 512:(i + 1) * 512], self.pair[:, i % 2, :]).then_inc(d.act_done, 1)
            act.wait_ge(d.act_done, 1)
            act.sem_inc(d.act_done, -1)
            act.sem_inc(self.pair_taken, 1)
        act.sem_inc(d.kept, 1)

    def sp(self, sp, t):
        k, s, d = self.k, self.s, self.d
        sp.wait_ge(d.kept, 1)
        sp.sem_inc(d.kept, -1)
        sp.dma_start(k.relation_table[bass.ds(t * (P * s.relations), P * s.relations), :].rearrange(
            "(p r) c -> p (r c)", r=s.relations), self.staged[:]).then_inc(d.stored, 16)
        sp.wait_ge(d.stored, 16)
        sp.sem_inc(d.stored, -16)
        sp.sem_inc(self.staged_free, 1)


class ToAttention:

    def __init__(self, k, s):
        self.k, self.s = k, s
        self.roots = True
        self.late = True
        self.dense = True

    def open(self, nc, ctx, d):
        self.d = d
        self.weighed = ctx.enter_context(nc.sbuf_tensor("attention_weighed", [P, 2, self.s.width], F32))
        self.rest = ctx.enter_context(nc.sbuf_tensor("attention_rest", [P, HEADS], F32))
        self.h_ready = self.k.sem("attention_h_ready")

    def dve(self, dve, t, acc):
        k, s, d = self.k, self.s, self.d
        x = k.x[:, bass.ds(t * s.width, s.width)]
        dve.tensor_tensor(x, x, acc[:, 0:s.width], ALU.add).then_inc(d.done, 1)
        dve.wait_ge(d.done, 1)
        dve.sem_inc(d.done, -1)
        dve.sem_inc(d.acc_taken, 1)
        dve.tensor_tensor(x, x, k.own[:, bass.ds(t * s.width, s.width)], ALU.add).then_inc(d.done, 1)
        dve.wait_ge(d.done, 1)
        dve.sem_inc(d.done, -1)
        dve.wait_ge(d.row_used, 1)
        dve.sem_inc(d.row_used, -1)
        normalize(dve, k, s, d, t)

    def dve_late(self, dve, t):
        k, s, d = self.k, self.s, self.d
        dve.wait_ge(self.h_ready, 1)
        dve.sem_inc(self.h_ready, -1)
        h = k.own[:, bass.ds(t * s.width, s.width)].unsqueeze(1).broadcast_to([P, 2, s.width])
        dve.tensor_tensor(self.weighed[:], h, k.att[:], ALU.mult).then_inc(d.done, 1)
        dve.wait_ge(d.done, 1)
        dve.sem_inc(d.done, -1)
        dve.tensor_reduce(k.attention[:].rearrange("p t h -> p (t h)")[:, bass.ds(t * 2 * HEADS, 2 * HEADS)],
                          self.weighed[:].rearrange("p a (h c) -> p (a h) c", h=HEADS), AX.X, ALU.add).then_inc(d.done, 1)
        dve.wait_ge(d.done, 1)
        dve.sem_inc(d.done, -1)
        parts = k.parts[:].bitcast(BF16)
        value = k.attention[:].rearrange("p t h -> p (t h)")[:, bass.ds(t * 2 * HEADS, HEADS)]
        for i in range(3):
            part = parts[:, bass.ds(t * PARTS + i * HEADS, HEADS)]
            dve.tensor_copy(part, value).then_inc(d.done, 1)
            dve.wait_ge(d.done, 1)
            dve.sem_inc(d.done, -1)
            if i < 2:
                dve.tensor_tensor(self.rest[:], value, part, ALU.subtract).then_inc(d.done, 1)
                dve.wait_ge(d.done, 1)
                dve.sem_inc(d.done, -1)
                value = self.rest[:]
        dve.sem_inc(d.kept, 1)

    def pe(self, pe):
        transposed_row(pe, self.k, self.d)
        product(pe, self.k, self.s, self.d, self.k.w_gat[:], None)

    def act(self, act, t):
        k, s, d = self.k, self.s, self.d
        act.wait_ge(d.product_ready, 1)
        act.sem_inc(d.product_ready, -1)
        act.copy(k.own[:, bass.ds(t * s.width, s.width)], d.product).then_inc(d.act_done, 1)
        act.wait_ge(d.act_done, 1)
        act.sem_inc(d.act_done, -1)
        act.sem_inc(d.product_taken, 1)
        act.sem_inc(self.h_ready, 1)

    def sp(self, sp, t):
        k, s, d = self.k, self.s, self.d
        sp.wait_ge(d.kept, 1)
        sp.sem_inc(d.kept, -1)
        rows = k.gat_table[bass.ds(t * P, P), :]
        sp.dma_start(rows[:, 0:s.width], k.own[:, bass.ds(t * s.width, s.width)]).then_inc(d.stored, 16)
        sp.dma_start(rows[:, s.width:s.width + HEADS],
                     k.attention[:].rearrange("p t h -> p (t h)")[:, bass.ds(t * 2 * HEADS, HEADS)]).then_inc(d.stored, 16)
        sp.dma_start(rows[:, s.width + HEADS:], k.parts[:, bass.ds(t * PART_WORDS, PART_WORDS)]).then_inc(d.stored, 16)
        sp.wait_ge(d.stored, 48)
        sp.sem_inc(d.stored, -48)


class ToOutput:

    def __init__(self, k, s, out):
        self.k, self.s, self.out = k, s, out
        self.roots = False
        self.late = False
        self.dense = False

    def open(self, nc, ctx, d):
        self.d = d

    def dve(self, dve, t, acc):
        k, s, d = self.k, self.s, self.d
        layer_sum(dve, k, s, d, t, acc, None)
        add_relu_row(dve, k, s, d, t)
        dve.sem_inc(d.kept, 1)

    def sp(self, sp, t):
        k, s, d = self.k, self.s, self.d
        sp.wait_ge(d.kept, 1)
        sp.sem_inc(d.kept, -1)
        sp.dma_start(self.out[bass.ds(t * P, P), :], k.x[:, bass.ds(t * s.width, s.width)]).then_inc(d.stored, 16)
        sp.wait_ge(d.stored, 16)
        sp.sem_inc(d.stored, -16)

    def sp_last(self, sp):
        k, s, d = self.k, self.s, self.d
        t = s.tiles - 1
        sp.wait_ge(d.kept, 1)
        sp.dma_start(self.out[t * P:s.nodes, :], k.x[0:s.last, t * s.width:(t + 1) * s.width]).then_inc(d.stored, 16)
        sp.wait_ge(d.stored, 16)


def project_input(nc, k, s):
    T, C = s.tiles, s.width
    with ExitStack() as ctx:
        def sb(n, shape, dtype=F32):
            return ctx.enter_context(nc.sbuf_tensor(f"input_{n}", shape, dtype))

        d = k.dense
        to = ToTable(k, s, layer=-1, source="gcn")
        to.open(nc, ctx, d)
        stats = sb("stats", [P, T, 6])
        mean_var = sb("mean_var", [P, T, 2])
        deviation = sb("deviation", [P, T])
        in_psum = ctx.enter_context(nc.psum_tensor("input_in_psum", [P, 512], F32))[:, 0:C]
        row_free = k.sem("input_row_free")
        block = ctx.enter_context(nc.Block())

        @block.sync
        def _(sp):
            with sp.Fori(0, T) as t:
                to.sp(sp, t)

        @block.vector
        def _(dve):
            dve.sem_inc(d.row_used, 1)
            dve.sem_inc(d.acc_taken, 1)
            for t in range(T):
                dve.bn_stats(stats[:, t, :], k.x[:, t * C:(t + 1) * C]).then_inc(d.done, 1)
            dve.wait_ge(d.done, T)
            dve.sem_inc(d.done, -T)
            for t in range(T):
                dve.bn_aggr(mean_var[:, t, :], stats[:, t, :]).then_inc(d.done, 1)
            dve.wait_ge(d.done, T)
            dve.sem_inc(d.done, -T)
            dve.tensor_scalar(deviation[:], mean_var[:, :, 1], EPS, None, ALU.add).then_inc(d.done, 1)
            dve.wait_ge(d.done, 1)
            dve.sem_inc(d.done, -1)
            dve.sem_inc(d.var_ready, 1)
            dve.wait_ge(d.deviation_ready, 1)
            dve.sem_inc(d.deviation_ready, -1)
            dve.reciprocal(deviation[:], deviation[:]).then_inc(d.done, 1)
            dve.wait_ge(d.done, 1)
            dve.sem_inc(d.done, -1)
            with dve.Fori(0, T) as t:
                dve.wait_ge(row_free, 1)
                dve.sem_inc(row_free, -1)
                dve.tensor_scalar(d.row[:], k.x[:, bass.ds(t * C, C)],
                                  mean_var[:].rearrange("p t m -> p (t m)")[:, bass.ds(t * 2, 1)],
                                  deviation[:, bass.ds(t, 1)], ALU.subtract, ALU.mult).then_inc(d.row_ready, 1)

        @block.scalar
        def _(act):
            act.wait_ge(d.var_ready, 1)
            act.sem_inc(d.var_ready, -1)
            act.activation(deviation[:], deviation[:], ACT.Sqrt).then_inc(d.deviation_ready, 1)
            with act.Fori(0, T) as t:
                act.wait_ge(d.transposed, 1)
                act.sem_inc(d.transposed, -1)
                act.sem_inc(row_free, 1)
                act.activation(d.turned[:].rearrange("p k n -> p (k n)"), in_psum, ACT.Relu).then_inc(d.act_done, 1)
                act.wait_ge(d.act_done, 1)
                act.sem_inc(d.act_done, -1)
                act.sem_inc(d.turned_ready, 1)
                to.act(act, t)

        @block.tensor
        def _(pe):
            def transposes():
                pe.wait_ge(d.row_ready, 1)
                pe.sem_inc(d.row_ready, -1)
                for b in range(KC):
                    mm = pe.transpose(in_psum[:, b * P:(b + 1) * P], d.row[:, b * P:(b + 1) * P], k.identity[:])
                mm.then_inc(d.transposed, 1)

            def layer():
                pe.wait_ge(d.product_taken, 1)
                pe.sem_inc(d.product_taken, -1)
                product(pe, k, s, d, to.weights, None)

            pe.sem_inc(d.product_taken, 1)
            pe.sem_inc(row_free, 1)
            transposes()
            with pe.Fori(0, T - 1):
                pe.wait_ge(d.turned_ready, 1)
                transposes()
                layer()
            layer()


def landings(groups, passes, g, further=0):
    return (groups * passes + g) * 16 + (16 + further * 16) if passes else g * 16 + 16


def aggregate(nc, k, s, name, table, to, index, weights, find_means=False):
    C, T, R = s.width, s.tiles, s.relations
    with ExitStack() as ctx:
        def sb(n, shape, dtype=F32):
            return ctx.enter_context(nc.sbuf_tensor(f"{name}_{n}", shape, dtype))

        def psum(n, shape, dtype=F32):
            return ctx.enter_context(nc.psum_tensor(f"{name}_{n}", shape, dtype))

        gathered = sb("gathered", [P, SLOTS, C])
        to_node = sb("to_node", [P, SLOTS, P])
        indices = sb("indices", [P, SLOTS], I32)
        acc = psum("acc", [P, C])
        d = k.dense
        landed, passes, further = k.landed, k.passes, k.further
        k.passes += 1
        to.open(nc, ctx, d)
        if find_means:
            from_node = sb("from_node", [P, TRIO, P], BF16)
            apart = sb("apart", [P, TRIO, P])
            of_type = sb("of_type", [P, TRIO, R])
            typed = sb("typed", [P, TRIO, 3, R])
            turned = psum("turned", [P, TRIO, P])
            found = psum("found", [P, TRIO, 3, R])
            turned_ready = k.sem(f"{name}_turned_ready")
            from_ready = k.sem(f"{name}_from_ready")
            found_ready = k.sem(f"{name}_found_ready")
            found_taken = k.sem(f"{name}_found_taken")
        source = k.records[:].bitcast(I32)
        block = ctx.enter_context(nc.Block())

        @block.gpsimd
        def _(pool):
            with pool.Fori(0, all_groups(pool, k, s)):
                for i in range(SLOTS):
                    if i % TRIO == 0:
                        pool.wait_ge(d.index_ready, 1)
                        pool.sem_inc(d.index_ready, -1)
                    pool.indirect_dma_start(gathered[:, i, :], None, table,
                                            IndirectOffsetOnAxis(ap=indices[:, i:i + 1], axis=0)).then_inc(landed[i], 16)
            pool.wait_ge(d.index_ready, TRIOS)
            pool.sem_inc(d.index_ready, -TRIOS)

        @block.vector
        def _(dve):
            def find_mean(g, i):
                at = bass.ds(g * SLOTS + i * TRIO, TRIO)
                dve.tensor_tensor(of_type[:], k.relation[:],
                                  k.records[:, at, TYPE:TYPE + 1].broadcast_to([P, TRIO, R]),
                                  ALU.is_equal).then_inc(d.done, 1)
                dve.wait_ge(d.done, 1)
                dve.sem_inc(d.done, -1)
                dve.wait_ge(found_ready, 1)
                dve.sem_inc(found_ready, -1)
                dve.tensor_tensor(typed[:], of_type[:].unsqueeze(2).broadcast_to([P, TRIO, 3, R]), found[:],
                                  ALU.mult).then_inc(d.done, 1)
                dve.wait_ge(d.done, 1)
                dve.sem_inc(d.done, -1)
                dve.sem_inc(found_taken, 1)
                dve.tensor_reduce(k.mean_weight[:, at], typed[:].rearrange("p c q r -> p c (q r)"),
                                  AX.X, ALU.add).then_inc(d.done, 1)
                dve.wait_ge(d.done, 1)
                dve.sem_inc(d.done, -1)
                dve.tensor_tensor(k.mean_weight[:, at], k.mean_weight[:, at],
                                  k.records[:, at, WEIGHT], ALU.mult).then_inc(d.done, 1)
                dve.wait_ge(d.done, 1)
                dve.sem_inc(d.done, -1)

            def trio(g, i):
                dve.wait_ge(d.slot_used, 1)
                dve.sem_inc(d.slot_used, -1)
                dve.tensor_copy(indices[:, i * TRIO:(i + 1) * TRIO],
                                source[:, bass.ds(g * SLOTS + i * TRIO, TRIO), index]).then_inc(d.done, 1)
                dve.wait_ge(d.done, 1)
                dve.sem_inc(d.done, -1)
                dve.sem_inc(d.index_ready, 1)
                for j in range(i * TRIO, (i + 1) * TRIO):
                    at = bass.ds(g * SLOTS + j, 1)
                    if weights is None:
                        mask = dve.tensor_scalar(to_node[:, j, :], k.lane[:], k.dst_in_tile[:, at], None,
                                                 ALU.is_equal)
                    else:
                        weight = k.mean_weight[:, at] if weights == "mean" else k.records[:, at, WEIGHT1]
                        mask = dve.tensor_scalar(to_node[:, j, :], k.lane[:], k.dst_in_tile[:, at], weight,
                                                 ALU.is_equal, ALU.mult)
                mask.then_inc(d.mask_ready, 1)

            def tile(t):
                g0, g1 = tile_groups(dve, k, s, t)
                with dve.Fori(g0, g1) as g:
                    for i in range(TRIOS):
                        trio(g + 1, i)
                        if find_means:
                            find_mean(g, i)
                dve.wait_ge(d.acc_ready, 1)
                dve.sem_inc(d.acc_ready, -1)
                to.dve(dve, t, acc)

            dve.sem_inc(d.slot_used, TRIOS)
            for i in range(TRIOS):
                trio(0, i)
            if to.late:
                tile(0)
                with dve.Fori(0, T - 1) as t:
                    tile(t + 1)
                    to.dve_late(dve, t)
                to.dve_late(dve, T - 1)
            else:
                with dve.Fori(0, T) as t:
                    tile(t)

        @block.tensor
        def _(pe):
            groups = all_groups(pe, k, s)

            def tile(t):
                g0, g1 = tile_groups(pe, k, s, t)
                pe.wait_ge(d.acc_taken, 1)
                pe.sem_inc(d.acc_taken, -1)
                pe.matmul(acc[:], k.zeros[:, 0:P], k.zeros[:, 0:C], start=True, stop=False)
                with pe.Fori(g0, g1) as g:
                    for i in range(TRIOS):
                        pe.wait_ge(d.mask_ready, 1)
                        pe.sem_inc(d.mask_ready, -1)
                        if find_means:
                            for j in range(TRIO):
                                mm = pe.matmul(turned[:, j, :], k.dst_bf16[:, bass.ds(g * SLOTS + i * TRIO + j, 1)]
                                               .broadcast_to([P, P]), k.identity_b[:], start=True, stop=True)
                            mm.then_inc(turned_ready, 1)
                        for j in range(i * TRIO, (i + 1) * TRIO):
                            pe.wait_ge(landed[j], landings(groups, passes, g, further if j < SLOTS // 2 + TRIO else 0))
                            mm = pe.matmul(acc[:], to_node[:, j, :], gathered[:, j, :], start=False, stop=False)
                        mm.then_inc(d.slot_used, 1)
                        if find_means:
                            pe.wait_ge(from_ready, 1)
                            pe.sem_inc(from_ready, -1)
                            pe.wait_ge(found_taken, 1)
                            pe.sem_inc(found_taken, -1)
                            for j in range(TRIO):
                                mm = pe.matmul(found[:, j, :, :].rearrange("p q r -> p (q r)"), from_node[:, j, :],
                                               k.count_parts[:].rearrange("p t q r -> p (t q r)")[
                                                   :, bass.ds(t * (3 * R), 3 * R)], start=True, stop=True)
                            mm.then_inc(found_ready, 1)
                pe.matmul(acc[:], k.zeros[:, 0:P], k.zeros[:, 0:C], start=False, stop=True).then_inc(d.acc_ready, 1)

            if find_means:
                pe.sem_inc(found_taken, 1)
            if to.dense:
                if isinstance(to, ToRelations):
                    pe.sem_inc(to.pair_taken, 2)
                tile(0)
                with pe.Fori(1, T) as t:
                    tile(t)
                    to.pe(pe)
                to.pe(pe)
            else:
                with pe.Fori(0, T) as t:
                    tile(t)
            pe.wait_ge(d.mask_ready, TRIOS)
            pe.sem_inc(d.mask_ready, -TRIOS)

        if to.dense:
            @block.scalar
            def _(act):
                def turn(t):
                    g0, g1 = tile_groups(act, k, s, t)
                    with act.Fori(g0, g1):
                        for i in range(TRIOS):
                            act.wait_ge(turned_ready, 1)
                            act.sem_inc(turned_ready, -1)
                            act.activation(apart[:], turned[:], ACT.Square, bias=k.minus_node[:]).then_inc(d.act_done, 1)
                            act.wait_ge(d.act_done, 1)
                            act.sem_inc(d.act_done, -1)
                            act.activation(from_node[:], apart[:], ACT.Relu, scale=-1.0, bias=1.0).then_inc(from_ready, 1)

                if isinstance(to, ToRelations):
                    act.sem_inc(to.staged_free, 1)
                if to.roots:
                    square_root(act, d)
                if find_means:
                    turn(0)
                with act.Fori(0, T - 1) as t:
                    if find_means:
                        turn(t + 1)
                    relu_turned(act, d)
                    if to.roots:
                        square_root(act, d)
                    to.act(act, t)
                relu_turned(act, d)
                to.act(act, T - 1)

        @block.sync
        def _(sp):
            if to.dense:
                with sp.Fori(0, T) as t:
                    to.sp(sp, t)
            else:
                with sp.Fori(0, T - 1) as t:
                    to.sp(sp, t)
                to.sp_last(sp)


def attend(nc, k, s):
    C, T = s.width, s.tiles
    HALF = SLOTS // 2
    HTRIOS = TRIOS // 2
    HC = C // HEADS
    W = C + HEADS
    ROW = W + PART_WORDS
    with ExitStack() as ctx:
        def sb(n, shape, dtype=F32):
            return ctx.enter_context(nc.sbuf_tensor(f"attend_{n}", shape, dtype))

        def psum(n, shape, dtype=F32):
            return ctx.enter_context(nc.psum_tensor(f"attend_{n}", shape, dtype))

        gathered = sb("gathered", [P, SLOTS, ROW])
        to_node = sb("to_node", [P, SLOTS, P])
        from_node = sb("from_node", [P, SLOTS, P], BF16)
        apart = sb("apart", [P, TRIO * P])
        outside = sb("outside", [P, 2, TRIO * P])
        part_rows = sb("part_rows", [PARTS, TRIO * P], BF16)
        masked = sb("masked", [P, HEADS, TRIO * P])
        indices = sb("indices", [P, SLOTS], I32)
        maxima = sb("maxima", [P, HEADS, HTRIOS + 1])
        source_max = sb("source_max", [P, HEADS])
        logit = sb("logit", [P, HEADS])
        target = sb("target", [P, HEADS])
        top = sb("top", [P, 2, HEADS])
        rest = sb("rest", [P, 2, HEADS])
        target_parts = sb("target_parts", [P, 3, 2 * HEADS], BF16)
        decay = sb("decay", [P, HEADS])
        found_sum = sb("found_sum", [P, HALF, 2 * HEADS])
        logits = sb("logits", [P, HALF, HEADS])
        sums = sb("sums", [P, W])
        last_sums = sb("last_sums", [P, W])
        inverse = sb("inverse", [P, HEADS])
        spread = psum("spread", [P, HEADS, 512])
        turned = psum("turned", [P, TRIO * P])
        part_turned = psum("part_turned", [PARTS, TRIO * P])
        bank = psum("bank", [P, 512])
        acc = bank[:, 0:W]
        found = bank[:, W:W + HALF * 6 * HEADS].rearrange("p (c h) -> p c h", h=6 * HEADS)
        d = k.dense
        turned_ready = k.sem("attend_turned_ready")
        copied = k.sem("attend_copied")
        spread_ready = k.sem("attend_spread_ready")
        spread_taken = k.sem("attend_spread_taken")
        target_ready = k.sem("attend_target_ready")
        decay_asked = k.sem("attend_decay_asked")
        decay_ready = k.sem("attend_decay_ready")
        found_ready = k.sem("attend_found_ready")
        logits_ready = k.sem("attend_logits_ready")
        weights_ready = k.sem("attend_weights_ready")
        scaled_dve = k.sem("attend_scaled_dve")
        scaled_act = k.sem("attend_scaled_act")
        landed, passes = k.landed, k.passes
        k.passes += 1
        k.further += 1
        source = k.records[:].bitcast(I32)
        parts = gathered[:].bitcast(BF16)[:, :, 2 * W:2 * W + PARTS]
        block = ctx.enter_context(nc.Block())

        @block.gpsimd
        def _(pool):
            def gathers(g, trios):
                for i in trios:
                    pool.wait_ge(d.slot_used, 1)
                    pool.sem_inc(d.slot_used, -1)
                    pool.tensor_copy(indices[:, i * TRIO:(i + 1) * TRIO],
                                     source[:, bass.ds(g * SLOTS + i * TRIO, TRIO), SRC]).then_inc(d.index_ready, 1)
                    pool.wait_ge(d.index_ready, 1)
                    pool.sem_inc(d.index_ready, -1)
                    for j in range(i * TRIO, (i + 1) * TRIO):
                        pool.indirect_dma_start(gathered[:, j, :], None, k.gat_table,
                                                IndirectOffsetOnAxis(ap=indices[:, j:j + 1], axis=0)
                                                ).then_inc(landed[j], 16)

            pool.sem_inc(d.slot_used, TRIOS)
            groups = all_groups(pool, k, s)
            with pool.Fori(0, groups) as g:
                gathers(g, range(TRIOS))
            gathers(groups, range(HTRIOS + 1))
            pool.wait_ge(d.slot_used, HTRIOS - 1)
            pool.sem_inc(d.slot_used, -(HTRIOS - 1))

        @block.vector
        def _(dve):
            by_head = "p (h c) -> p h c"

            def leaky(out, z):
                dve.scalar_tensor_tensor(out=out, in0=z, scalar=SLOPE, in1=z, op0=ALU.mult, op1=ALU.max).then_inc(d.done, 1)
                dve.wait_ge(d.done, 1)
                dve.sem_inc(d.done, -1)

            def in_parts(value, at):
                hi, mid, lo = (target_parts[:, i, at:at + HEADS] for i in range(3))
                dve.tensor_copy(hi, value).then_inc(d.done, 1)
                dve.wait_ge(d.done, 1)
                dve.sem_inc(d.done, -1)
                dve.tensor_tensor(mid, value, hi, ALU.subtract).then_inc(d.done, 1)
                dve.tensor_tensor(rest[:, 0, :], value, hi, ALU.subtract).then_inc(d.done, 1)
                dve.wait_ge(d.done, 2)
                dve.sem_inc(d.done, -2)
                dve.tensor_tensor(lo, rest[:, 0, :], mid, ALU.subtract).then_inc(d.done, 1)
                dve.wait_ge(d.done, 1)
                dve.sem_inc(d.done, -1)

            def masks(g, i):
                for j in range(i * TRIO, (i + 1) * TRIO):
                    dve.tensor_scalar(to_node[:, j, :], k.lane[:], k.dst_in_tile[:, bass.ds(g * SLOTS + j, 1)],
                                      None, ALU.is_equal).then_inc(d.done, 1)
                dve.wait_ge(d.done, TRIO)
                dve.sem_inc(d.done, -TRIO)

            def largest(i):
                dve.wait_ge(spread_ready, 1)
                dve.sem_inc(spread_ready, -1)
                for h in range(HEADS):
                    dve.tensor_tensor_reduce(
                        out=masked[:, h, :], in0=spread[:, h, 0:TRIO * P], in1=outside[:, i % 2, :],
                        scale=1.0, scalar=-FAR, op0=ALU.add, op1=ALU.max,
                        accum_out=maxima[:, h, i % HTRIOS:i % HTRIOS + 1]).then_inc(d.done, 1)
                dve.wait_ge(d.done, HEADS)
                dve.sem_inc(d.done, -HEADS)
                dve.sem_inc(spread_taken, 1)

            def add_sums():
                dve.wait_ge(d.acc_ready, 1)
                dve.sem_inc(d.acc_ready, -1)
                dve.sem_inc(d.slot_used, 1)
                dve.tensor_tensor(sums[:], sums[:], acc, ALU.add).then_inc(d.done, 1)
                dve.wait_ge(d.done, 1)
                dve.sem_inc(d.done, -1)

            def half(g, this, tail=None):
                ahead, other = (0, 1) if this == 0 else (1, 0)
                its = slice(this * HALF, (this + 1) * HALF)
                dve.tensor_reduce(source_max[:], maxima[:], AX.X, ALU.max).then_inc(d.done, 1)
                dve.wait_ge(d.done, 1)
                dve.sem_inc(d.done, -1)
                dve.tensor_tensor(logit[:], source_max[:], target[:], ALU.add).then_inc(d.done, 1)
                dve.wait_ge(d.done, 1)
                dve.sem_inc(d.done, -1)
                leaky(top[:, this, :], logit[:])
                in_parts(top[:, this, :], HEADS)
                dve.sem_inc(target_ready, 1)
                dve.tensor_copy(maxima[:, :, HTRIOS], source_max[:]).then_inc(d.done, 1)
                dve.tensor_tensor(decay[:], top[:, other, :], top[:, this, :], ALU.subtract).then_inc(d.done, 1)
                dve.wait_ge(d.done, 2)
                dve.sem_inc(d.done, -2)
                dve.sem_inc(decay_asked, 1)
                dve.wait_ge(found_ready, 1)
                dve.sem_inc(found_ready, -1)
                dve.tensor_reduce(found_sum[:], found.rearrange("p c (q h) -> p c h q", q=3), AX.X, ALU.add).then_inc(d.done, 1)
                dve.wait_ge(d.done, 1)
                dve.sem_inc(d.done, -1)
                dve.tensor_tensor(logits[:], gathered[:, its, C:W], found_sum[:, :, 0:HEADS], ALU.add).then_inc(d.done, 1)
                dve.wait_ge(d.done, 1)
                dve.sem_inc(d.done, -1)
                leaky(logits[:], logits[:])
                dve.tensor_tensor(logits[:], logits[:], found_sum[:, :, HEADS:2 * HEADS], ALU.subtract).then_inc(d.done, 1)
                dve.wait_ge(d.done, 1)
                dve.sem_inc(d.done, -1)
                dve.tensor_scalar(logits[:], logits[:], 0.0, None, ALU.min).then_inc(d.done, 1)
                dve.wait_ge(d.done, 1)
                dve.sem_inc(d.done, -1)
                dve.sem_inc(logits_ready, 1)
                if this == 1:
                    add_sums()
                masks(g + ahead, other * HTRIOS)
                dve.wait_ge(weights_ready, 1)
                dve.sem_inc(weights_ready, -1)
                for i in range(HTRIOS):
                    at = this * HALF + i * TRIO
                    rows = gathered[:, at:at + TRIO - 1, 0:C].rearrange("p s (h c) -> p s h c", h=HEADS)
                    dve.tensor_tensor(rows, rows, gathered[:, at:at + TRIO - 1, C:W].unsqueeze(3).broadcast_to(
                        [P, TRIO - 1, HEADS, HC]), ALU.mult).then_inc(scaled_dve, 1)
                dve.wait_ge(decay_ready, 1)
                dve.sem_inc(decay_ready, -1)
                rows = sums[:, 0:C].rearrange(by_head, h=HEADS)
                dve.tensor_tensor(rows, rows, decay[:].unsqueeze(2).broadcast_to([P, HEADS, HC]),
                                  ALU.mult).then_inc(d.done, 1)
                dve.tensor_tensor(sums[:, C:W], sums[:, C:W], decay[:], ALU.mult).then_inc(d.done, 1)
                dve.wait_ge(d.done, 2)
                dve.sem_inc(d.done, -2)
                if tail is not None:
                    residual(tail)
                largest(other * HTRIOS)
                if tail is not None:
                    normalize_finish(dve, k, s, d, tail)
                masks(g + ahead, other * HTRIOS + 1)
                largest(other * HTRIOS + 1)
                masks(g + ahead, other * HTRIOS + 2)
                largest(other * HTRIOS + 2)
                if this == 1:
                    add_sums()

            def residual(t):
                dve.wait_ge(d.row_used, 1)
                dve.sem_inc(d.row_used, -1)
                dve.tensor_scalar(inverse[:], last_sums[:, C:W], 1e-16, None, ALU.add).then_inc(d.done, 1)
                dve.wait_ge(d.done, 1)
                dve.sem_inc(d.done, -1)
                dve.reciprocal(inverse[:], inverse[:]).then_inc(d.done, 1)
                dve.wait_ge(d.done, 1)
                dve.sem_inc(d.done, -1)
                dve.tensor_tensor(d.row[:].rearrange(by_head, h=HEADS),
                                  last_sums[:, 0:C].rearrange(by_head, h=HEADS),
                                  inverse[:].unsqueeze(2).broadcast_to([P, HEADS, HC]), ALU.mult).then_inc(d.done, 1)
                dve.wait_ge(d.done, 1)
                dve.sem_inc(d.done, -1)
                dve.tensor_tensor(d.row[:], d.row[:], k.bias_gat[:], ALU.add).then_inc(d.done, 1)
                dve.wait_ge(d.done, 1)
                dve.sem_inc(d.done, -1)
                add_relu_row(dve, k, s, d, t)
                normalize_start(dve, k, s, d, t)

            def tile(t, tail=None):
                node = k.attention[:].rearrange("p t h -> p (t h)")
                g0, g1 = tile_groups(dve, k, s, t)
                dve.tensor_copy(maxima[:, :, HTRIOS], node[:, bass.ds(t * 2 * HEADS, HEADS)]).then_inc(d.done, 1)
                dve.tensor_copy(target[:], node[:, bass.ds(t * 2 * HEADS + HEADS, HEADS)]).then_inc(d.done, 1)
                dve.tensor_copy(sums[:, 0:C], k.own[:, bass.ds(t * C, C)]).then_inc(d.done, 1)
                dve.memset(sums[:, C:W], 1.0).then_inc(d.done, 1)
                dve.wait_ge(d.done, 4)
                dve.sem_inc(d.done, -4)
                dve.tensor_tensor(logit[:], maxima[:, :, HTRIOS], target[:], ALU.add).then_inc(d.done, 1)
                dve.wait_ge(d.done, 1)
                dve.sem_inc(d.done, -1)
                leaky(top[:, 1, :], logit[:])
                in_parts(target[:], 0)
                half(g0, 0, tail)
                half(g0, 1)
                with dve.If(g1 > g0 + 1):
                    with dve.Fori(g0 + 1, g1) as g:
                        half(g, 0)
                        half(g, 1)
                dve.tensor_copy(last_sums[:], sums[:]).then_inc(d.done, 1)
                dve.wait_ge(d.done, 1)
                dve.sem_inc(d.done, -1)

            for i in range(HTRIOS):
                masks(0, i)
                largest(i)
            tile(0)
            with dve.Fori(1, T) as t:
                tile(t, tail=t - 1)
            residual(T - 1)
            normalize_finish(dve, k, s, d, T - 1)

        @block.tensor
        def _(pe):
            groups = all_groups(pe, k, s)

            def turn(g, i):
                for j in range(TRIO):
                    pe.matmul(turned[:, j * P:(j + 1) * P],
                              k.dst_bf16[:, bass.ds(g * SLOTS + i * TRIO + j, 1)].broadcast_to([P, P]), k.identity_b[:],
                              start=True, stop=True)
                for j in range(TRIO):
                    pe.wait_ge(landed[i * TRIO + j], landings(groups, passes, g))
                    mm = pe.matmul(part_turned[:, j * P:(j + 1) * P], parts[:, i * TRIO + j, :], k.identity_b[:],
                                   start=True, stop=True)
                mm.then_inc(turned_ready, 1)

            def spread_heads():
                pe.wait_ge(copied, 1)
                pe.sem_inc(copied, -1)
                pe.wait_ge(spread_taken, 1)
                pe.sem_inc(spread_taken, -1)
                for h in range(HEADS):
                    mm = pe.matmul(spread[:, h, 0:TRIO * P], k.pick[:, h, :], part_rows[:], start=True, stop=True)
                mm.then_inc(spread_ready, 1)

            def sum_trio(this, i):
                pe.wait_ge(scaled_dve, 1)
                pe.sem_inc(scaled_dve, -1)
                pe.wait_ge(scaled_act, 1)
                pe.sem_inc(scaled_act, -1)
                for j in range(i * TRIO, (i + 1) * TRIO):
                    slot = this * HALF + j
                    mm = pe.matmul(acc, to_node[:, slot, :], gathered[:, slot, 0:W],
                                   start=(j == 0), stop=(j == HALF - 1))
                mm.then_inc(d.acc_ready if i == HTRIOS - 1 else d.slot_used, 1)

            def half(g, this, tail=False):
                ahead, other = (0, 1) if this == 0 else (1, 0)
                pe.wait_ge(target_ready, 1)
                pe.sem_inc(target_ready, -1)
                for j in range(this * HALF, (this + 1) * HALF):
                    mm = pe.matmul(found[:, j - this * HALF, :], from_node[:, j, :],
                                   target_parts[:].rearrange("p q h -> p (q h)"), start=True, stop=True)
                mm.then_inc(found_ready, 1)
                spread_heads()
                turn(g + ahead, other * HTRIOS + 1)
                sum_trio(this, 0)
                spread_heads()
                turn(g + ahead, other * HTRIOS + 2)
                sum_trio(this, 1)
                spread_heads()
                turn(g + 1, this * HTRIOS)
                if tail:
                    transposed_row(pe, k, d)
                sum_trio(this, 2)
                if tail:
                    product(pe, k, s, d, k.w_out[:, 0:KC, :], k.bias_out[:, 0, :])

            def tile(t, tail):
                g0, g1 = tile_groups(pe, k, s, t)
                half(g0, 0, tail)
                half(g0, 1)
                with pe.If(g1 > g0 + 1):
                    with pe.Fori(g0 + 1, g1) as g:
                        half(g, 0)
                        half(g, 1)

            pe.sem_inc(spread_taken, 1)
            for i in range(HTRIOS):
                turn(0, i)
                spread_heads()
            turn(0, HTRIOS)
            tile(0, False)
            with pe.Fori(1, T) as t:
                tile(t, True)
            transposed_row(pe, k, d)
            product(pe, k, s, d, k.w_out[:, 0:KC, :], k.bias_out[:, 0, :])

        @block.scalar
        def _(act):
            def turn(i):
                act.wait_ge(turned_ready, 1)
                act.sem_inc(turned_ready, -1)
                act.copy(part_rows[:], part_turned[:]).then_inc(d.act_done, 1)
                act.activation(apart[:], turned[:], ACT.Square, bias=k.minus_node[:]).then_inc(d.act_done, 1)
                act.wait_ge(d.act_done, 2)
                act.sem_inc(d.act_done, -2)
                trio = from_node[:, i * TRIO:(i + 1) * TRIO, :].rearrange("p c e -> p (c e)")
                act.activation(trio, apart[:], ACT.Relu, scale=-1.0, bias=1.0).then_inc(d.act_done, 1)
                act.wait_ge(d.act_done, 1)
                act.sem_inc(d.act_done, -1)
                act.activation(outside[:, i % 2, :], trio, ACT.Copy, scale=FAR, bias=-FAR).then_inc(d.act_done, 1)
                act.wait_ge(d.act_done, 1)
                act.sem_inc(d.act_done, -1)
                act.sem_inc(copied, 1)

            def scale(this, i):
                at = this * HALF + (i + 1) * TRIO - 1
                for h in range(HEADS):
                    head = gathered[:, at, h * HC:(h + 1) * HC]
                    act.activation(head, head, ACT.Copy, scale=gathered[:, at, C + h:C + h + 1]).then_inc(d.act_done, 1)
                act.wait_ge(d.act_done, HEADS)
                act.sem_inc(d.act_done, -HEADS)
                act.sem_inc(scaled_act, 1)

            def keep_product(t):
                relu_turned(act, d)
                act.wait_ge(d.product_ready, 1)
                act.sem_inc(d.product_ready, -1)
                act.activation(k.own[:, bass.ds(t * C, C)], d.product, ACT.Copy,
                               scale=k.dinv[:, bass.ds(t, 1)]).then_inc(d.act_done, 1)
                act.wait_ge(d.act_done, 1)
                act.sem_inc(d.act_done, -1)
                act.sem_inc(d.product_taken, 1)
                act.sem_inc(d.kept, 1)

            def half(this, tail=None):
                other = 1 - this
                act.wait_ge(decay_asked, 1)
                act.sem_inc(decay_asked, -1)
                act.activation(decay[:], decay[:], ACT.Exp).then_inc(decay_ready, 1)
                act.wait_ge(logits_ready, 1)
                act.sem_inc(logits_ready, -1)
                act.activation(gathered[:, this * HALF:(this + 1) * HALF, C:W], logits[:], ACT.Exp).then_inc(d.act_done, 1)
                act.wait_ge(d.act_done, 1)
                act.sem_inc(d.act_done, -1)
                act.sem_inc(weights_ready, 1)
                scale(this, 0)
                turn(other * HTRIOS + 1)
                scale(this, 1)
                scale(this, 2)
                if tail is not None:
                    square_root(act, d)
                turn(other * HTRIOS + 2)
                turn(this * HTRIOS)
                if tail is not None:
                    keep_product(tail)

            def tile(t, tail=None):
                g0, g1 = tile_groups(act, k, s, t)
                half(0, tail)
                half(1)
                with act.If(g1 > g0 + 1):
                    with act.Fori(g0 + 1, g1):
                        half(0)
                        half(1)

            for i in range(HTRIOS + 1):
                turn(i)
            tile(0)
            with act.Fori(1, T) as t:
                tile(t, tail=t - 1)
            square_root(act, d)
            keep_product(T - 1)

        @block.sync
        def _(sp):
            with sp.Fori(0, T) as t:
                sp.wait_ge(d.kept, 1)
                sp.sem_inc(d.kept, -1)
                sp.dma_start(k.table[0][bass.ds(t * P, P), :], k.own[:, bass.ds(t * C, C)]).then_inc(d.stored, 16)
                sp.wait_ge(d.stored, 16)
                sp.sem_inc(d.stored, -16)


INPUTS = ["x", "src", "dst", "edge_type_8", "edge_weight", "edge_weight1", "L0_gnn_W", "L0_gnn_b",
          "L1_gnn_weight", "L1_gnn_root", "L1_gnn_bias", "L2_gnn_W", "L2_gnn_att_src", "L2_gnn_att_dst",
          "L2_gnn_bias", "L3_gnn_W1", "L3_gnn_b1", "L3_gnn_W2", "L3_gnn_b2"]


def gnn_block(nc, a, out):
    nodes, width = a["x"].shape
    s = Shapes(nodes, a["src"].shape[0], width, a["L1_gnn_weight"].shape[0])
    with ExitStack() as ctx:
        k = Core(nc, ctx, s)
        prepare(nc, k, s, a)
        count(nc, k, s)
        k.dense = Dense(nc, ctx, k, s)
        project_input(nc, k, s)
        gcn = dict(index=SRC, weights=None)
        aggregate(nc, k, s, "gcn0", k.table[0], ToTable(k, s, layer=0, source="gcn"), **gcn)
        aggregate(nc, k, s, "gcn1", k.table[1], ToTable(k, s, layer=1, source="gcn"),
                  find_means=True, **gcn)
        aggregate(nc, k, s, "gcn2", k.table[0], ToRelations(k, s), **gcn)
        aggregate(nc, k, s, "relations", k.relation_table, ToAttention(k, s), index=SRC_TYPE, weights="mean")
        attend(nc, k, s)
        aggregate(nc, k, s, "out0", k.table[0], ToTable(k, s, layer=0, source="out"), index=SRC, weights="weight1")
        aggregate(nc, k, s, "out1", k.table[1], ToOutput(k, s, out), index=SRC, weights="weight1")


def kernel(**inputs):
    import concourse.bacc as bacc
    import numpy as np
    from concourse.bass_utils import run_bass_kernel_spmd

    nc = bacc.Bacc("TRN2", target_bir_lowering=False, num_devices=1)
    arrays = {f"in_{name}": np.ascontiguousarray(inputs[name]) for name in INPUTS}
    a = {name: nc.dram_tensor(f"in_{name}", arrays[f"in_{name}"].shape,
                              mybir.dt.from_np(arrays[f"in_{name}"].dtype), kind="ExternalInput").ap()
         for name in INPUTS}
    out = nc.dram_tensor("out", inputs["x"].shape, F32, kind="ExternalOutput").ap()
    gnn_block(nc, a, out)
    r = run_bass_kernel_spmd(nc, [arrays], core_ids=[0])
    return r.results[0]["out"]
```

```python
from contextlib import ExitStack

import concourse.bass as bass
from concourse import mybir
from concourse.bass import IndirectOffsetOnAxis

F32 = mybir.dt.float32
BF16 = mybir.dt.bfloat16
I32 = mybir.dt.int32
ALU = mybir.AluOpType
ACT = mybir.ActivationFunctionType
AX = mybir.AxisListType

P = 128
TRIO = 3
TRIOS = 6
SLOTS = TRIO * TRIOS
WORDS = 6
SRC, SRC_TYPE, DST, TYPE, WEIGHT, WEIGHT1 = range(WORDS)
HEADS = 4
SLOPE = 0.2
EPS = 1e-5
FAR = 1.0e30
PARTS = 3 * 2 * HEADS
PART_WORDS = PARTS // 2
WARM_BEFORE, WARM_BEHIND = 12, 20
KC = 2


class Shapes:

    def __init__(self, nodes, edges, width, relations):
        self.nodes, self.edges, self.width, self.relations = nodes, edges, width, relations
        self.tiles = -(-nodes // P)
        self.last = nodes - (self.tiles - 1) * P
        self.rows = max(r for r in range(1, P + 1) if edges % r == 0)
        self.cols = edges // self.rows
        self.group = SLOTS * P
        self.max_groups = self.tiles + edges // self.group
        self.more = self.max_groups - self.tiles






class Core:

    def __init__(self, nc, ctx, s):
        def sb(name, shape, dtype=F32):
            return ctx.enter_context(nc.sbuf_tensor(name, shape, dtype))

        self.sem = lambda name: ctx.enter_context(nc.semaphore(name))
        self.semaphores = lambda name, n: [self.sem(f"{name}{i}") for i in range(n)]
        self.landed = self.semaphores("landed", SLOTS)
        self.passes, self.further = 0, 0
        C, R = s.width, s.relations
        self.identity = sb("identity", [P, P])
        self.lane = sb("lane", [P, P])
        self.relation = sb("relation", [P, TRIO, R])
        self.tile_base = sb("tile_base", [P, s.tiles])
        self.group_base = sb("group_base", [P, s.max_groups])
        self.group_plan = sb("group_plan", [1, s.max_groups], I32)
        self.zeros = sb("zeros", [P, 512], BF16)
        self.ones_row = sb("ones_row", [1, P])
        self.plan = sb("plan", [1, s.tiles * 4], I32)
        self.unsorted = sb("unsorted", [1, 1], I32)
        self.x = sb("x_resident", [P, s.tiles * C])
        self.own = sb("own", [P, s.tiles * C])
        self.records = sb("records", [P, (s.max_groups + 1) * SLOTS, WORDS])
        self.dst_in_tile = sb("dst_in_tile", [P, (s.max_groups + 1) * SLOTS])
        self.dst_bf16 = sb("dst_bf16", [P, (s.max_groups + 1) * SLOTS], BF16)
        self.minus_node = sb("minus_node", [P, 1])
        self.count_parts = sb("count_parts", [P, s.tiles, 3, R], BF16)
        self.in_scale = sb("in_scale", [P, s.tiles])
        self.in_shift = sb("in_shift", [P, s.tiles])
        self.mean_weight = sb("mean_weight", [P, (s.max_groups + 1) * SLOTS])
        self.counts = sb("counts", [P, s.tiles * R])
        self.one_over_count = sb("one_over_count", [P, s.tiles * R])
        self.dinv = sb("dinv", [P, s.tiles])
        self.attention = sb("attention", [P, s.tiles * 3 * HEADS])
        self.parts = sb("parts", [P, s.tiles * PART_WORDS])
        self.identity_b = sb("identity_b", [P, P], BF16)
        self.pick = sb("pick", [PARTS, HEADS, P], BF16)
        self.w_gcn = sb("w_gcn", [P, 3 * KC, C])
        self.w_relation = sb("w_relation", [P, R * KC, C])
        self.w_root = sb("w_root", [P, KC, C])
        self.w_gat = sb("w_gat", [P, KC, C])
        self.w_out = sb("w_out", [P, 2 * KC, C])
        self.bias_gcn = sb("bias_gcn", [P, 3, C])
        self.bias_gat = sb("bias_gat", [P, C])
        self.att = sb("att", [P, 2, C])
        self.bias_out_all = sb("bias_out_all", [P, C])
        self.bias_root = sb("bias_root", [1, C])
        self.bias_out = sb("bias_out", [1, 2, C])
        dram = nc.dram_tensor
        self.edge_records = dram("edge_records", (s.edges + s.group, WORDS), F32).ap()
        n = s.tiles * P
        self.table = [dram(f"table_{i}", (n, C), F32).ap() for i in range(2)]
        self.relation_table = dram("relation_table", (n * R, C), F32).ap()
        self.gat_table = dram("gat_table", (n, C + HEADS + PART_WORDS), F32).ap()


def edges_unsorted(engine, k, s):
    return engine.value_load(k.unsorted[0:1, 0:1], min_val=0, max_val=s.rows)


def prepare(nc, k, s, a):
    C, T, R = s.width, s.tiles, s.relations
    with ExitStack() as ctx:
        def sb(name, shape, dtype=F32):
            return ctx.enter_context(nc.sbuf_tensor(name, shape, dtype))

        def psum(name, shape, dtype=F32):
            return ctx.enter_context(nc.psum_tensor(name, shape, dtype))

        rows, cols = s.rows, s.cols
        wide = T * cols
        pieces = [(i, min(512, wide - i)) for i in range(0, wide, 512)]
        ring = 5
        turns = cols // ring
        assert turns * ring == cols
        src = sb("p_src", [rows, cols], I32)
        dst = sb("p_dst", [rows, cols], I32)
        kind = sb("p_kind", [rows, cols], I32)
        weight = sb("p_weight", [rows, cols])
        weight1 = sb("p_weight1", [rows, cols])
        made = sb("p_made", [rows, cols * WORDS])
        tile_f = sb("p_tile_f", [rows, cols])
        place = sb("p_place", [P, wide + 1])
        before = sb("p_before", [rows, rows], BF16)
        ones = sb("p_ones", [rows, P], BF16)
        position = sb("p_position", [rows, cols], I32)
        next_dst = sb("p_next_dst", [rows, cols], I32)
        next_tile = sb("p_next_tile", [rows, cols])
        breaks = sb("p_breaks", [rows, 1], BF16)
        first = sb("p_first", [P, T + 1])
        number = sb("p_number", [P, T])
        multiples = sb("p_multiples", [P, s.more])
        beyond = sb("p_beyond", [P, T, s.more])
        numbers = sb("p_numbers", [P, s.max_groups])
        behind = sb("p_behind", [P, s.max_groups, T])
        group_tile = sb("p_group_tile", [P, s.max_groups])
        lead = sb("p_lead", [P, T])
        group_lead = sb("p_group_lead", [P, s.max_groups])
        groups = sb("p_groups", [P, T])
        group_end = sb("p_group_end", [P, T])
        part_of = sb("p_part_of", [PARTS, HEADS])
        stats = sb("p_stats", [P, T, 6])
        mean_var = sb("p_mean_var", [P, T, 2])
        pad = sb("p_pad", [P, SLOTS, WORDS])
        ring_at = sb("p_ring_at", [rows, ring], I32)
        ring_record = sb("p_ring_record", [rows, ring * WORDS])
        counted = psum("p_counted", [P, 2, 512])
        all_breaks = psum("p_all_breaks", [P, 1])
        turned = psum("p_turned", [P, 2, 512])
        fields = made[:].rearrange("p (c w) -> p c w", w=WORDS)
        int_fields = fields.bitcast(I32)
        w_raw = k.own[:, 0:2 * KC * C].rearrange("p (k c) -> p k c", c=C)
        in_tile = k.own[0:rows, 2 * KC * C:].bitcast(BF16)[:, 0:wide]

        edges_in = k.sem("edges_in")
        x_in = k.sem("x_in")
        weights_in = k.sem("weights_in")
        x_cleared = k.sem("x_cleared")
        constants = k.sem("p_constants")
        drafts = k.sem("p_drafts")
        pad_ready = k.sem("p_pad_ready")
        pad_out = k.sem("p_pad_out")
        tiles_known = k.sem("p_tiles_known")
        counted_ready = k.sem("p_counted_ready")
        counted_taken = k.sem("p_counted_taken")
        columns_counted = k.sem("p_columns_counted")
        before_ready = k.sem("p_before_ready")
        before_taken = k.sem("p_before_taken")
        turned_ready = k.sem("p_turned_ready")
        positions_ready = k.sem("p_positions_ready")
        slot_ready = k.sem("p_slot_ready")
        scattered = k.semaphores("p_scattered", ring)
        variance_ready = k.sem("p_variance_ready")
        root_ready = k.sem("p_root_ready")
        records_made = k.sem("p_records_made")
        in_place = k.sem("p_in_place")
        breaks_ready = k.sem("p_breaks_ready")
        breaks_counted = k.sem("p_breaks_counted")
        order_known = k.sem("p_order_known")
        dve_done = k.sem("p_dve_done")
        act_done = k.sem("p_act_done")
        weight_loads = 2 * 3 + R + 2 + 2 + 1 + 1 + 1 + 2 + 2
        n_constants = 15
        block = ctx.enter_context(nc.Block())

        @block.sync
        def _(sp):
            for buffer, name in ((dst, "dst"), (src, "src"), (kind, "edge_type_8"), (weight, "edge_weight")):
                sp.dma_start(buffer[:], a[name].rearrange("(p c) -> p c", c=cols)).then_inc(edges_in, 16)
            sp.dma_start(weight1[:], a["edge_weight1"].rearrange("(p c) o -> p (c o)", c=cols)).then_inc(edges_in, 16)
            last_row = (rows - 1) * cols
            sp.dma_start(next_dst[0:rows - 1, :], a["dst"][1:last_row + 1].rearrange("(p c) -> p c", c=cols)
                         ).then_inc(edges_in, 16)
            sp.dma_start(next_dst[rows - 1:rows, 0:cols - 1], a["dst"][last_row + 1:s.edges].unsqueeze(0)
                         ).then_inc(edges_in, 16)
            sp.dma_start(next_dst[rows - 1:rows, cols - 1:cols], a["dst"][s.edges - 1:s.edges].unsqueeze(0)
                         ).then_inc(edges_in, 16)
            sp.dma_start(k.x[:, 0:(T - 1) * C].rearrange("p (t c) -> p t c", c=C),
                         a["x"][0:(T - 1) * P, :].rearrange("(t p) c -> p t c", p=P)).then_inc(x_in, 16)
            sp.wait_ge(x_cleared, 1)
            sp.dma_start(k.x[0:s.last, (T - 1) * C:T * C], a["x"][(T - 1) * P:s.nodes, :]).then_inc(x_in, 16)
            for l in range(3):
                sp.dma_start(k.w_gcn[:, l * KC:(l + 1) * KC, :],
                             a["L0_gnn_W"][l].rearrange("(k p) c -> p k c", p=P)).then_inc(weights_in, 16)
                sp.dma_start(k.bias_gcn[:, l, :], a["L0_gnn_b"][l].partition_broadcast(P)).then_inc(weights_in, 16)
            for r in range(R):
                sp.dma_start(k.w_relation[:, r * KC:(r + 1) * KC, :],
                             a["L1_gnn_weight"][r].rearrange("(k p) c -> p k c", p=P)).then_inc(weights_in, 16)
            for buffer, name in ((k.w_root, "L1_gnn_root"), (k.w_gat, "L2_gnn_W")):
                sp.dma_start(buffer[:], a[name].rearrange("(k p) c -> p k c", p=P)).then_inc(weights_in, 16)
            for i, name in enumerate(("L3_gnn_W1", "L3_gnn_W2")):
                sp.dma_start(w_raw[:, i * KC:(i + 1) * KC, :],
                             a[name].rearrange("(k p) c -> p k c", p=P)).then_inc(weights_in, 16)
            sp.dma_start(k.bias_gat[:], a["L2_gnn_bias"].partition_broadcast(P)).then_inc(weights_in, 16)
            sp.dma_start(k.bias_out_all[:], a["L3_gnn_b1"].partition_broadcast(P)).then_inc(weights_in, 16)
            sp.dma_start(k.bias_root[:], a["L1_gnn_bias"].unsqueeze(0)).then_inc(weights_in, 16)
            for i, name in enumerate(("L3_gnn_b1", "L3_gnn_b2")):
                sp.dma_start(k.bias_out[:, i, :], a[name].unsqueeze(0)).then_inc(weights_in, 16)
            for i, name in enumerate(("L2_gnn_att_src", "L2_gnn_att_dst")):
                sp.dma_start(k.att[:, i, :],
                             a[name].rearrange("h c -> (h c)").partition_broadcast(P)).then_inc(weights_in, 16)
            sp.wait_ge(pad_ready, 1)
            sp.dma_start(k.edge_records[s.edges:s.edges + s.group, :].rearrange("(p c) w -> p c w", p=P),
                         pad[:]).then_inc(pad_out, 16)
            sp.wait_ge(records_made, 1)
            sp.dma_start(k.edge_records[0:s.edges, :].rearrange("(p c) w -> p (c w)", c=cols), made[:]).then_inc(in_place, 16)
            sp.wait_ge(in_place, 16)
            sp.wait_ge(pad_out, 16)
            sp.wait_ge(x_in, 32)
            sp.wait_ge(weights_in, 16 * weight_loads)

        @block.gpsimd
        def _(pool):
            pool.iota(k.lane[:], [[1, P]], base=0, channel_multiplier=0,
                      allow_small_or_imprecise_dtypes=True).then_inc(constants, 1)
            pool.iota(k.relation[:], [[0, TRIO], [1, R]], base=0, channel_multiplier=0,
                      allow_small_or_imprecise_dtypes=True).then_inc(constants, 1)
            pool.iota(k.tile_base[:], [[P, T]], base=0, channel_multiplier=0,
                      allow_small_or_imprecise_dtypes=True).then_inc(constants, 1)
            pool.iota(multiples[:], [[s.group, s.more]], base=s.group, channel_multiplier=0,
                      allow_small_or_imprecise_dtypes=True).then_inc(constants, 1)
            pool.iota(numbers[:], [[1, s.max_groups]], base=0, channel_multiplier=0,
                      allow_small_or_imprecise_dtypes=True).then_inc(constants, 1)
            pool.iota(k.minus_node[:], [[0, 1]], base=0, channel_multiplier=-1,
                      allow_small_or_imprecise_dtypes=True).then_inc(constants, 1)
            pool.memset(k.dst_bf16[:], 0.0).then_inc(constants, 1)
            pool.memset(ones[:], 1.0).then_inc(constants, 1)
            pool.memset(k.zeros[:], 0.0).then_inc(constants, 1)
            pool.memset(k.ones_row[:], 1.0).then_inc(constants, 1)
            pool.memset(k.records[:], 0.0).then_inc(constants, 1)
            pool.memset(k.mean_weight[:], 0.0).then_inc(constants, 1)
            pool.memset(k.dst_in_tile[:], 0.0).then_inc(constants, 1)
            pool.memset(k.identity[:], 0.0).then_inc(drafts, 1)
            pool.memset(before[:], 1.0).then_inc(drafts, 1)
            pool.memset(pad[:], 0.0).then_inc(drafts, 1)
            pool.wait_ge(drafts, 3)
            pool.memset(pad[:, :, DST:DST + 1], float(2 * P * T)).then_inc(pad_ready, 1)
            pool.affine_select(out=k.identity[:], in_=k.identity[:], compare_op=ALU.not_equal, fill=1.0,
                               base=0, pattern=[[-1, P]], channel_multiplier=1).then_inc(constants, 1)
            pool.affine_select(out=before[:], in_=before[:], compare_op=ALU.is_gt, fill=0.0,
                               base=0, pattern=[[1, rows]], channel_multiplier=-1).then_inc(constants, 1)
            pool.wait_ge(order_known, 1)
            with pool.If(edges_unsorted(pool, k, s) > 0):
                pool.wait_ge(in_place, 16)
                with pool.Fori(0, turns):
                    for i in range(ring):
                        pool.wait_ge(slot_ready, 1)
                        pool.sem_inc(slot_ready, -1)
                        pool.indirect_dma_start(k.edge_records[0:s.edges, :],
                                                IndirectOffsetOnAxis(ap=ring_at[:, i:i + 1], axis=0),
                                                ring_record[:, i * WORDS:(i + 1) * WORDS], None
                                                ).then_inc(scattered[i], 16)

        @block.scalar
        def _(act):
            for i, (at, n) in enumerate(pieces):
                act.wait_ge(counted_ready, 1)
                act.sem_inc(counted_ready, -1)
                act.copy(place[:, 1 + at:1 + at + n], counted[:, i % 2, 0:n]).then_inc(act_done, 1)
                act.wait_ge(act_done, 1)
                act.sem_inc(act_done, -1)
                act.sem_inc(counted_taken, 1)
            act.sem_inc(columns_counted, 1)
            act.wait_ge(variance_ready, 1)
            act.activation(k.in_scale[:], k.in_scale[:], ACT.Sqrt).then_inc(root_ready, 1)
            act.wait_ge(turned_ready, 1)
            act.sem_inc(turned_ready, -1)
            for i in range(2):
                for b in range(KC):
                    act.copy(k.w_out[:, i * KC + b, :], turned[:, i, b * C:(b + 1) * C]).then_inc(act_done, 1)
            act.wait_ge(act_done, 2 * KC)
            act.sem_inc(act_done, -(2 * KC))
            act.wait_ge(order_known, 1)
            with act.If(edges_unsorted(act, k, s) > 0):
                act.wait_ge(positions_ready, 1)
                for i in range(ring):
                    act.copy(ring_at[:, i:i + 1], position[:, i:i + 1]).then_inc(act_done, 1)
                    act.copy(ring_record[:, i * WORDS:(i + 1) * WORDS],
                             made[:, i * WORDS:(i + 1) * WORDS]).then_inc(act_done, 1)
                    act.wait_ge(act_done, 2)
                    act.sem_inc(act_done, -2)
                    act.sem_inc(slot_ready, 1)
                with act.Fori(0, turns - 1) as n:
                    for i in range(ring):
                        act.wait_ge(scattered[i], n * 16 + 16)
                        act.copy(ring_at[:, i:i + 1], position[:, bass.ds(n * ring + (ring + i), 1)]).then_inc(act_done, 1)
                        act.copy(ring_record[:, i * WORDS:(i + 1) * WORDS],
                                 made[:, bass.ds(n * (ring * WORDS) + (ring + i) * WORDS, WORDS)]).then_inc(act_done, 1)
                        act.wait_ge(act_done, 2)
                        act.sem_inc(act_done, -2)
                        act.sem_inc(slot_ready, 1)
                for i in range(ring):
                    act.wait_ge(scattered[i], 16 * turns)

        @block.vector
        def _(dve):
            dve.memset(k.x[:, (T - 1) * C:T * C], 0.0).then_inc(x_cleared, 1)
            dve.memset(first[:, T:T + 1], float(s.edges)).then_inc(dve_done, 1)
            dve.wait_ge(dve_done, 1)
            dve.sem_inc(dve_done, -1)
            dve.memset(place[:, 0:1], 0.0).then_inc(dve_done, 1)
            dve.wait_ge(dve_done, 1)
            dve.sem_inc(dve_done, -1)
            dve.wait_ge(edges_in, 16 * 8)
            dve.tensor_scalar(position[:], dst[:], P.bit_length() - 1, None, ALU.arith_shift_right).then_inc(dve_done, 1)
            dve.wait_ge(dve_done, 1)
            dve.sem_inc(dve_done, -1)
            dve.tensor_copy(tile_f[:], position[:]).then_inc(dve_done, 1)
            dve.wait_ge(dve_done, 1)
            dve.sem_inc(dve_done, -1)
            dve.tensor_scalar(next_dst[:], next_dst[:], P.bit_length() - 1, None, ALU.arith_shift_right).then_inc(dve_done, 1)
            dve.wait_ge(dve_done, 1)
            dve.sem_inc(dve_done, -1)
            dve.tensor_copy(next_tile[:], next_dst[:]).then_inc(dve_done, 1)
            dve.wait_ge(dve_done, 1)
            dve.sem_inc(dve_done, -1)
            dve.tensor_tensor(next_tile[:], next_tile[:], tile_f[:], ALU.is_lt).then_inc(dve_done, 1)
            dve.wait_ge(dve_done, 1)
            dve.sem_inc(dve_done, -1)
            dve.tensor_reduce(breaks[:], next_tile[:], AX.X, ALU.max).then_inc(breaks_ready, 1)
            for t in range(T):
                dve.tensor_scalar(in_tile[:, t * cols:(t + 1) * cols], tile_f[:], float(t), None,
                                  ALU.is_equal).then_inc(tiles_known, 1)
            dve.tensor_copy(int_fields[:, :, SRC], src[:]).then_inc(dve_done, 1)
            dve.scalar_tensor_tensor(out=int_fields[:, :, SRC_TYPE], in0=src[:], scalar=float(R), in1=kind[:],
                                     op0=ALU.mult, op1=ALU.add).then_inc(dve_done, 1)
            for word, array in ((DST, dst), (TYPE, kind), (WEIGHT, weight), (WEIGHT1, weight1)):
                dve.tensor_copy(fields[:, :, word], array[:]).then_inc(dve_done, 1)
            dve.wait_ge(dve_done, WORDS)
            dve.sem_inc(dve_done, -WORDS)
            dve.sem_inc(records_made, 1)
            dve.wait_ge(x_in, 32)
            for t in range(T):
                dve.bn_stats(stats[:, t, :], k.x[:, t * C:(t + 1) * C]).then_inc(dve_done, 1)
            dve.wait_ge(dve_done, T)
            dve.sem_inc(dve_done, -T)
            for t in range(T):
                dve.bn_aggr(mean_var[:, t, :], stats[:, t, :]).then_inc(dve_done, 1)
            dve.wait_ge(dve_done, T)
            dve.sem_inc(dve_done, -T)
            dve.tensor_scalar(k.in_scale[:], mean_var[:, :, 1], EPS, None, ALU.add).then_inc(variance_ready, 1)
            dve.wait_ge(root_ready, 1)
            dve.reciprocal(k.in_scale[:], k.in_scale[:]).then_inc(dve_done, 1)
            dve.wait_ge(dve_done, 1)
            dve.sem_inc(dve_done, -1)
            dve.scalar_tensor_tensor(out=k.in_shift[:], in0=mean_var[:, :, 0], scalar=-1.0, in1=k.in_scale[:],
                                     op0=ALU.mult, op1=ALU.mult).then_inc(dve_done, 1)
            dve.wait_ge(dve_done, 1)
            dve.sem_inc(dve_done, -1)
            dve.wait_ge(columns_counted, 1)
            dve.sem_inc(columns_counted, -1)
            dve.tensor_tensor_scan(place[:, 1:wide + 1], place[:, 1:wide + 1], place[:, 1:wide + 1],
                                   0.0, ALU.add, ALU.max).then_inc(dve_done, 1)
            dve.wait_ge(dve_done, 1)
            dve.sem_inc(dve_done, -1)
            dve.tensor_copy(first[:, 0:T], place[:, 0:wide].rearrange("p (t c) -> p t c", c=cols)[:, :, 0]).then_inc(dve_done, 1)
            dve.wait_ge(dve_done, 1)
            dve.sem_inc(dve_done, -1)
            dve.tensor_tensor(number[:], first[:, 1:T + 1], first[:, 0:T], ALU.subtract).then_inc(dve_done, 1)
            dve.wait_ge(dve_done, 1)
            dve.sem_inc(dve_done, -1)
            dve.wait_ge(constants, n_constants)
            dve.tensor_tensor(beyond[:], number[:].unsqueeze(2).broadcast_to([P, T, s.more]),
                              multiples[:].unsqueeze(1).broadcast_to([P, T, s.more]), ALU.is_gt).then_inc(dve_done, 1)
            dve.wait_ge(dve_done, 1)
            dve.sem_inc(dve_done, -1)
            dve.tensor_reduce(groups[:], beyond[:], AX.X, ALU.add).then_inc(dve_done, 1)
            dve.wait_ge(dve_done, 1)
            dve.sem_inc(dve_done, -1)
            dve.tensor_scalar(groups[:], groups[:], 1.0, None, ALU.add).then_inc(dve_done, 1)
            dve.wait_ge(dve_done, 1)
            dve.sem_inc(dve_done, -1)
            dve.tensor_tensor_scan(group_end[:], groups[:], groups[:], 0.0, ALU.add, ALU.max).then_inc(dve_done, 1)
            dve.wait_ge(dve_done, 1)
            dve.sem_inc(dve_done, -1)
            plan = k.plan[:].rearrange("p (t w) -> p t w", w=4)
            dve.tensor_reduce(part_of[:], k.identity[0:PARTS, 0:PARTS].rearrange("p (q h) -> p h q", h=2 * HEADS)[:, 0:HEADS, :],
                              AX.X, ALU.add).then_inc(dve_done, 1)
            dve.wait_ge(dve_done, 1)
            dve.sem_inc(dve_done, -1)
            dve.tensor_copy(k.pick[:], part_of[:].unsqueeze(2).broadcast_to([PARTS, HEADS, P])).then_inc(dve_done, 1)
            dve.wait_ge(dve_done, 1)
            dve.sem_inc(dve_done, -1)
            dve.tensor_copy(k.identity_b[:], k.identity[:]).then_inc(dve_done, 1)
            dve.wait_ge(dve_done, 1)
            dve.sem_inc(dve_done, -1)
            dve.tensor_copy(plan[:, :, 1], group_end[0:1, :]).then_inc(dve_done, 1)
            dve.tensor_copy(plan[:, :, 3], group_end[0:1, :]).then_inc(dve_done, 1)
            dve.tensor_copy(plan[:, :, 2], first[0:1, 0:T]).then_inc(dve_done, 1)
            dve.tensor_tensor(plan[:, :, 0], group_end[0:1, :], groups[0:1, :], ALU.subtract).then_inc(dve_done, 1)
            dve.wait_ge(dve_done, 4)
            dve.sem_inc(dve_done, -4)
            G = s.max_groups
            by_group = lambda of_tiles: of_tiles.unsqueeze(1).broadcast_to([P, G, T])
            of_group = numbers[:].unsqueeze(2).broadcast_to([P, G, T])
            dve.tensor_tensor(behind[:], of_group, by_group(group_end[:]), ALU.is_ge).then_inc(dve_done, 1)
            dve.wait_ge(dve_done, 1)
            dve.sem_inc(dve_done, -1)
            dve.tensor_reduce(group_tile[:], behind[:], AX.X, ALU.add).then_inc(dve_done, 1)
            dve.wait_ge(dve_done, 1)
            dve.sem_inc(dve_done, -1)
            dve.tensor_scalar(k.group_base[:], group_tile[:], float(P), None, ALU.mult).then_inc(dve_done, 1)
            dve.wait_ge(dve_done, 1)
            dve.sem_inc(dve_done, -1)
            dve.tensor_tensor(lead[:], group_end[:], groups[:], ALU.subtract).then_inc(dve_done, 1)
            dve.wait_ge(dve_done, 1)
            dve.sem_inc(dve_done, -1)
            dve.scalar_tensor_tensor(out=lead[:], in0=lead[:], scalar=-float(s.group), in1=first[:, 0:T],
                                     op0=ALU.mult, op1=ALU.add).then_inc(dve_done, 1)
            dve.wait_ge(dve_done, 1)
            dve.sem_inc(dve_done, -1)
            dve.tensor_tensor(behind[:], by_group(k.tile_base[:]),
                              k.group_base[:].unsqueeze(2).broadcast_to([P, G, T]), ALU.is_equal).then_inc(dve_done, 1)
            dve.wait_ge(dve_done, 1)
            dve.sem_inc(dve_done, -1)
            dve.tensor_tensor(behind[:], behind[:], by_group(lead[:]), ALU.mult).then_inc(dve_done, 1)
            dve.wait_ge(dve_done, 1)
            dve.sem_inc(dve_done, -1)
            dve.tensor_reduce(group_lead[:], behind[:], AX.X, ALU.add).then_inc(dve_done, 1)
            dve.wait_ge(dve_done, 1)
            dve.sem_inc(dve_done, -1)
            dve.scalar_tensor_tensor(out=group_lead[:], in0=numbers[:], scalar=float(s.group),
                                     in1=group_lead[:], op0=ALU.mult, op1=ALU.add).then_inc(dve_done, 1)
            dve.wait_ge(dve_done, 1)
            dve.sem_inc(dve_done, -1)
            dve.tensor_scalar(group_lead[:], group_lead[:], float(s.edges), None, ALU.min).then_inc(dve_done, 1)
            dve.wait_ge(dve_done, 1)
            dve.sem_inc(dve_done, -1)
            dve.tensor_copy(k.group_plan[:], group_lead[0:1, :]).then_inc(dve_done, 1)
            dve.wait_ge(dve_done, 1)
            dve.sem_inc(dve_done, -1)
            dve.wait_ge(breaks_counted, 1)
            dve.tensor_copy(k.unsorted[:], all_breaks[0:1, :]).then_inc(dve_done, 1)
            dve.wait_ge(dve_done, 1)
            dve.sem_inc(dve_done, -1)
            dve.sem_inc(order_known, 1)
            with dve.If(edges_unsorted(dve, k, s) > 0):
                for i, (at, n) in enumerate(pieces):
                    dve.wait_ge(before_ready, 1)
                    dve.sem_inc(before_ready, -1)
                    dve.tensor_tensor(place[0:rows, at:at + n], counted[0:rows, i % 2, 0:n],
                                      place[0:rows, at:at + n], ALU.add).then_inc(dve_done, 1)
                    dve.wait_ge(dve_done, 1)
                    dve.sem_inc(dve_done, -1)
                    dve.sem_inc(before_taken, 1)
                dve.tensor_tensor(place[0:rows, 0:wide], place[0:rows, 0:wide], in_tile, ALU.mult).then_inc(dve_done, 1)
                dve.wait_ge(dve_done, 1)
                dve.sem_inc(dve_done, -1)
                dve.tensor_reduce(tile_f[:], place[0:rows, 0:wide].rearrange("p (t c) -> p c t", c=cols),
                                  AX.X, ALU.add).then_inc(dve_done, 1)
                dve.wait_ge(dve_done, 1)
                dve.sem_inc(dve_done, -1)
                dve.tensor_copy(position[:], tile_f[:]).then_inc(dve_done, 1)
                dve.wait_ge(dve_done, 1)
                dve.sem_inc(dve_done, -1)
                dve.sem_inc(positions_ready, 1)

        @block.tensor
        def _(pe):
            pe.wait_ge(constants, n_constants)
            pe.wait_ge(breaks_ready, 1)
            pe.matmul(all_breaks[:], ones[:], breaks[:], start=True, stop=True).then_inc(breaks_counted, 1)
            pe.wait_ge(tiles_known, T)
            for i, (at, n) in enumerate(pieces):
                if i >= 2:
                    pe.wait_ge(counted_taken, 1)
                    pe.sem_inc(counted_taken, -1)
                pe.matmul(counted[:, i % 2, 0:n], ones[:], in_tile[:, at:at + n],
                          start=True, stop=True).then_inc(counted_ready, 1)
            pe.wait_ge(weights_in, 16 * weight_loads)
            for i in range(2):
                for b in range(KC):
                    for n in range(KC):
                        mm = pe.transpose(turned[:, i, b * C + n * P:b * C + (n + 1) * P],
                                          w_raw[:, i * KC + n, b * P:(b + 1) * P], k.identity[:])
            mm.then_inc(turned_ready, 1)
            pe.wait_ge(counted_taken, 2)
            pe.sem_inc(counted_taken, -2)
            pe.wait_ge(order_known, 1)
            with pe.If(edges_unsorted(pe, k, s) > 0):
                for i, (at, n) in enumerate(pieces):
                    if i >= 2:
                        pe.wait_ge(before_taken, 1)
                        pe.sem_inc(before_taken, -1)
                    pe.matmul(counted[0:rows, i % 2, 0:n], before[:], in_tile[:, at:at + n],
                              start=True, stop=True).then_inc(before_ready, 1)
                pe.wait_ge(before_taken, 2)
                pe.sem_inc(before_taken, -2)



def tile_groups(engine, k, s, t):
    g0 = engine.value_load(k.plan[0:1, bass.ds(t * 4, 1)], min_val=0, max_val=s.max_groups - 1)
    g1 = engine.value_load(k.plan[0:1, bass.ds(t * 4 + 1, 1)], min_val=1, max_val=s.max_groups)
    return g0, g1


def all_groups(engine, k, s):
    at = 4 * (s.tiles - 1) + 1
    return engine.value_load(k.plan[0:1, at:at + 1], min_val=1, max_val=s.max_groups)


def count(nc, k, s):
    T, R, C = s.tiles, s.relations, s.width
    PARTS_OF_TABLE = 5
    assert T % PARTS_OF_TABLE == 0
    with ExitStack() as ctx:
        def sb(name, shape, dtype=F32):
            return ctx.enter_context(nc.sbuf_tensor(name, shape, dtype))

        to_node = sb("c_to_node", [P, SLOTS, P], BF16)
        of_type = sb("c_of_type", [P, SLOTS, R], BF16)
        lane = sb("c_lane", [P, P], BF16)
        degree = sb("c_degree", [P, T])
        count_rest = sb("c_count_rest", [P, T, R])
        root = sb("c_root", [P, T])
        row = sb("c_row", [P, C])
        turned = sb("c_turned", [P, KC, P])
        counted = ctx.enter_context(nc.psum_tensor("c_counted", [P, 512], F32))[:, 0:R]
        in_psum = ctx.enter_context(nc.psum_tensor("c_in_psum", [P, 512], F32))[:, 0:C]
        product = ctx.enter_context(nc.psum_tensor("c_product", [P, 512], F32))[:, 0:C]
        row_ready = k.sem("c_row_ready")
        transposed = k.sem("c_transposed")
        turned_ready = k.sem("c_turned_ready")
        product_ready = k.sem("c_product_ready")
        part_ready = k.sem("c_part_ready")
        part_stored = k.sem("c_part_stored")
        fetched = k.sem("c_fetched")
        records_in = k.sem("c_records_in")
        masks_ready = k.sem("c_masks_ready")
        masks_used = k.sem("c_masks_used")
        group_counted = k.sem("c_group_counted")
        counts_ready = k.sem("c_counts_ready")
        act_done = k.sem("c_act_done")
        tile_counted = k.sem("c_tile_counted")
        tile_taken = k.sem("c_tile_taken")
        degree_ready = k.sem("c_degree_ready")
        root_ready = k.sem("c_root_ready")
        done = k.sem("c_done")
        words = k.records[:].rearrange("p c w -> p (c w)")
        block = ctx.enter_context(nc.Block())

        @block.sync
        def _(sp):
            with sp.Fori(0, all_groups(sp, k, s)) as group:
                edge = sp.value_load(k.group_plan[0:1, bass.ds(group, 1)], min_val=0, max_val=s.edges)
                sp.dma_start(words[:, bass.ds(group * (SLOTS * WORDS), SLOTS * WORDS)],
                             k.edge_records[bass.ds(edge, s.group), :].rearrange(
                                 "(p c) w -> p (c w)", p=P)).then_inc(fetched, 16)
                sp.wait_ge(fetched, 16)
                sp.sem_inc(fetched, -16)
                sp.sem_inc(records_in, 1)
            n = T // PARTS_OF_TABLE
            for i in range(PARTS_OF_TABLE):
                sp.wait_ge(part_ready, i + 1)
                sp.dma_start(k.table[0][i * n * P:(i + 1) * n * P, :].rearrange("(t p) c -> p t c", p=P),
                             k.own[:, i * n * C:(i + 1) * n * C].rearrange("p (t c) -> p t c", c=C)
                             ).then_inc(part_stored, 16)
            sp.wait_ge(part_stored, 16 * PARTS_OF_TABLE)

        @block.vector
        def _(dve):
            dve.tensor_copy(lane[:], k.lane[:]).then_inc(done, 1)
            dve.wait_ge(done, 1)
            dve.sem_inc(done, -1)
            with dve.Fori(0, all_groups(dve, k, s)) as g:
                its = bass.ds(g * SLOTS, SLOTS)
                dve.wait_ge(records_in, 1)
                dve.sem_inc(records_in, -1)
                dve.tensor_scalar(k.dst_in_tile[:, its], k.records[:, its, DST], k.group_base[:, bass.ds(g, 1)], None,
                                  ALU.subtract).then_inc(done, 1)
                dve.wait_ge(group_counted, 1)
                dve.sem_inc(group_counted, -1)
                dve.tensor_tensor(of_type[:], k.relation[:, 0:1, :].broadcast_to([P, SLOTS, R]),
                                  k.records[:, its, TYPE:TYPE + 1].broadcast_to([P, SLOTS, R]),
                                  ALU.is_equal).then_inc(done, 1)
                dve.wait_ge(done, 2)
                dve.sem_inc(done, -2)
                dve.tensor_copy(k.dst_bf16[:, its], k.dst_in_tile[:, its]).then_inc(done, 1)
                for i in range(TRIOS):
                    dve.wait_ge(masks_used, 1)
                    dve.sem_inc(masks_used, -1)
                    for j in range(i * TRIO, (i + 1) * TRIO):
                        mask = dve.tensor_scalar(to_node[:, j, :], lane[:], k.dst_in_tile[:, bass.ds(g * SLOTS + j, 1)],
                                                 None, ALU.is_equal)
                    mask.then_inc(masks_ready, 1)
                dve.wait_ge(done, 1)
                dve.sem_inc(done, -1)
            dve.wait_ge(counts_ready, 1)
            dve.tensor_scalar(k.one_over_count[:], k.counts[:], 1.0, None, ALU.max).then_inc(done, 1)
            dve.wait_ge(done, 1)
            dve.sem_inc(done, -1)
            dve.reciprocal(k.one_over_count[:], k.one_over_count[:]).then_inc(done, 1)
            dve.tensor_reduce(degree[:], k.counts[:].rearrange("p (t r) -> p t r", r=R), AX.X, ALU.add).then_inc(done, 1)
            dve.wait_ge(done, 2)
            dve.sem_inc(done, -2)
            dve.tensor_scalar(degree[:], degree[:], 1.0, None, ALU.add).then_inc(degree_ready, 1)
            dve.wait_ge(root_ready, 1)
            dve.reciprocal(k.dinv[:], root[:]).then_inc(done, 1)
            dve.wait_ge(done, 1)
            dve.sem_inc(done, -1)
            n = T // PARTS_OF_TABLE
            for i in range(PARTS_OF_TABLE):
                own = k.own[:, i * n * C:(i + 1) * n * C].rearrange("p (t c) -> p t c", c=C)
                dve.tensor_tensor(own, own, k.dinv[:, i * n:(i + 1) * n].unsqueeze(2).broadcast_to([P, n, C]),
                                  ALU.mult).then_inc(part_ready, 1)
            value = k.one_over_count[:].rearrange("p (t r) -> p t r", r=R)
            for i in range(3):
                dve.tensor_copy(k.count_parts[:, :, i, :], value).then_inc(done, 1)
                dve.wait_ge(done, 1)
                dve.sem_inc(done, -1)
                if i < 2:
                    dve.tensor_tensor(count_rest[:], value, k.count_parts[:, :, i, :], ALU.subtract).then_inc(done, 1)
                    dve.wait_ge(done, 1)
                    dve.sem_inc(done, -1)
                    value = count_rest[:]

        @block.scalar
        def _(act):
            def norm(t):
                act.activation(row[:], k.x[:, bass.ds(t * C, C)], ACT.Relu, scale=k.in_scale[:, bass.ds(t, 1)],
                               bias=k.in_shift[:, bass.ds(t, 1)]).then_inc(row_ready, 1)

            def finish(t):
                act.wait_ge(product_ready, 1)
                act.sem_inc(product_ready, -1)
                act.copy(k.own[:, bass.ds(t * C, C)], product).then_inc(act_done, 1)
                act.wait_ge(act_done, 1)
                act.sem_inc(act_done, -1)
                act.wait_ge(tile_counted, 1)
                act.sem_inc(tile_counted, -1)
                act.copy(k.counts[:, bass.ds(t * R, R)], counted).then_inc(act_done, 1)
                act.wait_ge(act_done, 1)
                act.sem_inc(act_done, -1)
                act.sem_inc(tile_taken, 1)

            def turn():
                act.wait_ge(transposed, 1)
                act.sem_inc(transposed, -1)
                act.copy(turned[:].rearrange("p k n -> p (k n)"), in_psum).then_inc(turned_ready, 1)

            norm(0)
            turn()
            with act.Fori(0, T - 1) as t:
                norm(t + 1)
                finish(t)
                turn()
            finish(T - 1)
            act.sem_inc(counts_ready, 1)
            act.wait_ge(degree_ready, 1)
            act.activation(root[:], degree[:], ACT.Sqrt).then_inc(root_ready, 1)

        @block.tensor
        def _(pe):
            pe.sem_inc(masks_used, TRIOS)
            pe.sem_inc(group_counted, 1)
            pe.sem_inc(tile_taken, 1)

            def transposes():
                pe.wait_ge(row_ready, 1)
                pe.sem_inc(row_ready, -1)
                for b in range(KC):
                    mm = pe.transpose(in_psum[:, b * P:(b + 1) * P], row[:, b * P:(b + 1) * P], k.identity[:])
                mm.then_inc(transposed, 1)

            def tile(t):
                g0, g1 = tile_groups(pe, k, s, t)
                pe.wait_ge(tile_taken, 1)
                pe.sem_inc(tile_taken, -1)
                pe.wait_ge(turned_ready, 1)
                pe.sem_inc(turned_ready, -1)
                for b in range(KC):
                    mm = pe.matmul(product, turned[:, b, :], k.w_gcn[:, b, :], start=(b == 0), stop=(b == KC - 1))
                mm.then_inc(product_ready, 1)
                pe.matmul(counted, k.zeros[:, 0:P], k.zeros[:, 0:R], start=True, stop=False)
                with pe.Fori(g0, g1):
                    for i in range(TRIOS):
                        pe.wait_ge(masks_ready, 1)
                        pe.sem_inc(masks_ready, -1)
                        for j in range(i * TRIO, (i + 1) * TRIO):
                            mm = pe.matmul(counted, to_node[:, j, :], of_type[:, j, :], start=False, stop=False)
                        mm.then_inc(masks_used, 1)
                    pe.matmul(counted, k.zeros[:, 0:P], k.zeros[:, 0:R], start=False, stop=False).then_inc(group_counted, 1)
                pe.matmul(counted, k.zeros[:, 0:P], k.zeros[:, 0:R], start=False, stop=True).then_inc(tile_counted, 1)

            transposes()
            with pe.Fori(0, T - 1) as t:
                tile(t)
                transposes()
            tile(T - 1)


class Dense:

    def __init__(self, nc, ctx, k, s):
        def sb(n, shape, dtype=F32):
            return ctx.enter_context(nc.sbuf_tensor(f"dense_{n}", shape, dtype))

        self.row = sb("row", [P, s.width])
        self.stats = sb("stats", [P, 6])
        self.mean_var = sb("mean_var", [P, 2])
        self.deviation = sb("deviation", [P, 1])
        self.turned = sb("turned", [P, KC, P])
        self.row_ready = k.sem("row_ready")
        self.row_used = k.sem("row_used")
        self.var_ready = k.sem("var_ready")
        self.deviation_ready = k.sem("deviation_ready")
        self.transposed = k.sem("transposed")
        self.turned_ready = k.sem("turned_ready")
        self.product_ready = k.sem("product_ready")
        self.product_taken = k.sem("product_taken")
        self.kept = k.sem("kept")
        self.stored = k.sem("stored")
        self.done = k.sem("done")
        self.act_done = k.sem("act_done")
        self.acc_ready = k.sem("acc_ready")
        self.acc_taken = k.sem("acc_taken")
        self.slot_used = k.sem("slot_used")
        self.mask_ready = k.sem("mask_ready")
        self.index_ready = k.sem("index_ready")
        bank = ctx.enter_context(nc.psum_tensor("dense", [P, 2, s.width], F32))
        self.in_psum, self.product = bank[:, 0, :], bank[:, 1, :]


def normalize_start(dve, k, s, d, t):
    x = k.x[:, bass.ds(t * s.width, s.width)]
    dve.bn_stats(d.stats[:], x).then_inc(d.done, 1)
    dve.wait_ge(d.done, 1)
    dve.sem_inc(d.done, -1)
    dve.bn_aggr(d.mean_var[:], d.stats[:]).then_inc(d.done, 1)
    dve.wait_ge(d.done, 1)
    dve.sem_inc(d.done, -1)
    dve.tensor_scalar(d.deviation[:], d.mean_var[:, 1:2], EPS, None, ALU.add).then_inc(d.done, 1)
    dve.wait_ge(d.done, 1)
    dve.sem_inc(d.done, -1)
    dve.sem_inc(d.var_ready, 1)


def normalize_finish(dve, k, s, d, t):
    x = k.x[:, bass.ds(t * s.width, s.width)]
    dve.wait_ge(d.deviation_ready, 1)
    dve.sem_inc(d.deviation_ready, -1)
    dve.reciprocal(d.deviation[:], d.deviation[:]).then_inc(d.done, 1)
    dve.wait_ge(d.done, 1)
    dve.sem_inc(d.done, -1)
    dve.tensor_scalar(d.row[:], x, d.mean_var[:, 0:1], d.deviation[:], ALU.subtract, ALU.mult).then_inc(d.row_ready, 1)


def normalize(dve, k, s, d, t):
    normalize_start(dve, k, s, d, t)
    normalize_finish(dve, k, s, d, t)


def square_root(act, d):
    act.wait_ge(d.var_ready, 1)
    act.sem_inc(d.var_ready, -1)
    act.activation(d.deviation[:], d.deviation[:], ACT.Sqrt).then_inc(d.deviation_ready, 1)


def transposed_row(pe, k, d):
    pe.wait_ge(d.row_ready, 1)
    pe.sem_inc(d.row_ready, -1)
    pe.wait_ge(d.product_taken, 1)
    pe.sem_inc(d.product_taken, -1)
    for b in range(KC):
        mm = pe.transpose(d.in_psum[:, b * P:(b + 1) * P], d.row[:, b * P:(b + 1) * P], k.identity[:])
    mm.then_inc(d.transposed, 1)


def relu_turned(act, d):
    act.wait_ge(d.transposed, 1)
    act.sem_inc(d.transposed, -1)
    act.activation(d.turned[:].rearrange("p k n -> p (k n)"), d.in_psum, ACT.Relu).then_inc(d.act_done, 1)
    act.wait_ge(d.act_done, 1)
    act.sem_inc(d.act_done, -1)
    act.sem_inc(d.turned_ready, 1)
    act.sem_inc(d.row_used, 1)


def product(pe, k, s, d, weights, bias):
    pe.wait_ge(d.turned_ready, 1)
    pe.sem_inc(d.turned_ready, -1)
    for b in range(KC):
        mm = pe.matmul(d.product, d.turned[:, b, :], weights[:, b, :],
                       start=(b == 0), stop=(b == KC - 1 and bias is None))
    if bias is not None:
        mm = pe.matmul(d.product, k.ones_row[:], bias, start=False, stop=True)
    mm.then_inc(d.product_ready, 1)


def begin_dense(nc, k):
    d = k.dense
    with ExitStack() as ctx:
        block = ctx.enter_context(nc.Block())

        @block.vector
        def _(dve):
            dve.sem_inc(d.row_used, 1)
            dve.sem_inc(d.acc_taken, 1)
            dve.sem_inc(d.product_taken, 1)


class ToTable:

    def __init__(self, k, s, layer, source):
        self.k, self.s, self.layer = k, s, layer
        self.gcn = source == "gcn"
        self.weights = k.w_gcn[:, (layer + 1) * KC:(layer + 2) * KC, :] if self.gcn else k.w_out[:, KC:2 * KC, :]
        self.bias = None if self.gcn else k.bias_out[:, 1, :]
        self.table = k.table[(layer + 1) % 2]
        self.roots = False
        self.late = False
        self.dense = True

    def open(self, nc, ctx, d):
        self.d = d

    def dve(self, dve, t, acc):
        k, s, d = self.k, self.s, self.d
        dve.wait_ge(d.row_used, 1)
        dve.sem_inc(d.row_used, -1)
        layer_sum(dve, k, s, d, t, acc, k.bias_gcn[:, self.layer, :] if self.gcn else None)
        dve.sem_inc(d.row_ready, 1)

    def pe(self, pe):
        transposed_row(pe, self.k, self.d)
        product(pe, self.k, self.s, self.d, self.weights, self.bias)

    def act(self, act, t):
        k, s, d = self.k, self.s, self.d
        act.wait_ge(d.product_ready, 1)
        act.sem_inc(d.product_ready, -1)
        act.activation(k.own[:, bass.ds(t * s.width, s.width)], d.product, ACT.Copy,
                       scale=k.dinv[:, bass.ds(t, 1)]).then_inc(d.act_done, 1)
        act.wait_ge(d.act_done, 1)
        act.sem_inc(d.act_done, -1)
        act.sem_inc(d.product_taken, 1)
        act.sem_inc(d.kept, 1)

    def sp(self, sp, t):
        k, s, d = self.k, self.s, self.d
        sp.wait_ge(d.kept, 1)
        sp.sem_inc(d.kept, -1)
        sp.dma_start(self.table[bass.ds(t * P, P), :], k.own[:, bass.ds(t * s.width, s.width)]).then_inc(d.stored, 16)
        sp.wait_ge(d.stored, 16)
        sp.sem_inc(d.stored, -16)


def layer_sum(dve, k, s, d, t, acc, bias):
    dve.tensor_tensor(d.row[:], acc[:, 0:s.width], k.own[:, bass.ds(t * s.width, s.width)], ALU.add).then_inc(d.done, 1)
    dve.wait_ge(d.done, 1)
    dve.sem_inc(d.done, -1)
    dve.sem_inc(d.acc_taken, 1)
    if bias is None:
        dve.tensor_scalar(d.row[:], d.row[:], k.dinv[:, bass.ds(t, 1)], None, ALU.mult).then_inc(d.done, 1)
        dve.wait_ge(d.done, 1)
        dve.sem_inc(d.done, -1)
    else:
        dve.scalar_tensor_tensor(out=d.row[:], in0=d.row[:], scalar=k.dinv[:, bass.ds(t, 1)], in1=bias,
                                 op0=ALU.mult, op1=ALU.add).then_inc(d.done, 1)
        dve.wait_ge(d.done, 1)
        dve.sem_inc(d.done, -1)


def add_relu_row(dve, k, s, d, t):
    x = k.x[:, bass.ds(t * s.width, s.width)]
    dve.scalar_tensor_tensor(out=x, in0=d.row[:], scalar=0.0, in1=x, op0=ALU.max, op1=ALU.add).then_inc(d.done, 1)
    dve.wait_ge(d.done, 1)
    dve.sem_inc(d.done, -1)


class ToRelations:

    def __init__(self, k, s):
        self.k, self.s = k, s
        self.roots = True
        self.late = False
        self.dense = True

    def open(self, nc, ctx, d):
        self.d = d
        self.staged = ctx.enter_context(nc.sbuf_tensor("relations_staged", [P, self.s.relations * self.s.width], F32))
        self.pair = ctx.enter_context(nc.psum_tensor("relations_pair", [P, 2, 512], F32))
        self.pair_ready = self.k.sem("relations_pair_ready")
        self.pair_taken = self.k.sem("relations_pair_taken")
        self.staged_free = self.k.sem("relations_staged_free")

    def dve(self, dve, t, acc):
        k, s, d = self.k, self.s, self.d
        dve.wait_ge(d.row_used, 1)
        dve.sem_inc(d.row_used, -1)
        layer_sum(dve, k, s, d, t, acc, k.bias_gcn[:, 2, :])
        add_relu_row(dve, k, s, d, t)
        normalize(dve, k, s, d, t)

    def pe(self, pe):
        k, s, d = self.k, self.s, self.d
        transposed_row(pe, k, d)
        product(pe, k, s, d, k.w_root[:], k.bias_root[:])
        by_half = k.w_relation[:].rearrange("p (r k) c -> p k r c", k=KC)
        for i in range(s.relations // 2):
            pe.wait_ge(self.pair_taken, 1)
            pe.sem_inc(self.pair_taken, -1)
            for b in range(KC):
                mm = pe.matmul(self.pair[:, i % 2, :], d.turned[:, b, :], by_half[:, b, 2 * i:2 * i + 2, :],
                               start=(b == 0), stop=(b == KC - 1))
            mm.then_inc(self.pair_ready, 1)

    def act(self, act, t):
        k, s, d = self.k, self.s, self.d
        act.wait_ge(d.product_ready, 1)
        act.sem_inc(d.product_ready, -1)
        act.copy(k.own[:, bass.ds(t * s.width, s.width)], d.product).then_inc(d.act_done, 1)
        act.wait_ge(d.act_done, 1)
        act.sem_inc(d.act_done, -1)
        act.sem_inc(d.product_taken, 1)
        act.wait_ge(self.staged_free, 1)
        act.sem_inc(self.staged_free, -1)
        for i in range(s.relations // 2):
            act.wait_ge(self.pair_ready, 1)
            act.sem_inc(self.pair_ready, -1)
            act.copy(self.staged[:, i * 512:(i + 1) * 512], self.pair[:, i % 2, :]).then_inc(d.act_done, 1)
            act.wait_ge(d.act_done, 1)
            act.sem_inc(d.act_done, -1)
            act.sem_inc(self.pair_taken, 1)
        act.sem_inc(d.kept, 1)

    def sp(self, sp, t):
        k, s, d = self.k, self.s, self.d
        sp.wait_ge(d.kept, 1)
        sp.sem_inc(d.kept, -1)
        sp.dma_start(k.relation_table[bass.ds(t * (P * s.relations), P * s.relations), :].rearrange(
            "(p r) c -> p (r c)", r=s.relations), self.staged[:]).then_inc(d.stored, 16)
        sp.wait_ge(d.stored, 16)
        sp.sem_inc(d.stored, -16)
        sp.sem_inc(self.staged_free, 1)


class ToAttention:

    def __init__(self, k, s):
        self.k, self.s = k, s
        self.roots = True
        self.late = True
        self.dense = True

    def open(self, nc, ctx, d):
        self.d = d
        self.weighed = ctx.enter_context(nc.sbuf_tensor("attention_weighed", [P, 2, self.s.width], F32))
        self.rest = ctx.enter_context(nc.sbuf_tensor("attention_rest", [P, 2 * HEADS], F32))
        self.h_ready = self.k.sem("attention_h_ready")

    def dve(self, dve, t, acc):
        k, s, d = self.k, self.s, self.d
        x = k.x[:, bass.ds(t * s.width, s.width)]
        dve.tensor_tensor(x, x, acc[:, 0:s.width], ALU.add).then_inc(d.done, 1)
        dve.wait_ge(d.done, 1)
        dve.sem_inc(d.done, -1)
        dve.sem_inc(d.acc_taken, 1)
        dve.tensor_tensor(x, x, k.own[:, bass.ds(t * s.width, s.width)], ALU.add).then_inc(d.done, 1)
        dve.wait_ge(d.done, 1)
        dve.sem_inc(d.done, -1)
        dve.wait_ge(d.row_used, 1)
        dve.sem_inc(d.row_used, -1)
        normalize(dve, k, s, d, t)

    def dve_late(self, dve, t):
        k, s, d = self.k, self.s, self.d
        dve.wait_ge(self.h_ready, 1)
        dve.sem_inc(self.h_ready, -1)
        h = k.own[:, bass.ds(t * s.width, s.width)].unsqueeze(1).broadcast_to([P, 2, s.width])
        dve.tensor_tensor(self.weighed[:], h, k.att[:], ALU.mult).then_inc(d.done, 1)
        dve.wait_ge(d.done, 1)
        dve.sem_inc(d.done, -1)
        source = k.attention[:, bass.ds(t * 3 * HEADS, HEADS)]
        target = k.attention[:, bass.ds(t * 3 * HEADS + HEADS, HEADS)]
        loop = k.attention[:, bass.ds(t * 3 * HEADS + 2 * HEADS, HEADS)]
        dve.tensor_reduce(k.attention[:, bass.ds(t * 3 * HEADS, 2 * HEADS)],
                          self.weighed[:].rearrange("p a (h c) -> p (a h) c", h=HEADS), AX.X, ALU.add).then_inc(d.done, 1)
        dve.wait_ge(d.done, 1)
        dve.sem_inc(d.done, -1)
        dve.tensor_tensor(self.rest[:, 0:HEADS], source, target, ALU.add).then_inc(d.done, 1)
        dve.wait_ge(d.done, 1)
        dve.sem_inc(d.done, -1)
        dve.scalar_tensor_tensor(out=loop, in0=self.rest[:, 0:HEADS], scalar=SLOPE, in1=self.rest[:, 0:HEADS], op0=ALU.mult,
                                 op1=ALU.max).then_inc(d.done, 1)
        dve.wait_ge(d.done, 1)
        dve.sem_inc(d.done, -1)
        parts = k.parts[:].bitcast(BF16)
        value = k.attention[:, bass.ds(t * 3 * HEADS, 2 * HEADS)]
        for i in range(3):
            part = parts[:, bass.ds(t * PARTS + i * 2 * HEADS, 2 * HEADS)]
            dve.tensor_copy(part, value).then_inc(d.done, 1)
            dve.wait_ge(d.done, 1)
            dve.sem_inc(d.done, -1)
            if i < 2:
                dve.tensor_tensor(self.rest[:], value, part, ALU.subtract).then_inc(d.done, 1)
                dve.wait_ge(d.done, 1)
                dve.sem_inc(d.done, -1)
                value = self.rest[:]
        dve.sem_inc(d.kept, 1)

    def pe(self, pe):
        transposed_row(pe, self.k, self.d)
        product(pe, self.k, self.s, self.d, self.k.w_gat[:], None)

    def act(self, act, t):
        k, s, d = self.k, self.s, self.d
        act.wait_ge(d.product_ready, 1)
        act.sem_inc(d.product_ready, -1)
        act.copy(k.own[:, bass.ds(t * s.width, s.width)], d.product).then_inc(d.act_done, 1)
        act.wait_ge(d.act_done, 1)
        act.sem_inc(d.act_done, -1)
        act.sem_inc(d.product_taken, 1)
        act.sem_inc(self.h_ready, 1)

    def sp(self, sp, t):
        k, s, d = self.k, self.s, self.d
        sp.wait_ge(d.kept, 1)
        sp.sem_inc(d.kept, -1)
        rows = k.gat_table[bass.ds(t * P, P), :]
        sp.dma_start(rows[:, 0:s.width], k.own[:, bass.ds(t * s.width, s.width)]).then_inc(d.stored, 16)
        sp.dma_start(rows[:, s.width:s.width + HEADS],
                     k.attention[:, bass.ds(t * 3 * HEADS, HEADS)]).then_inc(d.stored, 16)
        sp.dma_start(rows[:, s.width + HEADS:], k.parts[:, bass.ds(t * PART_WORDS, PART_WORDS)]).then_inc(d.stored, 16)
        sp.wait_ge(d.stored, 48)
        sp.sem_inc(d.stored, -48)


class ToOutput:

    def __init__(self, k, s, out):
        self.k, self.s, self.out = k, s, out
        self.roots = False
        self.late = False
        self.dense = False

    def open(self, nc, ctx, d):
        self.d = d

    def dve(self, dve, t, acc):
        k, s, d = self.k, self.s, self.d
        layer_sum(dve, k, s, d, t, acc, None)
        add_relu_row(dve, k, s, d, t)
        dve.sem_inc(d.kept, 1)

    def sp(self, sp, t):
        k, s, d = self.k, self.s, self.d
        sp.wait_ge(d.kept, 1)
        sp.sem_inc(d.kept, -1)
        sp.dma_start(self.out[bass.ds(t * P, P), :], k.x[:, bass.ds(t * s.width, s.width)]).then_inc(d.stored, 16)
        sp.wait_ge(d.stored, 16)
        sp.sem_inc(d.stored, -16)

    def sp_last(self, sp):
        k, s, d = self.k, self.s, self.d
        t = s.tiles - 1
        sp.wait_ge(d.kept, 1)
        sp.dma_start(self.out[t * P:s.nodes, :], k.x[0:s.last, t * s.width:(t + 1) * s.width]).then_inc(d.stored, 16)
        sp.wait_ge(d.stored, 16)


def project(nc, k, s, name, weights, bias):
    T, C = s.tiles, s.width
    assert T % 2 == 1
    with ExitStack() as ctx:
        def sb(n, shape, dtype=F32):
            return ctx.enter_context(nc.sbuf_tensor(f"{name}_{n}", shape, dtype))

        def psum(n):
            return ctx.enter_context(nc.psum_tensor(f"{name}_{n}", [P, 2, 512], F32))[:, :, 0:C]

        d = k.dense
        stats = sb("stats", [P, T, 6])
        mean_var = sb("mean_var", [P, T, 2])
        deviation = sb("deviation", [P, T])
        rows = sb("rows", [P, 2, C])
        turned = sb("turned", [P, 2, C])
        in_psum = psum("in_psum")
        products = psum("products")
        mark = ctx.enter_context(nc.psum_tensor(f"{name}_mark", [P, 512], F32))[0:1, 0:1]
        row_free = k.sem(f"{name}_row_free")
        row_ready = k.sem(f"{name}_row_ready")
        transposed = k.sem(f"{name}_transposed")
        turned_free = k.sem(f"{name}_turned_free")
        turned_ready = k.sem(f"{name}_turned_ready")
        product_free = k.sem(f"{name}_product_free")
        product_ready = k.sem(f"{name}_product_ready")
        block = ctx.enter_context(nc.Block())

        @block.sync
        def _(sp):
            with sp.Fori(0, T) as t:
                sp.wait_ge(d.kept, 1)
                sp.sem_inc(d.kept, -1)
                sp.dma_start(k.table[0][bass.ds(t * P, P), :], k.own[:, bass.ds(t * C, C)]).then_inc(d.stored, 16)
            sp.wait_ge(d.stored, 16 * T)
            sp.sem_inc(d.stored, -(16 * T))

        @block.vector
        def _(dve):
            def row(t, b):
                dve.wait_ge(row_free, 1)
                dve.sem_inc(row_free, -1)
                dve.tensor_scalar(rows[:, b, :], k.x[:, bass.ds(t * C, C)],
                                  mean_var[:].rearrange("p t m -> p (t m)")[:, bass.ds(t * 2, 1)],
                                  deviation[:, bass.ds(t, 1)], ALU.subtract, ALU.mult).then_inc(row_ready, 1)

            def keep(t, b):
                own = k.own[:, bass.ds(t * C, C)]
                dve.wait_ge(product_ready, 1)
                dve.sem_inc(product_ready, -1)
                dve.tensor_tensor(own, products[:, b, :], bias, ALU.add).then_inc(d.done, 1)
                dve.wait_ge(d.done, 1)
                dve.sem_inc(d.done, -1)
                dve.sem_inc(product_free, 1)
                dve.tensor_scalar(own, own, k.dinv[:, bass.ds(t, 1)], None, ALU.mult).then_inc(d.done, 1)
                dve.wait_ge(d.done, 1)
                dve.sem_inc(d.done, -1)
                dve.sem_inc(d.kept, 1)

            for t in range(T):
                dve.bn_stats(stats[:, t, :], k.x[:, t * C:(t + 1) * C]).then_inc(d.done, 1)
            dve.wait_ge(d.done, T)
            dve.sem_inc(d.done, -T)
            for t in range(T):
                dve.bn_aggr(mean_var[:, t, :], stats[:, t, :]).then_inc(d.done, 1)
            dve.wait_ge(d.done, T)
            dve.sem_inc(d.done, -T)
            dve.tensor_scalar(deviation[:], mean_var[:, :, 1], EPS, None, ALU.add).then_inc(d.done, 1)
            dve.wait_ge(d.done, 1)
            dve.sem_inc(d.done, -1)
            dve.sem_inc(d.var_ready, 1)
            dve.wait_ge(d.deviation_ready, 1)
            dve.sem_inc(d.deviation_ready, -1)
            dve.reciprocal(deviation[:], deviation[:]).then_inc(d.done, 1)
            dve.wait_ge(d.done, 1)
            dve.sem_inc(d.done, -1)
            dve.sem_inc(row_free, 2)
            row(0, 0)
            row(1, 1)
            with dve.Fori(0, T // 2 - 1) as n:
                row(2 * n + 2, 0)
                keep(2 * n, 0)
                row(2 * n + 3, 1)
                keep(2 * n + 1, 1)
            row(T - 1, 0)
            keep(T - 3, 0)
            keep(T - 2, 1)
            keep(T - 1, 0)

        @block.scalar
        def _(act):
            def relu(b):
                act.wait_ge(transposed, 1)
                act.sem_inc(transposed, -1)
                act.sem_inc(row_free, 1)
                act.wait_ge(turned_free, 1)
                act.sem_inc(turned_free, -1)
                act.activation(turned[:, b, :], in_psum[:, b, :], ACT.Relu).then_inc(turned_ready, 1)

            act.wait_ge(d.var_ready, 1)
            act.sem_inc(d.var_ready, -1)
            act.activation(deviation[:], deviation[:], ACT.Sqrt).then_inc(d.deviation_ready, 1)
            with act.Fori(0, T // 2):
                relu(0)
                relu(1)
            relu(0)

        @block.tensor
        def _(pe):
            def transposes(b):
                pe.wait_ge(row_ready, 1)
                pe.sem_inc(row_ready, -1)
                for i in range(KC):
                    mm = pe.transpose(in_psum[:, b, i * P:(i + 1) * P], rows[:, b, i * P:(i + 1) * P], k.identity[:])
                mm.then_inc(transposed, 1)

            def layer(b):
                pe.wait_ge(turned_ready, 1)
                pe.sem_inc(turned_ready, -1)
                pe.wait_ge(product_free, 1)
                pe.sem_inc(product_free, -1)
                for i in range(KC):
                    mm = pe.matmul(products[:, b, :], turned[:, b, i * P:(i + 1) * P], weights[:, i, :],
                                   start=(i == 0), stop=(i == KC - 1))
                mm.then_inc(product_ready, 1)
                pe.matmul(mark, k.zeros[:, 0:1], k.zeros[:, 0:1], start=True, stop=True).then_inc(turned_free, 1)

            pe.sem_inc(product_free, 2)
            pe.sem_inc(turned_free, 2)
            transposes(0)
            with pe.Fori(0, T // 2):
                transposes(1)
                layer(0)
                transposes(0)
                layer(1)
            layer(0)


def landings(groups, passes, g, further=0):
    return (groups * passes + g) * 16 + (16 + further * 16) if passes else g * 16 + 16


def aggregate(nc, k, s, name, table, to, index, weights, find_means=False):
    C, T, R = s.width, s.tiles, s.relations
    with ExitStack() as ctx:
        def sb(n, shape, dtype=F32):
            return ctx.enter_context(nc.sbuf_tensor(f"{name}_{n}", shape, dtype))

        def psum(n, shape, dtype=F32):
            return ctx.enter_context(nc.psum_tensor(f"{name}_{n}", shape, dtype))

        gathered = sb("gathered", [P, SLOTS, C])
        to_node = sb("to_node", [P, SLOTS, P])
        indices = sb("indices", [P, SLOTS], I32)
        acc = psum("acc", [P, C])
        d = k.dense
        landed, passes, further = k.landed, k.passes, k.further
        k.passes += 1
        to.open(nc, ctx, d)
        if find_means:
            from_node = sb("from_node", [P, TRIO, P], BF16)
            apart = sb("apart", [P, TRIO, P])
            of_type = sb("of_type", [P, SLOTS, R])
            typed = sb("typed", [P, SLOTS, 3, R])
            mark = sb("mark", [P, 1])
            turned = psum("turned", [P, TRIO, P])
            found_banks = psum("found", [P, 2, 512])
            found = found_banks[:, :, 0:TRIO * 3 * R].rearrange("p b (c q r) -> p b c q r", q=3, r=R)
            turned_ready = k.sem(f"{name}_turned_ready")
            from_ready = k.sem(f"{name}_from_ready")
            found_ready = k.sem(f"{name}_found_ready")
            found_taken = k.sem(f"{name}_found_taken")
        source = k.records[:].bitcast(I32)
        block = ctx.enter_context(nc.Block())

        @block.gpsimd
        def _(pool):
            with pool.Fori(0, all_groups(pool, k, s)):
                for i in range(SLOTS):
                    if i % TRIO == 0:
                        pool.wait_ge(d.index_ready, 1)
                        pool.sem_inc(d.index_ready, -1)
                    pool.indirect_dma_start(gathered[:, i, :], None, table,
                                            IndirectOffsetOnAxis(ap=indices[:, i:i + 1], axis=0)).then_inc(landed[i], 16)
            pool.wait_ge(d.index_ready, TRIOS)
            pool.sem_inc(d.index_ready, -TRIOS)

        @block.vector
        def _(dve):
            def types(g):
                its = bass.ds(g * SLOTS, SLOTS)
                dve.tensor_tensor(of_type[:], k.relation[:, 0:1, :].broadcast_to([P, SLOTS, R]),
                                  k.records[:, its, TYPE:TYPE + 1].broadcast_to([P, SLOTS, R]),
                                  ALU.is_equal).then_inc(d.done, 1)
                dve.wait_ge(d.done, 1)
                dve.sem_inc(d.done, -1)

            def find_trio(i):
                its = slice(i * TRIO, (i + 1) * TRIO)
                dve.wait_ge(found_ready, 1)
                dve.sem_inc(found_ready, -1)
                dve.tensor_tensor(typed[:, its], of_type[:, its, :].unsqueeze(2).broadcast_to([P, TRIO, 3, R]),
                                  found[:, i % 2], ALU.mult).then_inc(found_taken, 1)

            def means(g):
                its = bass.ds(g * SLOTS, SLOTS)
                dve.memset(mark[:], 0.0).then_inc(d.done, 1)
                dve.wait_ge(d.done, 1)
                dve.sem_inc(d.done, -1)
                dve.tensor_reduce(k.mean_weight[:, its], typed[:].rearrange("p c q r -> p c (q r)"),
                                  AX.X, ALU.add).then_inc(d.done, 1)
                dve.wait_ge(d.done, 1)
                dve.sem_inc(d.done, -1)
                dve.tensor_tensor(k.mean_weight[:, its], k.mean_weight[:, its],
                                  k.records[:, its, WEIGHT], ALU.mult).then_inc(d.done, 1)
                dve.wait_ge(d.done, 1)
                dve.sem_inc(d.done, -1)

            def trio(g, i):
                dve.wait_ge(d.slot_used, 1)
                dve.sem_inc(d.slot_used, -1)
                dve.tensor_copy(indices[:, i * TRIO:(i + 1) * TRIO],
                                source[:, bass.ds(g * SLOTS + i * TRIO, TRIO), index]).then_inc(d.done, 1)
                dve.wait_ge(d.done, 1)
                dve.sem_inc(d.done, -1)
                dve.sem_inc(d.index_ready, 1)
                for j in range(i * TRIO, (i + 1) * TRIO):
                    at = bass.ds(g * SLOTS + j, 1)
                    if weights is None:
                        mask = dve.tensor_scalar(to_node[:, j, :], k.lane[:], k.dst_in_tile[:, at], None,
                                                 ALU.is_equal)
                    else:
                        weight = k.mean_weight[:, at] if weights == "mean" else k.records[:, at, WEIGHT1]
                        mask = dve.tensor_scalar(to_node[:, j, :], k.lane[:], k.dst_in_tile[:, at], weight,
                                                 ALU.is_equal, ALU.mult)
                mask.then_inc(d.mask_ready, 1)

            def tile(t):
                g0, g1 = tile_groups(dve, k, s, t)
                with dve.Fori(g0, g1) as g:
                    if find_means:
                        types(g)
                    for i in range(TRIOS):
                        trio(g + 1, i)
                        if find_means:
                            find_trio(i)
                    if find_means:
                        means(g)
                dve.wait_ge(d.acc_ready, 1)
                dve.sem_inc(d.acc_ready, -1)
                to.dve(dve, t, acc)

            dve.sem_inc(d.slot_used, TRIOS)
            for i in range(TRIOS):
                trio(0, i)
            if to.late:
                tile(0)
                with dve.Fori(0, T - 1) as t:
                    tile(t + 1)
                    to.dve_late(dve, t)
                to.dve_late(dve, T - 1)
            else:
                with dve.Fori(0, T) as t:
                    tile(t)

        @block.tensor
        def _(pe):
            groups = all_groups(pe, k, s)

            def tile(t):
                g0, g1 = tile_groups(pe, k, s, t)
                pe.wait_ge(d.acc_taken, 1)
                pe.sem_inc(d.acc_taken, -1)
                pe.matmul(acc[:], k.zeros[:, 0:P], k.zeros[:, 0:C], start=True, stop=False)
                with pe.Fori(g0, g1) as g:
                    for i in range(TRIOS):
                        pe.wait_ge(d.mask_ready, 1)
                        pe.sem_inc(d.mask_ready, -1)
                        if find_means:
                            for j in range(TRIO):
                                mm = pe.matmul(turned[:, j, :], k.dst_bf16[:, bass.ds(g * SLOTS + i * TRIO + j, 1)]
                                               .broadcast_to([P, P]), k.identity_b[:], start=True, stop=True)
                            mm.then_inc(turned_ready, 1)
                        for j in range(i * TRIO, (i + 1) * TRIO):
                            pe.wait_ge(landed[j], landings(groups, passes, g, further if j < SLOTS // 2 + TRIO else 0))
                            mm = pe.matmul(acc[:], to_node[:, j, :], gathered[:, j, :], start=False, stop=False)
                        mm.then_inc(d.slot_used, 1)
                        if find_means:
                            pe.wait_ge(from_ready, 1)
                            pe.sem_inc(from_ready, -1)
                            pe.wait_ge(found_taken, 1)
                            pe.sem_inc(found_taken, -1)
                            for j in range(TRIO):
                                mm = pe.matmul(found_banks[:, i % 2, j * 3 * R:(j + 1) * 3 * R], from_node[:, j, :],
                                               k.count_parts[:].rearrange("p t q r -> p (t q r)")[
                                                   :, bass.ds(t * (3 * R), 3 * R)], start=True, stop=True)
                            mm.then_inc(found_ready, 1)
                pe.matmul(acc[:], k.zeros[:, 0:P], k.zeros[:, 0:C], start=False, stop=True).then_inc(d.acc_ready, 1)

            if find_means:
                pe.sem_inc(found_taken, 2)
            if to.dense:
                if isinstance(to, ToRelations):
                    pe.sem_inc(to.pair_taken, 2)
                tile(0)
                with pe.Fori(1, T) as t:
                    tile(t)
                    to.pe(pe)
                to.pe(pe)
            else:
                with pe.Fori(0, T) as t:
                    tile(t)
            pe.wait_ge(d.mask_ready, TRIOS)
            pe.sem_inc(d.mask_ready, -TRIOS)

        if to.dense:
            @block.scalar
            def _(act):
                def turn(t):
                    g0, g1 = tile_groups(act, k, s, t)
                    with act.Fori(g0, g1):
                        for i in range(TRIOS):
                            act.wait_ge(turned_ready, 1)
                            act.sem_inc(turned_ready, -1)
                            act.activation(apart[:], turned[:], ACT.Square, bias=k.minus_node[:]).then_inc(d.act_done, 1)
                            act.wait_ge(d.act_done, 1)
                            act.sem_inc(d.act_done, -1)
                            act.activation(from_node[:], apart[:], ACT.Relu, scale=-1.0, bias=1.0).then_inc(from_ready, 1)

                if isinstance(to, ToRelations):
                    act.sem_inc(to.staged_free, 1)
                if to.roots:
                    square_root(act, d)
                if find_means:
                    turn(0)
                with act.Fori(0, T - 1) as t:
                    if find_means:
                        turn(t + 1)
                    relu_turned(act, d)
                    if to.roots:
                        square_root(act, d)
                    to.act(act, t)
                relu_turned(act, d)
                to.act(act, T - 1)

        @block.sync
        def _(sp):
            if to.dense:
                with sp.Fori(0, T) as t:
                    to.sp(sp, t)
            else:
                with sp.Fori(0, T - 1) as t:
                    to.sp(sp, t)
                to.sp_last(sp)


def attend(nc, k, s):
    C, T = s.width, s.tiles
    HALF = SLOTS // 2
    HTRIOS = TRIOS // 2
    HC = C // HEADS
    W = C + HEADS
    ROW = W + PART_WORDS
    with ExitStack() as ctx:
        def sb(n, shape, dtype=F32):
            return ctx.enter_context(nc.sbuf_tensor(f"attend_{n}", shape, dtype))

        def psum(n, shape, dtype=F32):
            return ctx.enter_context(nc.psum_tensor(f"attend_{n}", shape, dtype))

        gathered = sb("gathered", [P, SLOTS, ROW])
        to_node = sb("to_node", [P, SLOTS, P])
        from_node = sb("from_node", [P, SLOTS, P], BF16)
        apart = sb("apart", [P, TRIO * P])
        outside = sb("outside", [P, HTRIOS, TRIO * P])
        part_rows = sb("part_rows", [PARTS, 2, TRIO * P], BF16)
        masked = sb("masked", [P, HTRIOS, HEADS, TRIO * P])
        indices = sb("indices", [P, SLOTS], I32)
        maxima = sb("maxima", [P, HEADS, HTRIOS + 1])
        source_max = sb("source_max", [P, HEADS])
        logit = sb("logit", [P, HEADS])
        top = sb("top", [P, 2, HEADS])
        rest = sb("rest", [P, HEADS])
        mark = sb("mark", [P, 1])
        ahead = sb("ahead", [1, 1])
        target_parts = sb("target_parts", [P, 3, 2 * HEADS], BF16)
        decay = sb("decay", [P, 2, HEADS])
        found_sum = sb("found_sum", [P, HALF, 2 * HEADS])
        logits = sb("logits", [P, HALF, HEADS])
        sums = sb("sums", [P, W])
        last_sums = sb("last_sums", [P, W])
        inverse = sb("inverse", [P, HEADS])
        spread = psum("spread", [P, HEADS, 512])
        turned = psum("turned", [P, TRIO * P])
        part_turned = psum("part_turned", [PARTS, TRIO * P])
        bank = psum("bank", [P, 512])
        acc = bank[:, 0:W]
        found = bank[:, W:W + HALF * 6 * HEADS].rearrange("p (c h) -> p c h", h=6 * HEADS)
        d = k.dense
        turned_ready = k.sem("attend_turned_ready")
        copied = k.sem("attend_copied")
        spread_ready = k.sem("attend_spread_ready")
        spread_taken = k.sem("attend_spread_taken")
        target_ready = k.sem("attend_target_ready")
        decay_asked = k.sem("attend_decay_asked")
        decay_ready = k.sem("attend_decay_ready")
        found_ready = k.sem("attend_found_ready")
        logits_ready = k.sem("attend_logits_ready")
        weights_ready = k.sem("attend_weights_ready")
        maxima_ready = k.sem("attend_maxima_ready")
        last_ready = k.sem("attend_last_ready")
        sums_ready = k.sem("attend_sums_ready")
        sums_rescaled = k.sem("attend_sums_rescaled")
        scaled_dve = k.sem("attend_scaled_dve")
        scaled_act = k.sem("attend_scaled_act")
        landed, passes = k.landed, k.passes
        k.passes += 1
        k.further += 1
        source = k.records[:].bitcast(I32)
        parts = gathered[:].bitcast(BF16)[:, :, 2 * W:2 * W + PARTS]
        block = ctx.enter_context(nc.Block())

        @block.gpsimd
        def _(pool):
            def gathers(g, trios):
                for i in trios:
                    pool.wait_ge(d.slot_used, 1)
                    pool.sem_inc(d.slot_used, -1)
                    pool.tensor_copy(indices[:, i * TRIO:(i + 1) * TRIO],
                                     source[:, bass.ds(g * SLOTS + i * TRIO, TRIO), SRC]).then_inc(d.index_ready, 1)
                    pool.wait_ge(d.index_ready, 1)
                    pool.sem_inc(d.index_ready, -1)
                    for j in range(i * TRIO, (i + 1) * TRIO):
                        pool.indirect_dma_start(gathered[:, j, :], None, k.gat_table,
                                                IndirectOffsetOnAxis(ap=indices[:, j:j + 1], axis=0)
                                                ).then_inc(landed[j], 16)

            pool.sem_inc(d.slot_used, TRIOS)
            groups = all_groups(pool, k, s)
            with pool.Fori(0, groups) as g:
                gathers(g, range(TRIOS))
            gathers(groups, range(HTRIOS + 1))
            pool.wait_ge(d.slot_used, HTRIOS - 1)
            pool.sem_inc(d.slot_used, -(HTRIOS - 1))

        @block.vector
        def _(dve):
            by_head = "p (h c) -> p h c"

            def mask(g, slot):
                dve.tensor_scalar(to_node[:, slot, :], k.lane[:], k.dst_in_tile[:, bass.ds(g * SLOTS + slot, 1)],
                                  None, ALU.is_equal)

            def largest(i):
                for h in range(HEADS):
                    if h % 2 == 0:
                        dve.wait_ge(spread_ready, 1)
                        dve.sem_inc(spread_ready, -1)
                    found_largest = dve.tensor_tensor_reduce(
                        out=masked[:, i % HTRIOS, h, :], in0=spread[:, h, 0:TRIO * P], in1=outside[:, i % HTRIOS, :],
                        scale=1.0, scalar=-FAR, op0=ALU.add, op1=ALU.max,
                        accum_out=maxima[:, h, i % HTRIOS:i % HTRIOS + 1])
                    if h % 2 == 1:
                        found_largest.then_inc(spread_taken, 1)
                if i % HTRIOS == HTRIOS - 1:
                    dve.memset(mark[:], 0.0).then_inc(maxima_ready, 1)

            def half(g, this, target, loop=None, opening=None, tail=None):
                pending = loop is None
                ahead, other = (0, 1) if this == 0 else (1, 0)
                its = slice(this * HALF, (this + 1) * HALF)
                next_g, next_slot = g + ahead, other * HALF
                hi, mid, lo = (target_parts[:, i, HEADS:2 * HEADS] for i in range(3))
                dve.wait_ge(maxima_ready, 1)
                dve.sem_inc(maxima_ready, -1)
                dve.tensor_reduce(source_max[:], maxima[:], AX.X, ALU.max).then_inc(d.done, 1)
                mask(next_g, next_slot)
                dve.wait_ge(d.done, 1)
                dve.sem_inc(d.done, -1)
                dve.tensor_tensor(logit[:], source_max[:], target, ALU.add).then_inc(d.done, 1)
                mask(next_g, next_slot + 1)
                dve.wait_ge(d.done, 1)
                dve.sem_inc(d.done, -1)
                dve.scalar_tensor_tensor(out=top[:, this, :], in0=logit[:], scalar=SLOPE, in1=logit[:], op0=ALU.mult,
                                         op1=ALU.max).then_inc(d.done, 1)
                mask(next_g, next_slot + 2)
                dve.wait_ge(d.done, 1)
                dve.sem_inc(d.done, -1)
                dve.tensor_copy(hi, top[:, this, :]).then_inc(d.done, 1)
                mask(next_g, next_slot + 3)
                dve.wait_ge(d.done, 1)
                dve.sem_inc(d.done, -1)
                dve.tensor_tensor(mid, top[:, this, :], hi, ALU.subtract).then_inc(d.done, 1)
                dve.tensor_tensor(rest[:], top[:, this, :], hi, ALU.subtract).then_inc(d.done, 1)
                mask(next_g, next_slot + 4)
                dve.wait_ge(d.done, 2)
                dve.sem_inc(d.done, -2)
                dve.tensor_tensor(lo, rest[:], mid, ALU.subtract).then_inc(target_ready, 1)
                dve.tensor_tensor(decay[:, this, :], top[:, other, :] if pending else loop, top[:, this, :],
                                  ALU.subtract).then_inc(decay_asked, 1)
                dve.tensor_copy(maxima[:, :, HTRIOS], source_max[:]).then_inc(d.done, 1)
                mask(next_g, next_slot + 5)
                dve.wait_ge(d.done, 1)
                dve.sem_inc(d.done, -1)
                dve.wait_ge(found_ready, 1)
                dve.sem_inc(found_ready, -1)
                dve.tensor_reduce(found_sum[:], found.rearrange("p c (q h) -> p c h q", q=3), AX.X, ALU.add
                                  ).then_inc(d.done, 1)
                if pending:
                    add_sums()
                else:
                    opening()
                dve.wait_ge(d.done, 1)
                dve.sem_inc(d.done, -1)
                dve.tensor_tensor(logits[:], gathered[:, its, C:W], found_sum[:, :, 0:HEADS], ALU.add).then_inc(d.done, 1)
                mask(next_g, next_slot + 6)
                dve.wait_ge(d.done, 1)
                dve.sem_inc(d.done, -1)
                dve.scalar_tensor_tensor(out=logits[:], in0=logits[:], scalar=SLOPE, in1=logits[:], op0=ALU.mult,
                                         op1=ALU.max).then_inc(d.done, 1)
                mask(next_g, next_slot + 7)
                dve.wait_ge(d.done, 1)
                dve.sem_inc(d.done, -1)
                dve.tensor_tensor(logits[:], logits[:], found_sum[:, :, HEADS:2 * HEADS], ALU.subtract).then_inc(d.done, 1)
                mask(next_g, next_slot + 8)
                dve.wait_ge(d.done, 1)
                dve.sem_inc(d.done, -1)
                dve.tensor_scalar(logits[:], logits[:], 0.0, None, ALU.min).then_inc(logits_ready, 1)
                dve.wait_ge(decay_ready, 1)
                dve.sem_inc(decay_ready, -1)
                dve.tensor_tensor(sums[:, C:W], sums[:, C:W], decay[:, this, :], ALU.mult)
                dve.wait_ge(weights_ready, 1)
                dve.sem_inc(weights_ready, -1)
                for i in range(HTRIOS):
                    at = this * HALF + i * TRIO
                    rows = gathered[:, at:at + TRIO - 1, 0:C].rearrange("p s (h c) -> p s h c", h=HEADS)
                    dve.tensor_tensor(rows, rows, gathered[:, at:at + TRIO - 1, C:W].unsqueeze(3).broadcast_to(
                        [P, TRIO - 1, HEADS, HC]), ALU.mult).then_inc(scaled_dve, 1)
                    if i < HTRIOS - 1:
                        largest(other * HTRIOS + i)
                if tail is not None:
                    residual(tail)
                largest(other * HTRIOS + HTRIOS - 1)

            def add_sums():
                dve.wait_ge(d.acc_ready, 1)
                dve.sem_inc(d.acc_ready, -1)
                dve.sem_inc(d.slot_used, 1)
                dve.wait_ge(sums_rescaled, 1)
                dve.sem_inc(sums_rescaled, -1)
                dve.tensor_tensor(sums[:], sums[:], acc, ALU.add).then_inc(sums_ready, 1)

            def residual(t):
                dve.tensor_scalar(inverse[:], last_sums[:, C:W], 1e-16, None, ALU.add).then_inc(d.done, 1)
                dve.wait_ge(d.done, 1)
                dve.sem_inc(d.done, -1)
                dve.reciprocal(inverse[:], inverse[:]).then_inc(d.done, 1)
                dve.wait_ge(d.done, 1)
                dve.sem_inc(d.done, -1)
                dve.tensor_tensor(d.row[:].rearrange(by_head, h=HEADS),
                                  last_sums[:, 0:C].rearrange(by_head, h=HEADS),
                                  inverse[:].unsqueeze(2).broadcast_to([P, HEADS, HC]), ALU.mult).then_inc(d.done, 1)
                dve.wait_ge(d.done, 1)
                dve.sem_inc(d.done, -1)
                dve.tensor_tensor(d.row[:], d.row[:], k.bias_gat[:], ALU.add).then_inc(d.done, 1)
                dve.wait_ge(d.done, 1)
                dve.sem_inc(d.done, -1)
                add_relu_row(dve, k, s, d, t)

            def finish():
                dve.wait_ge(d.acc_ready, 1)
                dve.sem_inc(d.acc_ready, -1)
                dve.sem_inc(d.slot_used, 1)
                dve.wait_ge(sums_rescaled, 1)
                dve.sem_inc(sums_rescaled, -1)
                dve.tensor_tensor(last_sums[:], sums[:], acc, ALU.add).then_inc(last_ready, 1)

            def tile(t, tail=None):
                g0, g1 = tile_groups(dve, k, s, t)
                source, target, loop = (k.attention[:, bass.ds(t * 3 * HEADS + i * HEADS, HEADS)] for i in range(3))

                def opening():
                    if tail is not None:
                        finish()
                        dve.wait_ge(last_ready, 1)
                        dve.sem_inc(last_ready, -1)
                    dve.tensor_copy(sums[:, 0:C], k.own[:, bass.ds(t * C, C)]).then_inc(sums_ready, 1)
                    dve.memset(sums[:, C:W], 1.0).then_inc(last_ready, 1)
                    dve.wait_ge(last_ready, 1)
                    dve.sem_inc(last_ready, -1)

                dve.tensor_copy(maxima[:, :, HTRIOS], source).then_inc(d.done, 1)
                dve.tensor_copy(target_parts[:, :, 0:HEADS], k.parts[:].bitcast(BF16)[
                    :, bass.ds(t * PARTS, PARTS)].rearrange("p (q h) -> p q h", q=3)[:, :, HEADS:2 * HEADS]).then_inc(d.done, 1)
                dve.wait_ge(d.done, 2)
                dve.sem_inc(d.done, -2)
                half(g0, 0, target, loop, opening, tail)
                half(g0, 1, target)
                with dve.If(g1 > g0 + 1):
                    with dve.Fori(g0 + 1, g1) as g:
                        half(g, 0, target)
                        half(g, 1, target)

            for i in range(HTRIOS):
                for j in range(i * TRIO, (i + 1) * TRIO):
                    mask(0, j)
                largest(i)
            tile(0)
            with dve.Fori(1, T) as t:
                tile(t, tail=t - 1)
            finish()
            dve.wait_ge(last_ready, 1)
            dve.sem_inc(last_ready, -1)
            residual(T - 1)

        @block.tensor
        def _(pe):
            groups = all_groups(pe, k, s)

            def turn(g, i):
                for j in range(TRIO):
                    pe.matmul(turned[:, j * P:(j + 1) * P],
                              k.dst_bf16[:, bass.ds(g * SLOTS + i * TRIO + j, 1)].broadcast_to([P, P]), k.identity_b[:],
                              start=True, stop=True)
                for j in range(TRIO):
                    pe.wait_ge(landed[i * TRIO + j], landings(groups, passes, g))
                    mm = pe.matmul(part_turned[:, j * P:(j + 1) * P], parts[:, i * TRIO + j, :], k.identity_b[:],
                                   start=True, stop=True)
                mm.then_inc(turned_ready, 1)

            def spread_heads(i):
                for pair in range(2):
                    pe.wait_ge(spread_taken, 1)
                    pe.sem_inc(spread_taken, -1)
                    for h in range(2 * pair, 2 * pair + 2):
                        mm = pe.matmul(spread[:, h, 0:TRIO * P], k.pick[:, h, :], part_rows[:, i % 2, :], start=True, stop=True)
                    mm.then_inc(spread_ready, 1)

            def sum_trio(this, i):
                pe.wait_ge(scaled_dve, 1)
                pe.sem_inc(scaled_dve, -1)
                pe.wait_ge(scaled_act, 1)
                pe.sem_inc(scaled_act, -1)
                for j in range(i * TRIO, (i + 1) * TRIO):
                    slot = this * HALF + j
                    mm = pe.matmul(acc, to_node[:, slot, :], gathered[:, slot, 0:W],
                                   start=(j == 0), stop=(j == HALF - 1))
                mm.then_inc(d.acc_ready if i == HTRIOS - 1 else d.slot_used, 1)

            def keep_warm(n):
                for _ in range(n):
                    pe.matmul(d.in_psum, k.zeros[:, 0:P], k.zeros[:, 0:C], start=True, stop=True)

            def half(g, this):
                ahead, other = (0, 1) if this == 0 else (1, 0)
                nexts = other * HTRIOS
                keep_warm(WARM_BEFORE)
                pe.wait_ge(target_ready, 1)
                pe.sem_inc(target_ready, -1)
                for j in range(this * HALF, (this + 1) * HALF):
                    mm = pe.matmul(found[:, j - this * HALF, :], from_node[:, j, :],
                                   target_parts[:].rearrange("p q h -> p (q h)"), start=True, stop=True)
                mm.then_inc(found_ready, 1)
                pe.wait_ge(copied, 1)
                pe.sem_inc(copied, -1)
                turn(g + ahead, nexts + 1)
                spread_heads(nexts)
                keep_warm(WARM_BEHIND)
                sum_trio(this, 0)
                pe.wait_ge(copied, 1)
                pe.sem_inc(copied, -1)
                turn(g + ahead, nexts + 2)
                spread_heads(nexts + 1)
                sum_trio(this, 1)
                pe.wait_ge(copied, 1)
                pe.sem_inc(copied, -1)
                spread_heads(nexts + 2)
                turn(g + 1, this * HTRIOS)
                sum_trio(this, 2)

            def tile(t):
                g0, g1 = tile_groups(pe, k, s, t)
                half(g0, 0)
                half(g0, 1)
                with pe.If(g1 > g0 + 1):
                    with pe.Fori(g0 + 1, g1) as g:
                        half(g, 0)
                        half(g, 1)

            pe.sem_inc(spread_taken, 2)
            for i in range(HTRIOS):
                turn(0, i)
                pe.wait_ge(copied, 1)
                pe.sem_inc(copied, -1)
                spread_heads(i)
            turn(0, HTRIOS)
            with pe.Fori(0, T) as t:
                tile(t)

        @block.scalar
        def _(act):
            def take_turned(i):
                act.wait_ge(turned_ready, 1)
                act.sem_inc(turned_ready, -1)
                act.copy(part_rows[:, i % 2, :], part_turned[:]).then_inc(d.act_done, 1)
                act.activation(apart[:], turned[:], ACT.Square, bias=k.minus_node[:]).then_inc(d.act_done, 1)
                act.wait_ge(d.act_done, 2)
                act.sem_inc(d.act_done, -2)

            def compare(i):
                trio = from_node[:, i * TRIO:(i + 1) * TRIO, :].rearrange("p c e -> p (c e)")
                act.activation(trio, apart[:], ACT.Relu, scale=-1.0, bias=1.0).then_inc(d.act_done, 1)
                act.wait_ge(d.act_done, 1)
                act.sem_inc(d.act_done, -1)
                act.activation(outside[:, i % HTRIOS, :], trio, ACT.Copy, scale=FAR, bias=-FAR).then_inc(d.act_done, 1)
                act.wait_ge(d.act_done, 1)
                act.sem_inc(d.act_done, -1)
                act.sem_inc(copied, 1)

            def turn(i):
                take_turned(i)
                compare(i)

            def scale(this, i):
                at = this * HALF + (i + 1) * TRIO - 1
                for h in range(HEADS):
                    head = gathered[:, at, h * HC:(h + 1) * HC]
                    act.activation(head, head, ACT.Copy, scale=gathered[:, at, C + h:C + h + 1]).then_inc(d.act_done, 1)
                act.wait_ge(d.act_done, HEADS)
                act.sem_inc(d.act_done, -HEADS)
                act.sem_inc(scaled_act, 1)

            def half(this):
                other = 1 - this
                act.wait_ge(decay_asked, 1)
                act.sem_inc(decay_asked, -1)
                act.activation(decay[:, this, :], decay[:, this, :], ACT.Exp).then_inc(d.act_done, 1)
                act.wait_ge(d.act_done, 1)
                act.sem_inc(d.act_done, -1)
                act.sem_inc(decay_ready, 1)
                take_turned(other * HTRIOS + 1)
                act.wait_ge(logits_ready, 1)
                act.sem_inc(logits_ready, -1)
                act.activation(gathered[:, this * HALF:(this + 1) * HALF, C:W], logits[:], ACT.Exp).then_inc(d.act_done, 1)
                act.wait_ge(d.act_done, 1)
                act.sem_inc(d.act_done, -1)
                act.sem_inc(weights_ready, 1)
                scale(this, 0)
                compare(other * HTRIOS + 1)
                scale(this, 1)
                turn(other * HTRIOS + 2)
                scale(this, 2)
                act.wait_ge(sums_ready, 1)
                act.sem_inc(sums_ready, -1)
                for h in range(HEADS):
                    head = sums[:, h * HC:(h + 1) * HC]
                    act.activation(head, head, ACT.Copy, scale=decay[:, this, h:h + 1]).then_inc(d.act_done, 1)
                act.wait_ge(d.act_done, HEADS)
                act.sem_inc(d.act_done, -HEADS)
                act.sem_inc(sums_rescaled, 1)
                turn(this * HTRIOS)

            def tile(t):
                act.activation(ahead[:], k.ones_row[0:1, 0:1], ACT.Exp).then_inc(d.act_done, 1)
                g0, g1 = tile_groups(act, k, s, t)
                act.wait_ge(d.act_done, 1)
                act.sem_inc(d.act_done, -1)
                half(0)
                half(1)
                with act.If(g1 > g0 + 1):
                    with act.Fori(g0 + 1, g1):
                        half(0)
                        half(1)

            for i in range(HTRIOS + 1):
                turn(i)
            with act.Fori(0, T) as t:
                tile(t)


INPUTS = ["x", "src", "dst", "edge_type_8", "edge_weight", "edge_weight1", "L0_gnn_W", "L0_gnn_b",
          "L1_gnn_weight", "L1_gnn_root", "L1_gnn_bias", "L2_gnn_W", "L2_gnn_att_src", "L2_gnn_att_dst",
          "L2_gnn_bias", "L3_gnn_W1", "L3_gnn_b1", "L3_gnn_W2", "L3_gnn_b2"]


def gnn_block(nc, a, out):
    nodes, width = a["x"].shape
    s = Shapes(nodes, a["src"].shape[0], width, a["L1_gnn_weight"].shape[0])
    with ExitStack() as ctx:
        k = Core(nc, ctx, s)
        prepare(nc, k, s, a)
        count(nc, k, s)
        k.dense = Dense(nc, ctx, k, s)
        begin_dense(nc, k)
        gcn = dict(index=SRC, weights=None)
        aggregate(nc, k, s, "gcn0", k.table[0], ToTable(k, s, layer=0, source="gcn"), **gcn)
        aggregate(nc, k, s, "gcn1", k.table[1], ToTable(k, s, layer=1, source="gcn"),
                  find_means=True, **gcn)
        aggregate(nc, k, s, "gcn2", k.table[0], ToRelations(k, s), **gcn)
        aggregate(nc, k, s, "relations", k.relation_table, ToAttention(k, s), index=SRC_TYPE, weights="mean")
        attend(nc, k, s)
        project(nc, k, s, "out", k.w_out[:, 0:KC, :], k.bias_out_all[:])
        aggregate(nc, k, s, "out0", k.table[0], ToTable(k, s, layer=0, source="out"), index=SRC, weights="weight1")
        aggregate(nc, k, s, "out1", k.table[1], ToOutput(k, s, out), index=SRC, weights="weight1")


def kernel(**inputs):
    import concourse.bacc as bacc
    import numpy as np
    from concourse.bass_utils import run_bass_kernel_spmd

    nc = bacc.Bacc("TRN2", target_bir_lowering=False, num_devices=1)
    arrays = {f"in_{name}": np.ascontiguousarray(inputs[name]) for name in INPUTS}
    a = {name: nc.dram_tensor(f"in_{name}", arrays[f"in_{name}"].shape,
                              mybir.dt.from_np(arrays[f"in_{name}"].dtype), kind="ExternalInput").ap()
         for name in INPUTS}
    out = nc.dram_tensor("out", inputs["x"].shape, F32, kind="ExternalOutput").ap()
    gnn_block(nc, a, out)
    r = run_bass_kernel_spmd(nc, [arrays], core_ids=[0])
    return r.results[0]["out"]
```
